# Optimizing a Trainium2 kernel written in Bass

```python
import numpy as np
import jax
import jax.numpy as jnp

def _softmax(x, axis=-1):
    return jax.nn.softmax(x, axis=axis)

def _gelu(x):
    return jax.nn.gelu(x, approximate=True)

def _silu(x):
    return jax.nn.silu(x)

def _sigmoid(x):
    return jax.nn.sigmoid(x)

def _layernorm(x, axis=-1, eps=1e-05):
    m = jnp.mean(x, axis=axis, keepdims=True)
    v = jnp.var(x, axis=axis, keepdims=True)
    return (x - m) / jnp.sqrt(v + eps)

def _scatter_add(tgt, idx, src, axis=0):
    return tgt.at[idx].add(src)

def _segment_sum(src, seg, n):
    return jax.ops.segment_sum(src, seg, n)
kernel_name = 'mk_gnn_resnorm_d2_gnn_r8_9e4f00'

def setup_inputs(seed: int=0):
    np.random.seed(seed)
    _w = jnp.asarray

    def _rec_inputs():
        import jax
        import jax.numpy as jnp
        _gk = jax.random.key(seed)
        x = -0.0001126 + 1 * jax.random.normal(jax.random.fold_in(_gk, 1), (1250, 768), jnp.float32)
        src = jax.random.randint(jax.random.fold_in(_gk, 2), (20000,), 0, 1250, jnp.int32)
        dst = jax.random.randint(jax.random.fold_in(_gk, 3), (20000,), 0, 1250, jnp.int32)
        _o = jnp.argsort(dst, stable=True)
        src = src[_o]
        dst = dst[_o]
        edge_weight1 = -0.00472126 + 0.997171 * jax.random.normal(jax.random.fold_in(_gk, 13), (20000, 1), jnp.float32)
        return (x, src, dst, edge_weight1)
    x, src, dst, edge_weight1 = _rec_inputs()

    def _L0_gnn_setup():
        import jax, jax.numpy as jnp
        import numpy as np
        N, E, D, H, C = (1250, 12500, 768, 4, 192)
        NEG_SLOPE = 0.2

        def gat_conv(x, src, dst, W, a_src, a_dst, b):
            h = (x @ W).reshape(N, H, C)
            as_n = (h * a_src).sum(-1)
            ad_n = (h * a_dst).sum(-1)
            e = jax.nn.leaky_relu(as_n[src] + ad_n[dst], NEG_SLOPE)
            m = jax.ops.segment_max(e, dst, num_segments=N)
            p = jnp.exp(e - m[dst])
            s = jax.ops.segment_sum(p, dst, num_segments=N)
            alpha = p / (s[dst] + 1e-16)
            out = jax.ops.segment_sum(alpha[:, :, None] * h[src], dst, num_segments=N)
            return out.reshape(N, H * C) + b
        key = jax.random.key(seed)
        ks = jax.random.split(key, 16)
        w = lambda k, shape: jax.random.normal(k, shape, dtype=jnp.float32) * 0.02
        inp = {}
        inp['x'] = jax.random.normal(ks[0], (N, D), dtype=jnp.float32)
        inp['edge_index'] = jax.random.randint(ks[1], (2, E), 0, N, dtype=jnp.int32)
        inp['batch'] = jnp.zeros((N,), dtype=jnp.int32)
        inp['edge_attr'] = jax.random.normal(ks[2], (E, 1), dtype=jnp.float32)
        inp['W_ah'] = w(ks[3], (D, D))
        inp['b_ah'] = jnp.zeros((D,), jnp.float32)
        for i in range(3):
            inp[f'W{i}'] = w(ks[4 + 3 * i], (D, H * C))
            inp[f'a_src{i}'] = w(ks[5 + 3 * i], (H, C))
            inp[f'a_dst{i}'] = w(ks[6 + 3 * i], (H, C))
            inp[f'b{i}'] = jnp.zeros((H * C,), jnp.float32)
        inp['W_out'] = w(ks[13], (3 * D, D))
        inp['b_out'] = jnp.zeros((D,), jnp.float32)
        return inp
    _L0_gnn_all = _L0_gnn_setup()
    _L0_gnn_in = {k: v for k, v in _L0_gnn_all.items() if k in ('W_ah', 'b_ah', 'W0', 'a_src0', 'a_dst0', 'b0', 'W1', 'a_src1', 'a_dst1', 'b1', 'W2', 'a_src2', 'a_dst2', 'b2', 'W_out', 'b_out')}
    del _L0_gnn_all

    def _L1_gnn_setup():
        import jax, jax.numpy as jnp
        import numpy as np
        N_NODES = 1250
        N_EDGES = 10000
        IN_DIM, HID, OUT_DIM, HEADS = (768, 512, 768, 4)
        NEG_SLOPE = 0.2

        def _gat_layer(x, src, dst, W, a_src, a_dst, b, heads, d_out, concat):
            N = x.shape[0]
            h = (x @ W).reshape(N, heads, d_out)
            as_n = jnp.einsum('nhd,hd->nh', h, a_src)
            ad_n = jnp.einsum('nhd,hd->nh', h, a_dst)
            e = jax.nn.leaky_relu(as_n[src] + ad_n[dst], NEG_SLOPE)
            e_max = jax.lax.stop_gradient(jax.ops.segment_max(e, dst, num_segments=N))
            ex = jnp.exp(e - e_max[dst])
            denom = jax.ops.segment_sum(ex, dst, num_segments=N)
            alpha = ex / (denom[dst] + 1e-16)
            msg = alpha[:, :, None] * h[src]
            out = jax.ops.segment_sum(msg, dst, num_segments=N)
            out = out.reshape(N, heads * d_out) if concat else out.mean(axis=1)
            return out + b
        key = jax.random.key(seed)
        ks = jax.random.split(key, 10)
        g = 0.05
        return {'x': jax.random.normal(ks[0], (N_NODES, IN_DIM), jnp.float32), 'edge_index': jax.random.randint(ks[1], (2, N_EDGES), 0, N_NODES, jnp.int64), 'W1': jax.random.normal(ks[2], (IN_DIM, HEADS * HID), jnp.float32) * g, 'a1_src': jax.random.normal(ks[3], (HEADS, HID), jnp.float32) * g, 'a1_dst': jax.random.normal(ks[4], (HEADS, HID), jnp.float32) * g, 'b1': jnp.zeros((HEADS * HID,), jnp.float32), 'W2': jax.random.normal(ks[5], (HEADS * HID, OUT_DIM), jnp.float32) * g, 'a2_src': jax.random.normal(ks[6], (1, OUT_DIM), jnp.float32) * g, 'a2_dst': jax.random.normal(ks[7], (1, OUT_DIM), jnp.float32) * g, 'b2': jnp.zeros((OUT_DIM,), jnp.float32)}
    _L1_gnn_all = _L1_gnn_setup()
    _L1_gnn_in = {k: v for k, v in _L1_gnn_all.items() if k in ('W1', 'a1_src', 'a1_dst', 'b1', 'W2', 'a2_src', 'a2_dst', 'b2')}
    del _L1_gnn_all
    return {'x': x, 'src': src, 'dst': dst, 'edge_weight1': edge_weight1, 'L0_gnn_W_ah': _L0_gnn_in['W_ah'], 'L0_gnn_b_ah': _L0_gnn_in['b_ah'], 'L0_gnn_W0': _L0_gnn_in['W0'], 'L0_gnn_a_src0': _L0_gnn_in['a_src0'], 'L0_gnn_a_dst0': _L0_gnn_in['a_dst0'], 'L0_gnn_b0': _L0_gnn_in['b0'], 'L0_gnn_W1': _L0_gnn_in['W1'], 'L0_gnn_a_src1': _L0_gnn_in['a_src1'], 'L0_gnn_a_dst1': _L0_gnn_in['a_dst1'], 'L0_gnn_b1': _L0_gnn_in['b1'], 'L0_gnn_W2': _L0_gnn_in['W2'], 'L0_gnn_a_src2': _L0_gnn_in['a_src2'], 'L0_gnn_a_dst2': _L0_gnn_in['a_dst2'], 'L0_gnn_b2': _L0_gnn_in['b2'], 'L0_gnn_W_out': _L0_gnn_in['W_out'], 'L0_gnn_b_out': _L0_gnn_in['b_out'], 'L1_gnn_W1': _L1_gnn_in['W1'], 'L1_gnn_a1_src': _L1_gnn_in['a1_src'], 'L1_gnn_a1_dst': _L1_gnn_in['a1_dst'], 'L1_gnn_b1': _L1_gnn_in['b1'], 'L1_gnn_W2': _L1_gnn_in['W2'], 'L1_gnn_a2_src': _L1_gnn_in['a2_src'], 'L1_gnn_a2_dst': _L1_gnn_in['a2_dst'], 'L1_gnn_b2': _L1_gnn_in['b2']}

def reference(x, src, dst, edge_weight1, L0_gnn_W_ah, L0_gnn_b_ah, L0_gnn_W0, L0_gnn_a_src0, L0_gnn_a_dst0, L0_gnn_b0, L0_gnn_W1, L0_gnn_a_src1, L0_gnn_a_dst1, L0_gnn_b1, L0_gnn_W2, L0_gnn_a_src2, L0_gnn_a_dst2, L0_gnn_b2, L0_gnn_W_out, L0_gnn_b_out, L1_gnn_W1, L1_gnn_a1_src, L1_gnn_a1_dst, L1_gnn_b1, L1_gnn_W2, L1_gnn_a2_src, L1_gnn_a2_dst, L1_gnn_b2):
    import jax
    import jax.numpy as jnp

    def _L0_gnn_ref(x, edge_index, batch, edge_attr, W_ah, b_ah, W0, a_src0, a_dst0, b0, W1, a_src1, a_dst1, b1, W2, a_src2, a_dst2, b2, W_out, b_out):
        import jax, jax.numpy as jnp
        import numpy as np
        N, E, D, H, C = (1250, 12500, 768, 4, 192)
        NEG_SLOPE = 0.2

        def gat_conv(x, src, dst, W, a_src, a_dst, b):
            h = (x @ W).reshape(N, H, C)
            as_n = (h * a_src).sum(-1)
            ad_n = (h * a_dst).sum(-1)
            e = jax.nn.leaky_relu(as_n[src] + ad_n[dst], NEG_SLOPE)
            m = jax.ops.segment_max(e, dst, num_segments=N)
            p = jnp.exp(e - m[dst])
            s = jax.ops.segment_sum(p, dst, num_segments=N)
            alpha = p / (s[dst] + 1e-16)
            out = jax.ops.segment_sum(alpha[:, :, None] * h[src], dst, num_segments=N)
            return out.reshape(N, H * C) + b
        loops = jnp.arange(N, dtype=edge_index.dtype)
        src = jnp.concatenate([edge_index[0], loops])
        dst = jnp.concatenate([edge_index[1], loops])
        x1 = jax.nn.relu(x @ W_ah + b_ah)
        xs = [jax.nn.relu(gat_conv(x1, src, dst, W, a_s, a_d, b)) for W, a_s, a_d, b in ((W0, a_src0, a_dst0, b0), (W1, a_src1, a_dst1, b1), (W2, a_src2, a_dst2, b2))]
        node_emb = jnp.concatenate(xs, axis=1)
        return jax.nn.relu(node_emb @ W_out + b_out)

    def _L1_gnn_ref(x, edge_index, W1, a1_src, a1_dst, b1, W2, a2_src, a2_dst, b2):
        import jax, jax.numpy as jnp
        import numpy as np
        N_NODES = 1250
        N_EDGES = 10000
        IN_DIM, HID, OUT_DIM, HEADS = (768, 512, 768, 4)
        NEG_SLOPE = 0.2

        def _gat_layer(x, src, dst, W, a_src, a_dst, b, heads, d_out, concat):
            N = x.shape[0]
            h = (x @ W).reshape(N, heads, d_out)
            as_n = jnp.einsum('nhd,hd->nh', h, a_src)
            ad_n = jnp.einsum('nhd,hd->nh', h, a_dst)
            e = jax.nn.leaky_relu(as_n[src] + ad_n[dst], NEG_SLOPE)
            e_max = jax.lax.stop_gradient(jax.ops.segment_max(e, dst, num_segments=N))
            ex = jnp.exp(e - e_max[dst])
            denom = jax.ops.segment_sum(ex, dst, num_segments=N)
            alpha = ex / (denom[dst] + 1e-16)
            msg = alpha[:, :, None] * h[src]
            out = jax.ops.segment_sum(msg, dst, num_segments=N)
            out = out.reshape(N, heads * d_out) if concat else out.mean(axis=1)
            return out + b
        N = x.shape[0]
        loops = jnp.arange(N, dtype=edge_index.dtype)
        src = jnp.concatenate([edge_index[0], loops])
        dst = jnp.concatenate([edge_index[1], loops])
        h = _gat_layer(x, src, dst, W1, a1_src, a1_dst, b1, HEADS, HID, True)
        h = jax.nn.elu(h)
        out = _gat_layer(h, src, dst, W2, a2_src, a2_dst, b2, 1, OUT_DIM, False)
        return out
    edge_index = jnp.stack([src, dst])
    batch0 = jnp.zeros((1250,), jnp.int32)
    x = _layernorm(x + _L0_gnn_ref(x, edge_index, batch0, edge_weight1, L0_gnn_W_ah, L0_gnn_b_ah, L0_gnn_W0, L0_gnn_a_src0, L0_gnn_a_dst0, L0_gnn_b0, L0_gnn_W1, L0_gnn_a_src1, L0_gnn_a_dst1, L0_gnn_b1, L0_gnn_W2, L0_gnn_a_src2, L0_gnn_a_dst2, L0_gnn_b2, L0_gnn_W_out, L0_gnn_b_out), axis=-1)
    x = _layernorm(x + _L1_gnn_ref(x, edge_index, L1_gnn_W1, L1_gnn_a1_src, L1_gnn_a1_dst, L1_gnn_b1, L1_gnn_W2, L1_gnn_a2_src, L1_gnn_a2_dst, L1_gnn_b2), axis=-1)
    return x

_drawn_inputs = setup_inputs


def setup_inputs(seed=0):
    import zlib

    import numpy as np

    out = dict(_drawn_inputs(seed))
    spreads = {'L0_gnn_b_ah': (0.0, 0.298),
     'L0_gnn_b0': (0.0, 0.1),
     'L0_gnn_b1': (0.0, 0.1),
     'L0_gnn_b2': (0.0, 0.1),
     'L0_gnn_b_out': (0.0, 0.1),
     'L1_gnn_b1': (0.0, 0.1),
     'L1_gnn_b2': (0.0, 0.1)}
    factors = {'L0_gnn_a_src0': 64.0,
     'L0_gnn_a_dst0': 64.0,
     'L0_gnn_a_src1': 64.0,
     'L0_gnn_a_dst1': 64.0,
     'L0_gnn_a_src2': 64.0,
     'L0_gnn_a_dst2': 64.0}
    for name, (base, spread) in spreads.items():
        noise = np.random.default_rng([zlib.crc32(name.encode()), seed]).standard_normal(out[name].shape)
        drawn = base * np.exp(spread * noise) if base else spread * noise
        out[name] = jnp.asarray(drawn.astype(out[name].dtype))
    for name, factor in factors.items():
        out[name] = (out[name] * factor).astype(out[name].dtype)
    return out
```

```python
import concourse.bass as bass
from concourse import mybir
from contextlib import ExitStack

F32 = mybir.dt.float32
F32R = mybir.dt.float32r
BF16 = mybir.dt.bfloat16
U16 = mybir.dt.uint16
I16 = mybir.dt.int16
I32 = mybir.dt.int32
ALU = mybir.AluOpType
ACT = mybir.ActivationFunctionType
AX = mybir.AxisListType

N = 1250
D = 768
E = 20000
T = 125
NT = N // T
KD = D // 128
EP = E // (2 * T)
SLOPE = 0.2
EPS = 1e-5
NO_EDGE = -3e38

H0, C0 = 4, 192
CONVS = 3
PAIR = 2 * C0
HC0 = C0 + 2
H1, C1 = 4, 512
HALF1 = C1 // 2
DH = N // 2
NH = NT // 2
K1 = H1 * C1 // 128
KO = CONVS * D // 128


class Core:

    def __init__(self, nc):
        self.nc = nc
        self.stages = 0

    def tools(self, ctx):
        nc, n = self.nc, self.stages
        self.stages += 1
        sb = lambda name, shape, dt: ctx.enter_context(nc.sbuf_tensor(f"{name}_{n}", shape, dt))
        pb = lambda name, shape: ctx.enter_context(nc.psum_tensor(f"{name}_{n}", shape, F32))
        sems = []

        def sem(name):
            sems.append(nc.alloc_semaphore(f"{name}_{n}"))
            return sems[-1]

        def clear():
            if sems:
                nc.clear_and_free_semaphores(sems)
                nc.all_engine_barrier()

        ctx.callback(clear)
        return sb, pb, sem


def rows_of(dram_rows):
    return dram_rows.rearrange("(t p) f -> p t f", p=T)


def spread(dram_row, parts):
    return dram_row.partition_broadcast(parts)


def wait_apart(eng, sem, value):
    eng.wait_ge(sem, value)
    eng.sem_inc(sem_of_waits[0], 1)


sem_of_waits = [None]


class Chain:

    def __init__(self, eng, sem):
        self.eng, self.sem, self.n = eng, sem, 0

    def __call__(self, ins):
        self.n += 1
        ins.then_inc(self.sem, 1)
        self.eng.wait_ge(self.sem, self.n)


def counts_and_x1(nc, core, src, dst, x, w_ah, b_ah):
    ident, CT, G, x1T = core.ident, core.CT, core.G, core.x1T
    BT = 2 * T
    NB = NT // 2
    CH = [(0, 418), (418, 416), (834, 416)]
    with ExitStack() as ctx:
        sb, pb, sem = core.tools(ctx)
        edge_i = sb("edge_i", [EP, 2, 2 * T], I32)
        edge_f = sb("edge_f", [EP, 2, 2 * T], F32)
        dst_ends = sb("dst_ends", [EP, 2], F32)
        ends_row = sb("ends_row", [128, 2, EP], F32)
        edge_col = sb("edge_col", [T, 2, 2, 2 * EP], F32)
        spare = CT[0:1, :, :].rearrange("p t n -> p (t n)")[:, 0:2 * 5 * NT * EP].bitcast(F32) \
            .rearrange("p (a t e) -> p a t e", a=5, t=NT)
        meets, meets_b, meets_c = (spare[:, i] for i in range(3))
        tile_lo, pair_no = (spare[:, i].bitcast(I32) for i in (3, 4))
        range_f = sb("range_f", [1, 3, NT], F32)
        ones_row = sb("ones_row", [1, NT], F32)
        range_i = sb("range_i", [1, 3, NT], I32)
        node_no = sb("node_no", [T, N], I16)
        src_hot = sb("src_hot", [T, 2, N], BF16)
        dst_hot = sb("dst_hot", [T, 2, T], BF16)
        band = sb("band", [T, 2 * N - T], BF16)
        ident_b = sb("ident_b", [T, T], BF16)
        zeros_b = sb("zeros_b", [T, T], BF16)
        count_row = sb("count_row", [T, N], F32)
        w_raw = sb("w_raw", [128, 2, D], F32)
        w_hi = sb("w_hi", [128, KD, D], F32R)
        w_lo = sb("w_lo", [128, KD, D], F32R)
        bias = sb("bias_ah", [128, KD], F32)
        x_in = sb("x_in", [T, 2, D], F32)
        xT_hi = sb("xT_hi", [128, KD, BT], F32R)
        xT_lo = sb("xT_lo", [128, KD, BT], F32R)
        x1_f = sb("x1_f", [128, 2, 2 * BT], F32)
        p_count = pb("p_count", [T, 3, 512])
        p_turn = pb("p_turn", [128, 3, 512])
        p_x = pb("p_x", [128, 2, 512])

        edges_in = sem("edges_in")
        w_in = [sem(f"w_in{i}") for i in range(2)]
        bias_in = sem("bias_in")
        consts = sem("consts")
        steps = sem("steps")
        edges_turned = sem("edges_turned")
        cols_ready = sem("cols_ready")
        ranges_ready = sem("ranges_ready")
        hot_ready = sem("hot_ready")
        hot_free = sem("hot_free")
        counted = sem("counted")
        row_staged = sem("row_staged")
        mask_done = sem("mask_done")
        row_turned = sem("row_turned")
        ct_done = sem("ct_done")
        w_split = sem("w_split")
        x_loaded = sem("x_loaded")
        x_turned = sem("x_turned")
        xhi_done = sem("xhi_done")
        xlo_done = sem("xlo_done")
        x1_summed = sem("x1_summed")
        x1_relu = sem("x1_relu")
        x1_hi_done = sem("x1_hi_done")
        x1_lo_done = sem("x1_lo_done")

        block = ctx.enter_context(nc.Block())

        @block.sync
        def _(sp):
            sp.dma_start(edge_i[:, 0, :], src.rearrange("(p e) -> p e", e=2 * T)).then_inc(edges_in, 16)
            sp.dma_start(edge_i[:, 1, :], dst.rearrange("(p e) -> p e", e=2 * T)).then_inc(edges_in, 16)
            sp.dma_start(x_in[:], rows_of(x)[:, 0:2, :]).then_inc(x_loaded, 16)
            sp.dma_start(bias[:], b_ah).then_inc(bias_in, 16)
            for k in range(KD):
                if k >= 2:
                    sp.wait_ge(w_split, 2 * (k - 1))
                sp.dma_start(w_raw[:, k % 2, :], w_ah[k * 128:(k + 1) * 128, :]).then_inc(w_in[k % 2], 16)
            for b in range(1, NB):
                sp.wait_ge(x_turned, 3 * b)
                sp.dma_start(x_in[:], rows_of(x)[:, 2 * b:2 * b + 2, :]).then_inc(x_loaded, 16)

        @block.gpsimd
        def _(pool):
            pool.iota(node_no[:], [[1, N]], base=0, channel_multiplier=0).then_inc(consts, 1)
            pool.iota(tile_lo, [[T, NT], [0, EP]], base=0, channel_multiplier=0).then_inc(consts, 1)
            pool.iota(pair_no, [[0, NT], [1, EP]], base=0, channel_multiplier=0).then_inc(consts, 1)
            for m in (band, ident_b, zeros_b):
                pool.memset(m[:], 0.0).then_inc(consts, 1)
            pool.wait_ge(consts, 6)
            pool.affine_select(out=ident_b[:], in_=ident_b[:], compare_op=ALU.not_equal, fill=1.0, base=0,
                               pattern=[[-1, T]], channel_multiplier=1).then_inc(consts, 1)
            pool.affine_select(out=band[:], in_=band[:], compare_op=ALU.not_equal, fill=1.0, base=N - T,
                               pattern=[[-1, 2 * N - T]], channel_multiplier=1).then_inc(consts, 1)
            for k in range(KD):
                pool.wait_ge(w_in[k % 2], 16 * (k // 2 + 1))
                pool.tensor_copy(w_hi[:, k, :], w_raw[:, k % 2, :]).then_inc(w_split, 1)
                pool.wait_ge(w_split, 2 * k + 1)
                pool.tensor_tensor(w_lo[:, k, :], w_raw[:, k % 2, :], w_hi[:, k, :].bitcast(F32),
                                   ALU.subtract).then_inc(w_split, 1)

        @block.vector
        def _(dve):
            v = nc.vector
            step = Chain(dve, steps)
            dve.wait_ge(edges_in, 32)
            step(v.tensor_copy(edge_f[:], edge_i[:]))
            step(v.tensor_reduce(out=dst_ends[:, 0:1], in_=edge_f[:, 1, :], axis=AX.X, op=ALU.min))
            step(v.tensor_reduce(out=dst_ends[:, 1:2], in_=edge_f[:, 1, :], axis=AX.X, op=ALU.max))
            dve.wait_ge(edges_turned, 1)
            v.tensor_copy(edge_col[:, :, :, 0:EP],
                          p_turn[0:T, 0, 0:4 * EP].rearrange("p (a b c) -> p a b c", a=2, b=2)).then_inc(cols_ready, 1)
            step(v.tensor_copy(ends_row[:], p_turn[:, 1, 0:2 * EP].rearrange("p (a c) -> p a c", a=2)))
            dve.wait_ge(consts, 3)
            least = ends_row[0:1, 0:1, :].broadcast_to([1, NT, EP])
            most = ends_row[0:1, 1:2, :].broadcast_to([1, NT, EP])
            step(v.tensor_tensor(meets, most, tile_lo, ALU.is_ge))
            step(v.scalar_tensor_tensor(meets_b, tile_lo, float(T), least, ALU.add, ALU.is_gt))
            step(v.tensor_tensor(meets, meets, meets_b, ALU.mult))
            step(v.scalar_tensor_tensor(meets_b, pair_no, float(-EP), meets, ALU.add, ALU.mult))
            step(v.scalar_tensor_tensor(meets_c, pair_no, 1.0, meets, ALU.add, ALU.mult))
            step(v.tensor_reduce(out=range_f[:, 0, :], in_=meets_b, axis=AX.X, op=ALU.min))
            step(v.tensor_reduce(out=range_f[:, 1, :], in_=meets_c, axis=AX.X, op=ALU.max))
            step(v.tensor_scalar(range_f[:, 0, :], range_f[:, 0, :], float(EP), float(EP - 1), ALU.add, ALU.min))
            step(v.tensor_tensor(range_f[:, 1, :], range_f[:, 1, :], range_f[:, 0, :], ALU.subtract))
            step(v.tensor_scalar(range_f[:, 1, :], range_f[:, 1, :], 1.0, None, ALU.max))
            step(v.memset(ones_row[:], 1.0))
            step(v.tensor_tensor_scan(range_f[:, 2, :], ones_row[:], range_f[:, 1, :], 0.0, ALU.mult, ALU.add))
            step(v.tensor_tensor(range_f[:, 2, :], range_f[:, 2, :], range_f[:, 1, :], ALU.subtract))
            v.tensor_copy(range_i[:], range_f[:]).then_inc(ranges_ready, 1)
            dve.wait_ge(ranges_ready, 1)
            dve.wait_ge(cols_ready, 1)

            def one_hots(t):
                first = dve.value_load(range_i[0:1, 0, bass.ds(t, 1)], min_val=0, max_val=EP - 1)
                count = dve.value_load(range_i[0:1, 1, bass.ds(t, 1)], min_val=1, max_val=EP)
                before = dve.value_load(range_i[0:1, 2, bass.ds(t, 1)], min_val=0, max_val=EP * NT)
                with dve.Fori(0, count) as j:
                    for h in range(2):
                        dve.wait_ge(hot_free, (before + j) * 2 + (h + 1))
                        at = bass.ds(first + j, 1)
                        v.tensor_scalar(src_hot[:, h, :], node_no[:], edge_col[:, 0, h, at], None, ALU.is_equal)
                        v.tensor_scalar(dst_hot[:, h, :], node_no[:, bass.ds(t * T, T)], edge_col[:, 1, h, at],
                                        None, ALU.is_equal).then_inc(hot_ready, 1)

            def mask(t):
                dve.wait_ge(row_staged, t + 1)
                v.tensor_scalar(G[:, bass.ds(t, 1), :], count_row[:].rearrange("p (o n) -> p o n", o=1),
                                0.0, NO_EDGE, ALU.is_equal, ALU.mult).then_inc(mask_done, 1)

            with dve.Fori(0, NB) as b:
                for g in range(3):
                    dve.wait_ge(xhi_done, b * 3 + (g + 1))
                    v.tensor_tensor(xT_lo[:, 2 * g:2 * g + 2, :],
                                    p_x[:, g % 2, 0:2 * BT].rearrange("p (k n) -> p k n", k=2),
                                    xT_hi[:, 2 * g:2 * g + 2, :].bitcast(F32), ALU.subtract).then_inc(xlo_done, 1)
                one_hots(b * 2)
                mask(b * 2)
                for g in range(3):
                    dve.wait_ge(x1_hi_done, b * 3 + (g + 1))
                    at = bass.ds(b * BT, BT)
                    v.tensor_tensor(x1T[1][:, 2 * g:2 * g + 2, at],
                                    x1_f[:, g % 2, :].rearrange("p (k n) -> p k n", k=2),
                                    x1T[0][:, 2 * g:2 * g + 2, at].bitcast(F32), ALU.subtract).then_inc(x1_lo_done, 1)
                one_hots(b * 2 + 1)
                mask(b * 2 + 1)

        @block.scalar
        def _(act):
            nc.scalar.sem_inc(x1_lo_done, 1)
            nc.scalar.sem_inc(mask_done, 1)

            act.wait_ge(bias_in, 16)

            def stage_row(t):
                act.wait_ge(counted, t + 1)
                act.wait_ge(mask_done, t + 1)
                act.wait_ge(row_turned, t * 3 + 1)
                for i, (a, w) in enumerate(CH):
                    last = nc.scalar.activation(count_row[:, a:a + w], p_count[:, i, 0:w], ACT.Copy)
                last.then_inc(row_staged, 1)

            def keep_turned(t):
                for i in range(3):
                    k = 4 if i < 2 else 2
                    act.wait_ge(row_turned, t * 3 + (i + 2))
                    nc.scalar.activation(CT[:, 4 * i:4 * i + k, bass.ds(t * T, T)],
                                         p_turn[0:T, i, 0:k * T].rearrange("p (k q) -> p k q", q=T),
                                         ACT.Copy).then_inc(ct_done, 1)

            with act.Fori(0, NB) as b:
                for g in range(3):
                    act.wait_ge(x_turned, b * 3 + (g + 1))
                    nc.scalar.activation(xT_hi[:, 2 * g:2 * g + 2, :],
                                         p_x[:, g % 2, 0:2 * BT].rearrange("p (k n) -> p k n", k=2),
                                         ACT.Copy).then_inc(xhi_done, 1)
                stage_row(b * 2)
                for g in range(3):
                    act.wait_ge(x1_summed, b * 3 + (g + 1))
                    act.wait_ge(x1_lo_done, b * 3 + (g + 1))
                    for m in range(2):
                        last = nc.scalar.activation(x1_f[:, g % 2, m * BT:(m + 1) * BT], p_x[:, g % 2, m * BT:(m + 1) * BT],
                                                    ACT.Relu, bias=bias[:, 2 * g + m:2 * g + m + 1])
                    last.then_inc(x1_relu, 1)
                    act.wait_ge(x1_relu, b * 3 + (g + 1))
                    nc.scalar.activation(x1T[0][:, 2 * g:2 * g + 2, bass.ds(b * BT, BT)],
                                         x1_f[:, g % 2, :].rearrange("p (k n) -> p k n", k=2),
                                         ACT.Copy).then_inc(x1_hi_done, 1)
                keep_turned(b * 2)
                stage_row(b * 2 + 1)
                keep_turned(b * 2 + 1)

        @block.tensor
        def _(pe):
            pe.wait_ge(core.ident_ready, 2)
            pe.wait_ge(steps, 3)
            for a in range(2):
                for h in range(2):
                    nc.tensor.transpose(p_turn[0:T, 0, (2 * a + h) * EP:(2 * a + h + 1) * EP],
                                        edge_f[:, a, h * T:h * T + T], ident[0:EP, 0:EP])
            for a in range(2):
                last = nc.tensor.transpose(p_turn[:, 1, a * EP:(a + 1) * EP],
                                           dst_ends[:, a:a + 1].broadcast_to([EP, 128]), ident[0:EP, 0:EP])
            last.then_inc(edges_turned, 1)
            nc.tensor.sem_inc(hot_free, 2)
            nc.tensor.sem_inc(row_turned, 1)
            nc.tensor.sem_inc(xlo_done, 2)
            pe.wait_ge(consts, 8)
            pe.wait_ge(w_split, 2 * KD)
            pe.wait_ge(ranges_ready, 1)
            nc.tensor.sem_inc(ct_done, 1)

            def count(t):
                count_ = pe.value_load(range_i[0:1, 1, bass.ds(t, 1)], min_val=1, max_val=EP)
                before = pe.value_load(range_i[0:1, 2, bass.ds(t, 1)], min_val=0, max_val=EP * NT)
                for i, (a, w) in enumerate(CH):
                    nc.tensor.matmul(p_count[:, i, 0:w], ident_b[:], band[:, bass.ds(t * -T + (N - T + a), w)],
                                     start=True, stop=False, skip_group_check=True)
                with pe.Fori(0, count_) as j:
                    for h in range(2):
                        pe.wait_ge(hot_ready, (before + j) * 2 + (h + 1))
                        for i, (a, w) in enumerate(CH):
                            last = nc.tensor.matmul(p_count[:, i, 0:w], dst_hot[:, h, :], src_hot[:, h, a:a + w],
                                                    start=False, stop=False, skip_group_check=True)
                        last.then_inc(hot_free, 1)
                nc.tensor.matmul(p_count[:, 0, 0:2], zeros_b[:], src_hot[:, 0, 0:2], start=False, stop=True,
                                 skip_group_check=True).then_inc(counted, 1)

            def turn_row(t):
                pe.wait_ge(row_staged, t + 1)
                pe.wait_ge(ct_done, t * 3 + 1)
                for i in range(3):
                    for k in range(4 if i < 2 else 2):
                        q = 4 * i + k
                        last = nc.tensor.transpose(p_turn[0:T, i, k * T:k * T + T], count_row[:, q * T:q * T + T],
                                                   ident[0:T, 0:T])
                    last.then_inc(row_turned, 1)

            for b in range(NB):
                pe.wait_ge(x_loaded, 16 * (b + 1))
                for g in range(3):
                    if g == 2:
                        pe.wait_ge(xlo_done, 3 * b + 3)
                    elif b:
                        pe.wait_ge(x1_relu, 3 * b)
                    for k in (2 * g, 2 * g + 1):
                        for i in range(2):
                            last = nc.tensor.transpose(p_x[:, g % 2, (k % 2) * BT + i * T:(k % 2) * BT + (i + 1) * T],
                                                       x_in[:, i, k * 128:(k + 1) * 128], ident[0:T, 0:T])
                    last.then_inc(x_turned, 1)
                count(2 * b)
                turn_row(2 * b)
                pe.wait_ge(xlo_done, 3 * b + 5)
                for g in range(3):
                    if g == 2:
                        pe.wait_ge(x1_relu, 3 * b + 1)
                    for m in range(2):
                        for k in range(KD):
                            for n, (wp, xp) in enumerate(((w_hi, xT_hi), (w_hi, xT_lo), (w_lo, xT_hi))):
                                last = nc.tensor.matmul(p_x[:, g % 2, m * BT:(m + 1) * BT],
                                                        wp[:, k, (2 * g + m) * 128:(2 * g + m + 1) * 128], xp[:, k, :],
                                                        start=(m == 0 and k == 0 and n == 0),
                                                        stop=(k == KD - 1 and n == 2), skip_group_check=True)
                    last.then_inc(x1_summed, 1)
                count(2 * b + 1)
                turn_row(2 * b + 1)


def project(nc, core, xT, w, a_vec, h_rows, score_rows, iters, width, heads, col_src, u_col, v_col):
    per = max(1, heads // 2)
    cw = width // per
    hw = h_rows.shape[2]
    R = 2 * heads * NT
    ident, G = core.ident, core.G
    with ExitStack() as ctx:
        sb, pb, sem = core.tools(ctx)
        w_raw = sb("pw_raw", [128, 2, KD, width], F32)
        w_hi = sb("pw_hi", [128, 2, KD, width + 2 * per], F32R)
        w_lo = sb("pw_lo", [128, 2, KD, width + 2 * per], F32R)
        a_all = sb("a_all", [128, 2, 2, width], F32)
        wa = sb("wa", [128, 2, KD, 2 * per], F32)
        junk = sb("wa_junk", [128, 2, cw], BF16)
        junk_b = sb("max_junk", [T, 2, N], BF16)
        h_out = sb("h_out", [T, 2, NH, per, hw], F32)
        part = sb("part", [T, 2, 2, per, NT], F32)
        score = sb("score", [T, 2, heads, NT], F32)
        turned = sb("turned", [R, T], F32)
        src_row = sb("src_row", [T, 2, N], F32)
        most = sb("most", [T, heads, NT], F32)
        tmp = sb("tmp", [T, heads, NT], F32)
        tmp2 = sb("tmp2", [T, heads, NT], F32)
        turned_uv = sb("turned_uv", [iters * heads * NT, 2, T], F32)
        p_h = pb("p_h", [T, 4, 512])
        p_s = pb("p_s", [128, 512])

        w_in = [sem(f"pw_in{u}") for u in range(2)]
        wa_steps = sem("wa_steps")
        wa_summed = sem("wa_summed")
        maxed = sem("maxed")
        max_steps = sem("max_steps")
        hi_done = sem("hi_done")
        split_done = sem("split_done")
        wa_split = sem("wa_split")
        h_summed = sem("h_summed")
        h_kept = sem("h_kept")
        h_stored = [sem(f"h_stored{u}") for u in range(2)]
        ones_set = sem("ones_set")
        score_done = sem("score_done")
        score_turned = sem("score_turned")
        turned_kept = sem("turned_kept")
        row_stored = sem("row_stored")
        row_in = [sem(f"row_in{u}") for u in range(2)]
        uv_done = sem("uv_done")

        block = ctx.enter_context(nc.Block())

        def row_free(i, h):
            return i * (heads * NT) + (max(0, h - 1) * NT + 2)

        @block.sync
        def _(sp):
            def load_w(i):
                for u in range(2):
                    q = i * 2 + u
                    sp.wait_ge(split_done, q + 1)
                    sp.wait_ge(wa_split, q + 1)
                    sp.dma_start(w_raw[:, u, :, :], w[bass.ds(q, 1)].rearrange("o (k p) c -> p (o k) c", p=128)).then_inc(w_in[u], 16)
                    sp.dma_start(a_all[:, u, :, :], a_vec[bass.ds(q, 1)].broadcast_to([128, 2, width])).then_inc(w_in[u], 16)

            def store_and_spread(i):
                for u in range(2):
                    for part_no in range(2):
                        wait_apart(sp, h_kept, i * (2 * NT) + (NT * u + NH * (part_no + 1) + 4))
                        for g in range(per):
                            to = h_rows[bass.ds(i * (2 * per) + (u * per + g), 1), part_no * DH:(part_no + 1) * DH, :]
                            sp.dma_start(to.rearrange("o (t p) c -> p (o t) c", p=T),
                                         h_out[:, part_no, :, g, :]).then_inc(h_stored[part_no], 16)
                wait_apart(sp, turned_kept, i + 1)
                sp.dma_start(score_rows[bass.ds(i * R, R), :], turned[:]).then_inc(row_stored, 16)
                wait_apart(sp, row_stored, i * 16 + 32)
                for h in range(heads):
                    wait_apart(sp, maxed, row_free(i, h))
                    sp.dma_start(src_row[:, h % 2, :],
                                 score_rows[bass.ds(i * R + h * NT, NT), :].rearrange("(o t) p -> o (t p)", o=1)
                                 .broadcast_to([T, N])).then_inc(row_in[h % 2], 16)

            load_w(0)
            with sp.Fori(0, iters - 1) as i:
                load_w(i + 1)
                store_and_spread(i)
            store_and_spread(iters - 1)
            for u in range(2):
                sp.wait_ge(h_stored[u], 16 * per * (2 * iters + 1))
            for kind in range(2):
                sp.wait_ge(turned_kept, iters + kind + 1)
                sp.dma_start(core.uv_rows[kind, 0:iters * heads * NT, :], turned_uv[:, kind, :]).then_inc(row_stored, 16)
            sp.wait_ge(row_stored, 16 * (iters + 3))

        @block.gpsimd
        def _(pool):
            pool.sem_inc(split_done, 2)
            if hw > cw:
                pool.memset(h_out[:, :, :, :, cw:], 0.0).then_inc(ones_set, 1)
                pool.wait_ge(ones_set, 1)
                pool.memset(h_out[:, :, :, :, cw:cw + 1], 1.0).then_inc(ones_set, 1)
            with pool.Fori(0, iters) as i:
                for u in range(2):
                    pool.wait_ge(w_in[u], i * 32 + 32)
                    wait_apart(pool, h_summed, i * (2 * NT) + (u + 1) * NT)
                    pool.tensor_copy(w_hi[:, u, :, 0:width], w_raw[:, u, :, :]).then_inc(hi_done, 1)
                    pool.wait_ge(hi_done, i * 2 + (u + 1))
                    pool.tensor_tensor(w_lo[:, u, :, 0:width], w_raw[:, u, :, :],
                                       w_hi[:, u, :, 0:width].bitcast(F32), ALU.subtract).then_inc(split_done, 1)

        @block.vector
        def _(dve):
            v = nc.vector
            nc.vector.sem_inc(wa_split, 2)
            nc.vector.sem_inc(score_done, 1)
            nc.vector.sem_inc(wa_summed, 2)
            nc.vector.sem_inc(maxed, 2)
            SUMS = KD * 2 * per

            def weights_by_a(i):
                for u in range(2):
                    wait_apart(dve, w_in[u], i * 32 + 32)
                    for k in range(KD):
                        for kind in range(2):
                            for g in range(per):
                                n = (k * 2 + kind) * per + g
                                wait_apart(dve, wa_summed, i * (2 * SUMS) + (u * SUMS + n + 1))
                                v.tensor_tensor_reduce(out=junk[:, n % 2, :], in0=w_raw[:, u, k, g * cw:(g + 1) * cw],
                                                       in1=a_all[:, u, kind, g * cw:(g + 1) * cw], scale=1.0, scalar=0.0,
                                                       op0=ALU.mult, op1=ALU.add,
                                                       accum_out=wa[:, u, k, kind * per + g:kind * per + g + 1]
                                                       ).then_inc(wa_summed, 1)
                    dve.wait_ge(wa_summed, i * (2 * SUMS) + ((u + 1) * SUMS + 2))
                    dve.wait_ge(h_summed, i * (2 * NT) + (u + 1) * NT)
                    v.tensor_copy(w_hi[:, u, :, width:], wa[:, u, :, :]).then_inc(wa_steps, 1)
                    dve.wait_ge(wa_steps, i * 2 + (u + 1))
                    v.tensor_tensor(w_lo[:, u, :, width:], wa[:, u, :, :], w_hi[:, u, :, width:].bitcast(F32),
                                    ALU.subtract).then_inc(wa_split, 1)

            def scores(i):
                dve.wait_ge(h_kept, i * (2 * NT) + (2 * NT + 4))
                if per > 1:
                    v.tensor_copy(score[:], part[:].rearrange("p a u g t -> p a (u g) t")).then_inc(score_done, 1)
                else:
                    v.tensor_tensor(score[:], part[:, :, 0], part[:, :, 1], ALU.add).then_inc(score_done, 1)
                dve.wait_ge(score_done, i + 2)
                hs = bass.ds(i * heads, heads)
                v.tensor_copy(col_src[0][:, hs, :], score[:, 0])
                v.tensor_scalar(col_src[1][:, hs, :], score[:, 0], SLOPE, None, ALU.mult)
                for h in range(heads):
                    per_slot = (heads + 1) // 2
                    wait_apart(dve, row_in[h % 2], i * (16 * per_slot) + 16 * (h // 2 + 1))
                    for t in range(NT):
                        wait_apart(dve, maxed, i * (heads * NT) + (h * NT + t + 1))
                        v.tensor_tensor_reduce(out=junk_b[:, t % 2, :], in0=src_row[:, h % 2, :], in1=G[:, t, :], scale=1.0,
                                               scalar=NO_EDGE, op0=ALU.add, op1=ALU.max,
                                               accum_out=most[:, h, t:t + 1]).then_inc(maxed, 1)
                dve.wait_ge(maxed, i * (heads * NT) + (heads * NT + 2))
                v.tensor_tensor(tmp[:], most[:], score[:, 1], ALU.add).then_inc(max_steps, 1)
                dve.wait_ge(max_steps, i * 3 + 1)
                v.scalar_tensor_tensor(tmp2[:], tmp[:], SLOPE, tmp[:], ALU.mult, ALU.max).then_inc(max_steps, 1)
                dve.wait_ge(max_steps, i * 3 + 2)
                v.tensor_tensor(u_col[:, hs, :], score[:, 1], tmp2[:], ALU.subtract)
                v.scalar_tensor_tensor(v_col[:, hs, :], score[:, 1], SLOPE, tmp2[:], ALU.mult, ALU.subtract).then_inc(max_steps, 1)
                dve.wait_ge(max_steps, i * 3 + 3)

            weights_by_a(0)
            with dve.Fori(0, iters - 1) as i:
                weights_by_a(i + 1)
                scores(i)
            scores(iters - 1)
            nc.vector.sem_inc(uv_done, 1)

        @block.scalar
        def _(act):
            a = nc.scalar
            a.sem_inc(h_kept, 4)
            for u in range(2):
                a.sem_inc(h_stored[u], 16 * per)
            a.sem_inc(row_stored, 16)
            if hw > cw:
                act.wait_ge(ones_set, 2)
            with act.Fori(0, iters) as i:
                act.wait_ge(score_done, i + 1)
                for u in range(2):
                    for t in range(NT):
                        if t % NH == 0:
                            act.wait_ge(h_stored[t // NH], i * (32 * per) + 16 * per * (u + 1))
                        act.wait_ge(h_summed, i * (2 * NT) + (2 * NT + u * NT + t + 1))
                        a.activation(h_out[:, t // NH, t % NH, :, 0:cw], p_h[:, (u * NT + t) % 4, 0:width].rearrange("p (g c) -> p g c", g=per), ACT.Copy)
                        a.activation(part[:, :, u, :, t], p_h[:, (u * NT + t) % 4, width:width + 2 * per].rearrange("p (a g) -> p a g", a=2),
                                     ACT.Copy).then_inc(h_kept, 1)
                act.wait_ge(score_turned, i + 1)
                act.wait_ge(row_stored, i * 16 + 16)
                a.activation(turned[:], p_s[0:R, 0:T], ACT.Copy).then_inc(turned_kept, 1)
            for kind in range(2):
                act.wait_ge(score_turned, iters + kind + 1)
                a.activation(turned_uv[:, kind, :], p_s[0:iters * heads * NT, 0:T], ACT.Copy).then_inc(turned_kept, 1)

        @block.tensor
        def _(pe):
            nc.tensor.sem_inc(h_summed, 2 * NT)
            with pe.Fori(0, iters) as i:
                for u in range(2):
                    pe.wait_ge(split_done, i * 2 + (u + 3))
                    pe.wait_ge(wa_split, i * 2 + (u + 3))
                    for t in range(NT):
                        pe.wait_ge(h_kept, i * (2 * NT) + (u * NT + t + 1))
                        rows = slice(t * T, (t + 1) * T)
                        for k in range(KD):
                            for n, (xp, wp) in enumerate(((xT[0], w_hi), (xT[0], w_lo), (xT[1], w_hi))):
                                last = nc.tensor.matmul(p_h[:, (u * NT + t) % 4, 0:width + 2 * per], xp[:, k, rows], wp[:, u, k, :],
                                                        start=(k == 0 and n == 0), stop=(k == KD - 1 and n == 2))
                        last.then_inc(h_summed, 1)
                pe.wait_ge(score_done, i + 2)
                nc.tensor.transpose(p_s[0:R, 0:T], score[:].rearrange("p a h t -> p (a h t)"), ident[0:T, 0:T]).then_inc(score_turned, 1)
            pe.wait_ge(uv_done, 1)
            for kind, col in enumerate((u_col, v_col)):
                pe.wait_ge(turned_kept, iters + kind)
                nc.tensor.transpose(p_s[0:iters * heads * NT, 0:T], col[:, 0:iters * heads, :].rearrange("p h t -> p (h t)"),
                                    ident[0:T, 0:T]).then_inc(score_turned, 1)


def aggregate(nc, core, h_rows, col_src, bias, turned_rows, iters, layer):
    ident, CT = core.ident, core.CT
    parts = 1 if layer == 0 else 2
    W = N // parts
    DT = NT // parts
    C = C0 if layer == 0 else C1
    HW = HC0 if layer == 0 else C1
    GROUPS = 2 * parts
    STEPS = GROUPS * NT
    BANKS = 5
    IN_BANK = DT // BANKS
    CW = 2 * C // 128 if layer == 0 else C // 128
    TURNS = 1 if layer == 0 else GROUPS
    N_OUT = TURNS * CW
    SLOTS = 3 if layer == 0 else 2
    PER_HEAD = NT * parts
    RING = 4
    LOADS = 48 + 16 * layer
    with ExitStack() as ctx:
        sb, pb, sem = core.tools(ctx)
        uv = sb("uv", [T, 2, 2, N], F32)
        h_in = sb("h_in", [T, 2, NT, HW], F32)
        e = sb("e", [T, RING, W], F32)
        p = sb("p", [T, RING, W], F32)
        res = sb("res", [T, DT, 2 * C if layer == 0 else C], F32)
        sums = sb("sums", [T, 2, DT], F32)
        ones = sb("ones", [T, 2], F32)
        b_col = sb("b_col", [128, iters, 2 * C // 128], F32)
        out_f = sb("out_f", [128, SLOTS, W], F32)
        z = sb("z", [128, 2, 3, W], F32) if layer else None
        p_o = pb("p_o", [T, BANKS, 512])
        p_sum = pb("p_sum", [T, 512]) if layer else None
        p_t = pb("p_t", [128, 3 if layer == 0 else 2, 512])

        loaded = [sem(f"loaded{i}") for i in range(2)]
        bias_in = sem("bias_in")
        ones_set = sem("ones_set")
        v_ready = sem("v_ready")
        e_ready = sem("e_ready")
        exp_ready = sem("exp_ready")
        p_ready = sem("p_ready")
        p_used = sem("p_used")
        sum_steps = sem("sum_steps")
        bank_free = sem("bank_free")
        turned = sem("turned")
        kept = sem("kept")
        elu_low = sem("elu_low")
        elu_up = sem("elu_up")
        elu_exped = sem("elu_exped")
        out_ready = sem("out_ready")
        stored = [sem(f"stored{i}") for i in range(SLOTS)]

        block = ctx.enter_context(nc.Block())

        def at(g):
            q, s = divmod(g, NT)
            return (*divmod(q, parts), s)

        @block.sync
        def _(sp):
            sp.dma_start(b_col[:], bias).then_inc(bias_in, 16)

            def load(i, s):
                wait_apart(sp, e_ready, i * STEPS + (s + 1) * PER_HEAD)
                wait_apart(sp, p_used, i * STEPS + (s + 1) * PER_HEAD)
                head = i * 2 + s
                for kind in range(2):
                    sp.dma_start(uv[:, s, kind, :],
                                 core.uv_rows[kind, bass.ds(head * NT, NT), :].rearrange("(o t) p -> o (t p)", o=1)
                                 .broadcast_to([T, N])).then_inc(loaded[s], 16)
                if layer == 0:
                    sp.dma_start(h_in[:, s], h_rows[bass.ds(head, 1)].rearrange("o (t p) c -> p (o t) c", p=T)).then_inc(loaded[s], 16)
                else:
                    for q in range(2):
                        sp.dma_start(h_in[:, s, :, q * HALF1:(q + 1) * HALF1],
                                     h_rows[bass.ds(head * 2 + q, 1)].rearrange("o (t p) c -> p (o t) c", p=T)).then_inc(loaded[s], 16)

            def store(i, turn):
                hh, part = divmod(turn, parts)
                for c in range(CW):
                    n = turn * CW + c
                    chunk = i * (2 * C // 128) + (hh * CW + c)
                    wait_apart(sp, out_ready, i * N_OUT + (n + 1 + 2 * layer))
                    sp.dma_start(turned_rows[bass.ds(chunk, 1), :, part * W:(part + 1) * W].rearrange("o p n -> p (o n)"),
                                 out_f[:, n % SLOTS, :]).then_inc(stored[n % SLOTS], 16)

            load(0, 0)
            load(0, 1)
            with sp.Fori(0, iters - 1) as i:
                if layer == 0:
                    load(i + 1, 0)
                    load(i + 1, 1)
                    store(i, 0)
                else:
                    store(i, 0)
                    load(i + 1, 0)
                    store(i, 1)
                    store(i, 2)
                    load(i + 1, 1)
                    store(i, 3)
            for turn in range(TURNS):
                store(iters - 1, turn)
            for s in range(SLOTS):
                sp.wait_ge(stored[s], 16 * (1 + iters * N_OUT // SLOTS))

        @block.scalar
        def _(act):
            a = nc.scalar
            for s in range(SLOTS):
                a.sem_inc(stored[s], 16)
            a.sem_inc(bank_free, BANKS)
            act.wait_ge(bias_in, 16)

            with act.Fori(0, iters) as i:
                def low(g):
                    hh, part, s = at(g)
                    if s == 0 and part == 0:
                        act.wait_ge(loaded[hh], i * LOADS + LOADS)
                    wait_apart(act, p_ready, i * STEPS + (g + 1))
                    a.activation(e[:, g % RING, :], uv[:, hh, 1, part * W:(part + 1) * W], ACT.Identity,
                                 bias=col_src[1][:, bass.ds(i * 2 + hh, 1), s]).then_inc(v_ready, 1)

                def exp(g):
                    act.wait_ge(e_ready, i * STEPS + (g + 1 + 2 * PER_HEAD))
                    a.activation(e[:, g % RING, :], e[:, g % RING, :], ACT.Exp).then_inc(exp_ready, 1)

                def leave(q):
                    hh, part = divmod(q, parts)
                    act.wait_ge(sum_steps, i * (2 * GROUPS) + (2 * q + 2))
                    if q == 0 or layer:
                        act.wait_ge(turned, i * N_OUT + (q + 1) * CW)
                    for b in range(BANKS):
                        for n in range(IN_BANK):
                            d = b * IN_BANK + n
                            to = res[:, d, hh * C:(hh + 1) * C] if layer == 0 else res[:, d, :]
                            last = a.activation(to, p_o[:, b, n * 256:n * 256 + C], ACT.Copy, scale=sums[:, 1, d:d + 1])
                        last.then_inc(bank_free, 1)

                def keep(n):
                    act.wait_ge(turned, i * N_OUT + (n + 1 + CW))
                    b_at = b_col[:, bass.ds(i, 1), (n // CW // parts) * CW + n % CW]
                    if layer == 0:
                        wait_apart(act, stored[n % SLOTS], i * (16 * N_OUT // SLOTS) + 16 * (n // SLOTS + 1))
                        to, func, sem_to = out_f[:, n % SLOTS, :], ACT.Relu, out_ready
                        views = ((0, 4), (1, 4), (2, 2))
                    else:
                        wait_apart(act, out_ready, i * N_OUT + (n + 1))
                        to, func, sem_to = z[:, n % 2, 0, :], ACT.Identity, kept
                        views = ((0, 4), (1, 1))
                    for b, k in views:
                        last = a.activation(to[:, 4 * b * T:(4 * b + k) * T], p_t[:, b, 0:k * T], func, bias=b_at)
                    last.then_inc(sem_to, 1)

                def elu_exp(n):
                    act.wait_ge(elu_low, i * N_OUT + (n + 1))
                    a.activation(z[:, n % 2, 1, :], z[:, n % 2, 1, :], ACT.Exp).then_inc(elu_exped, 1)

                low(0)
                for g in range(STEPS):
                    if g + 1 < STEPS:
                        low(g + 1)
                    exp(g)
                    q, s = divmod(g, NT)
                    if q and s == 1:
                        leave(q - 1)
                    if layer and q and s >= 3 and s % 2:
                        keep((q - 1) * CW + (s - 3) // 2)
                        elu_exp((q - 1) * CW + (s - 3) // 2)
                leave(GROUPS - 1)
                for c in range(CW):
                    keep((TURNS - 1) * CW + c)
                    if layer:
                        elu_exp((TURNS - 1) * CW + c)

        @block.vector
        def _(dve):
            v = nc.vector
            v.sem_inc(p_ready, RING)
            v.sem_inc(e_ready, 2 * PER_HEAD)
            if layer:
                v.sem_inc(out_ready, 2)
            v.memset(ones[:], 1.0).then_inc(ones_set, 1)
            with dve.Fori(0, iters) as i:
                def upper(g):
                    hh, part, s = at(g)
                    dve.wait_ge(v_ready, i * STEPS + (g + 1))
                    v.scalar_tensor_tensor(e[:, g % RING, :], uv[:, hh, 0, part * W:(part + 1) * W],
                                           col_src[0][:, bass.ds(i * 2 + hh, 1), s], e[:, g % RING, :],
                                           ALU.add, ALU.max).then_inc(e_ready, 1)

                def weigh(g):
                    hh, part, s = at(g)
                    dve.wait_ge(exp_ready, i * STEPS + (g + 1))
                    dve.wait_ge(p_used, i * STEPS + (g + 1 + 2 * PER_HEAD - RING))
                    v.scalar_tensor_tensor(p[:, g % RING, :], e[:, g % RING, :], 1.0, CT[:, s, part * W:(part + 1) * W],
                                           ALU.min, ALU.mult).then_inc(p_ready, 1)

                def divisors(q):
                    dve.wait_ge(p_used, i * STEPS + ((q + 1) * NT + 2 * PER_HEAD))
                    if layer == 0:
                        at_sums = p_o[:, :, :].rearrange("p b (n c) -> p b n c", n=2)[:, :, :, C]
                        to = sums[:, 0, :].rearrange("p (b n) -> p b n", n=2)
                    else:
                        at_sums, to = p_sum[:, 0:DT], sums[:, 0, :]
                    v.tensor_scalar(to, at_sums, 1e-16, None, ALU.add).then_inc(sum_steps, 1)
                    dve.wait_ge(sum_steps, i * (2 * GROUPS) + (2 * q + 1))
                    v.reciprocal(sums[:, 1, :], sums[:, 0, :]).then_inc(sum_steps, 1)

                def elu(n):
                    dve.wait_ge(kept, i * N_OUT + (n + 1))
                    v.tensor_scalar(z[:, n % 2, 1, :], z[:, n % 2, 0, :], 0.0, None, ALU.min).then_inc(elu_low, 1)
                    v.tensor_scalar(z[:, n % 2, 2, :], z[:, n % 2, 0, :], 0.0, None, ALU.max).then_inc(elu_up, 1)
                    dve.wait_ge(elu_up, i * N_OUT + (n + 1))
                    dve.wait_ge(elu_exped, i * N_OUT + (n + 1))
                    dve.wait_ge(stored[n % SLOTS], i * (16 * N_OUT // SLOTS) + 16 * (n // SLOTS + 1))
                    v.scalar_tensor_tensor(out_f[:, n % SLOTS, :], z[:, n % 2, 1, :], -1.0, z[:, n % 2, 2, :],
                                           ALU.add, ALU.add).then_inc(out_ready, 1)

                upper(0)
                for g in range(STEPS):
                    if g + 1 < STEPS:
                        upper(g + 1)
                    weigh(g)
                    q, s = divmod(g, NT)
                    if q and s == 1:
                        divisors(q - 1)
                    if layer and q and s >= 3 and s % 2:
                        elu((q - 1) * CW + (s - 3) // 2)
                divisors(GROUPS - 1)
                if layer:
                    for c in range(CW):
                        elu((TURNS - 1) * CW + c)

        @block.tensor
        def _(pe):
            nc.tensor.sem_inc(p_used, 2 * PER_HEAD)
            nc.tensor.sem_inc(turned, CW)
            pe.wait_ge(ones_set, 1)
            with pe.Fori(0, iters) as i:
                def turn(n):
                    turn_no, c = divmod(n, CW)
                    if n:
                        pe.wait_ge(kept if layer else out_ready, i * N_OUT + n)
                    for d in range(DT):
                        last = nc.tensor.transpose(p_t[:, d // 4, (d % 4) * T:(d % 4 + 1) * T],
                                                   res[:, d, c * 128:(c + 1) * 128], ident[0:T, 0:T])
                    last.then_inc(turned, 1)

                for g in range(STEPS):
                    hh, part, s = at(g)
                    q = g // NT
                    if s == 0 and part == 0:
                        pe.wait_ge(loaded[hh], i * LOADS + LOADS)
                    pe.wait_ge(p_ready, i * STEPS + (g + 1 + RING))
                    for d in range(DT):
                        b, n = divmod(d, IN_BANK)
                        if s == 0 and n == 0:
                            pe.wait_ge(bank_free, i * (BANKS * GROUPS) + (BANKS * q + b + 1))
                        width = C + 1 if layer == 0 else C
                        last = nc.tensor.matmul(p_o[:, b, n * 256:n * 256 + width], p[:, g % RING, d * T:(d + 1) * T],
                                                h_in[:, hh, s, 0:width], start=(s == 0 and n == 0), stop=(s == NT - 1),
                                                skip_group_check=True)
                        if layer:
                            last = nc.tensor.matmul(p_sum[:, d:d + 1], p[:, g % RING, d * T:(d + 1) * T], ones[:, 0:1],
                                                    start=(s == 0 and d == 0), stop=(s == NT - 1), skip_group_check=True)
                    last.then_inc(p_used, 1)
                    if layer and q and s >= 1 and s % 2 and s < 9:
                        if s == 1:
                            pe.wait_ge(bank_free, i * (BANKS * GROUPS) + BANKS * (q + 1))
                        turn((q - 1) * CW + (s - 1) // 2)
                pe.wait_ge(bank_free, i * (BANKS * GROUPS) + BANKS * (GROUPS + 1))
                for c in range(CW):
                    turn((TURNS - 1) * CW + c)


def from_turned(nc, core, turned_rows, K, w, out_rows, x=None, bias=None, a_vec=None, score_rows=None,
                col_src=None):
    ident, G = core.ident, core.G
    CW = D // 2
    PARTS = 3 if K % 3 == 0 else 4
    KP, KH = K // PARTS, K // 2
    extra = 2 if a_vec is not None else 0
    IN = [16 * (1 + extra if n == 0 else 1) for n in range(PARTS)]
    with ExitStack() as ctx:
        sb, pb, sem = core.tools(ctx)
        w_raw = sb("fw_raw", [128, K, CW], F32)
        w_hi = sb("fw_hi", [128, K, CW + extra], F32R)
        w_lo = sb("fw_lo", [128, K, CW + extra], F32R)
        f_raw = sb("f_raw", [128, 2, KH, T], F32)
        f_hi = sb("f_hi", [128, 2, KH, T], F32R)
        f_lo = sb("f_lo", [128, 2, KH, T], F32R)
        biased = sb("biased", [T, 2, CW], F32) if x is not None else None
        b_row = sb("b_row", [T, D], F32) if x is not None else None
        p_y = pb("p_y", [T, 2, 512])
        if extra:
            a_row = sb("a_row", [128, 2, CW], F32)
            wa = sb("wa2", [128, K, 2], F32)
            junk = sb("wa2_junk", [128, 2, CW], BF16)
            junk_b = sb("max2_junk", [T, 2, N], BF16)
            part = sb("part2", [T, 2, 2, NT], F32)
            score = sb("score2", [T, 2, NT], F32)
            turned = sb("turned2", [4 * NT, T], F32)
            turned_b = sb("turned2b", [4 * NT, T], F32)
            src_row = sb("src_row2", [T, N], F32)
            uv = sb("uv_col2", [T, 2, NT], F32)
            most = sb("most2", [T, NT], F32)
            tmp = sb("tmp_a", [T, NT], F32)
            tmp2 = sb("tmp_b", [T, NT], F32)
            p_s = pb("p_s2", [128, 512])

        w_in = [sem(f"fw_in{i}") for i in range(PARTS)]
        small_in = sem("small_in")
        f_in = [sem(f"f_in{i}") for i in range(2)]
        hi_done = sem("w_hi_done")
        w_split = sem("w_split")
        wa_steps = sem("wa_steps2")
        wa_summed = sem("wa_summed2")
        maxed = sem("maxed2")
        wa_split = sem("wa_split2")
        f_hi_done = sem("f_hi_done")
        f_lo_done = sem("f_lo_done")
        piece_used = sem("piece_used")
        y_left = sem("y_left")
        y_biased = sem("y_biased")
        steps = sem("fsteps")
        turned_done = sem("turned_done")
        turned_kept = sem("turned_kept2")
        rows_stored = sem("rows_stored2")
        row_in = sem("row_in2")

        block = ctx.enter_context(nc.Block())

        @block.sync
        def _(sp):
            if x is not None:
                sp.dma_start(out_rows[:], rows_of(x)).then_inc(small_in, 16)
                sp.dma_start(b_row[:], bias.rearrange("(o f) -> o f", o=1).broadcast_to([T, D])).then_inc(small_in, 16)
            with sp.Fori(0, 2) as half:
                for part_no in range(PARTS):
                    wait_apart(sp, w_split, half * PARTS + (part_no + 1))
                    if extra:
                        wait_apart(sp, wa_split, half + 1)
                    if extra and part_no == 0:
                        for kind in range(2):
                            sp.dma_start(a_row[:, kind, :], a_vec[kind:kind + 1, bass.ds(half * CW, CW)].broadcast_to([128, CW])).then_inc(w_in[0], 16)
                    ks = slice(part_no * KP, (part_no + 1) * KP)
                    sp.dma_start(w_raw[:, ks, :],
                                 w.rearrange("(k p) c -> p k c", p=128)[:, ks, bass.ds(half * CW, CW)]).then_inc(w_in[part_no], 16)
                for t in range(NT):
                    for kh in range(2):
                        wait_apart(sp, f_lo_done, half * (2 * NT) + (2 * t + kh + 1))
                        sp.dma_start(f_raw[:, kh, :, :],
                                     turned_rows[kh * KH:(kh + 1) * KH, :, t * T:(t + 1) * T].rearrange("k p n -> p k n")).then_inc(f_in[kh], 16)
            if extra:
                sp.wait_ge(turned_kept, 1)
                sp.dma_start(score_rows[0:2 * NT, :], turned[0:2 * NT, :]).then_inc(rows_stored, 16)
                sp.wait_ge(rows_stored, 16)
                sp.dma_start(src_row[:], score_rows[0:NT, :].rearrange("(o t) p -> o (t p)", o=1).broadcast_to([T, N])).then_inc(row_in, 16)
                sp.wait_ge(turned_kept, 2)
                sp.dma_start(core.uv_rows[0, 0:NT, :], turned_b[0:NT, :]).then_inc(rows_stored, 16)
                sp.dma_start(core.uv_rows[1, 0:NT, :], turned_b[NT:2 * NT, :]).then_inc(rows_stored, 16)
                sp.wait_ge(rows_stored, 48)

        @block.gpsimd
        def _(pool):
            pool.sem_inc(w_split, PARTS)
            with pool.Fori(0, 2) as half:
                for part_no in range(PARTS):
                    ks = slice(part_no * KP, (part_no + 1) * KP)
                    pool.wait_ge(w_in[part_no], half * IN[part_no] + IN[part_no])
                    wait_apart(pool, piece_used, half * (2 * NT) + 2 * NT)
                    pool.tensor_copy(w_hi[:, ks, 0:CW], w_raw[:, ks, :]).then_inc(hi_done, 1)
                    pool.wait_ge(hi_done, half * PARTS + (part_no + 1))
                    pool.tensor_tensor(w_lo[:, ks, 0:CW], w_raw[:, ks, :], w_hi[:, ks, 0:CW].bitcast(F32),
                                       ALU.subtract).then_inc(w_split, 1)

        @block.vector
        def _(dve):
            v = nc.vector
            v.sem_inc(f_lo_done, 2)
            if x is not None:
                v.sem_inc(y_left, 2)
                dve.wait_ge(small_in, 32)
            else:
                v.sem_inc(wa_split, 1)
                v.sem_inc(wa_summed, 2)
            with dve.Fori(0, 2) as half:
                if extra:
                    for part_no in range(PARTS):
                        wait_apart(dve, w_in[part_no], half * IN[part_no] + IN[part_no])
                        for k in range(part_no * KP, (part_no + 1) * KP):
                            for kind in range(2):
                                wait_apart(dve, wa_summed, half * (2 * K) + (2 * k + kind + 1))
                                v.tensor_tensor_reduce(out=junk[:, kind, :], in0=w_raw[:, k, :], in1=a_row[:, kind, :],
                                                       scale=1.0, scalar=0.0, op0=ALU.mult, op1=ALU.add,
                                                       accum_out=wa[:, k, kind:kind + 1]).then_inc(wa_summed, 1)
                    dve.wait_ge(wa_summed, half * (2 * K) + (2 * K + 2))
                    dve.wait_ge(piece_used, half * (2 * NT) + 2 * NT)
                    v.tensor_copy(w_hi[:, :, CW:], wa[:]).then_inc(wa_steps, 1)
                    dve.wait_ge(wa_steps, half + 1)
                    v.tensor_tensor(w_lo[:, :, CW:], wa[:], w_hi[:, :, CW:].bitcast(F32), ALU.subtract).then_inc(wa_split, 1)

                def leave(t):
                    dve.wait_ge(piece_used, half * (2 * NT) + (2 * t + 2 + 2 * NT))
                    cols = bass.ds(half * CW, CW)
                    v.tensor_tensor(biased[:, t % 2, :], p_y[:, t % 2, 0:CW], b_row[:, cols], ALU.add).then_inc(y_left, 1)
                    dve.wait_ge(y_left, half * NT + (t + 3))
                    v.scalar_tensor_tensor(out_rows[:, t, cols], biased[:, t % 2, :], 0.0, out_rows[:, t, cols],
                                           ALU.max, ALU.add).then_inc(y_biased, 1)

                for t in range(NT):
                    for kh in range(2):
                        dve.wait_ge(f_hi_done, half * (2 * NT) + (2 * t + kh + 1))
                        v.tensor_tensor(f_lo[:, kh], f_raw[:, kh], f_hi[:, kh].bitcast(F32), ALU.subtract).then_inc(f_lo_done, 1)
                    if x is not None and t:
                        leave(t - 1)
                if x is not None:
                    leave(NT - 1)
            if extra:
                step = Chain(dve, steps)
                dve.wait_ge(y_left, 2 * NT + 2)
                step(v.tensor_tensor(score[:], part[:, :, 0], part[:, :, 1], ALU.add))
                v.tensor_copy(col_src[0][:, 0, :], score[:, 0])
                step(v.tensor_scalar(col_src[1][:, 0, :], score[:, 0], SLOPE, None, ALU.mult))
                dve.wait_ge(row_in, 16)
                for t in range(NT):
                    if t >= 2:
                        dve.wait_ge(maxed, t - 1)
                    v.tensor_tensor_reduce(out=junk_b[:, t % 2, :], in0=src_row[:], in1=G[:, t, :], scale=1.0, scalar=NO_EDGE,
                                           op0=ALU.add, op1=ALU.max, accum_out=most[:, t:t + 1]).then_inc(maxed, 1)
                dve.wait_ge(maxed, NT)
                step(v.tensor_tensor(tmp[:], most[:], score[:, 1], ALU.add))
                step(v.scalar_tensor_tensor(tmp2[:], tmp[:], SLOPE, tmp[:], ALU.mult, ALU.max))
                v.tensor_tensor(uv[:, 0], score[:, 1], tmp2[:], ALU.subtract)
                step(v.scalar_tensor_tensor(uv[:, 1], score[:, 1], SLOPE, tmp2[:], ALU.mult, ALU.subtract))

        @block.scalar
        def _(act):
            a = nc.scalar
            if extra:
                a.sem_inc(y_left, 2)
            with act.Fori(0, 2) as half:
                def leave(t):
                    act.wait_ge(piece_used, half * (2 * NT) + (2 * t + 2 + 2 * NT))
                    a.activation(out_rows[:, t, bass.ds(half * CW, CW)], p_y[:, t % 2, 0:CW], ACT.Copy)
                    a.activation(part[:, :, bass.ds(half, 1), t], p_y[:, t % 2, CW:CW + 2].rearrange("p (a o) -> p a o", o=1),
                                 ACT.Copy).then_inc(y_left, 1)

                for t in range(NT):
                    for kh in range(2):
                        act.wait_ge(f_in[kh], half * (16 * NT) + 16 * (t + 1))
                        act.wait_ge(piece_used, half * (2 * NT) + (2 * t + kh + 2 * NT - 1))
                        a.activation(f_hi[:, kh], f_raw[:, kh], ACT.Copy).then_inc(f_hi_done, 1)
                    if extra and t:
                        leave(t - 1)
                if extra:
                    leave(NT - 1)
            if extra:
                for n, to in enumerate((turned, turned_b)):
                    act.wait_ge(turned_done, n + 1)
                    a.activation(to[0:2 * NT, :], p_s[0:2 * NT, 0:T], ACT.Copy).then_inc(turned_kept, 1)

        @block.tensor
        def _(pe):
            nc.tensor.sem_inc(piece_used, 2 * NT)
            with pe.Fori(0, 2) as half:
                if extra:
                    pe.wait_ge(wa_split, half + 2)
                for t in range(NT):
                    pe.wait_ge(y_left, half * NT + (t + 1))
                    for kh in range(2):
                        pe.wait_ge(f_lo_done, half * (2 * NT) + (2 * t + kh + 3))
                        for kk in range(KH):
                            k = kh * KH + kk
                            if t == 0 and k % KP == 0:
                                pe.wait_ge(w_split, half * PARTS + (k // KP + 1 + PARTS))
                            for n, (fp, wp) in enumerate(((f_hi, w_hi), (f_hi, w_lo), (f_lo, w_hi))):
                                last = nc.tensor.matmul(p_y[:, t % 2, 0:CW + extra], fp[:, kh, kk, :], wp[:, k, :],
                                                        start=(k == 0 and n == 0), stop=(k == K - 1 and n == 2))
                        last.then_inc(piece_used, 1)
            if extra:
                pe.wait_ge(steps, 1)
                nc.tensor.transpose(p_s[0:2 * NT, 0:T], score[:].rearrange("p a t -> p (a t)"), ident[0:T, 0:T]).then_inc(turned_done, 1)
                pe.wait_ge(steps, 5)
                pe.wait_ge(turned_kept, 1)
                nc.tensor.transpose(p_s[0:2 * NT, 0:T], uv[:].rearrange("p a t -> p (a t)"), ident[0:T, 0:T]).then_inc(turned_done, 1)


def normalize(nc, core, y, to_dram, xT=None):
    ident = core.ident
    with ExitStack() as ctx:
        sb, pb, sem = core.tools(ctx)
        stats = sb("ln_stats", [T, NT, 2, 6], F32)
        moments = sb("ln_moments", [T, NT, 2], F32)
        var = sb("ln_var", [T, NT], F32)
        root = sb("ln_root", [T, NT], F32)
        inv = sb("ln_inv", [T, NT], F32)
        tmp = sb("ln_tmp", [T, NT], F32)
        better = sb("ln_better", [T, NT], F32)
        normed = sb("normed", [T, NT, D], F32)
        p_t = pb("ln_p", [128, 4, 512]) if xT else None
        steps = sem("ln_steps")
        var_done = sem("var_done")
        root_done = sem("root_done")
        normed_done = sem("normed_done")
        stored = sem("ln_stored")
        turned = sem("ln_turned")
        hi_done = sem("ln_hi")
        lo_done = sem("ln_lo")
        block = ctx.enter_context(nc.Block())
        HT = NH

        @block.sync
        def _(sp):
            for q in range(2):
                sp.wait_ge(normed_done, HT * (q + 1))
                sp.dma_start(rows_of(to_dram)[:, q * HT:(q + 1) * HT, :], normed[:, q * HT:(q + 1) * HT, :]).then_inc(stored, 16)
            sp.wait_ge(stored, 32)

        @block.vector
        def _(dve):
            v = nc.vector
            step = Chain(dve, steps)
            for t in range(NT):
                for q in range(2):
                    last = v.bn_stats(stats[:, t, q, :], y[:, t, q * (D // 2):(q + 1) * (D // 2)])
            step(last)
            for t in range(NT):
                last = v.bn_aggr(moments[:, t, :], stats[:, t, :, :])
            step(last)
            v.tensor_scalar(var[:], moments[:, :, 1], EPS, None, ALU.add).then_inc(var_done, 1)
            dve.wait_ge(root_done, 1)
            step(v.reciprocal(inv[:], root[:]))
            step(v.tensor_tensor(tmp[:], inv[:], inv[:], ALU.mult))
            step(v.scalar_tensor_tensor(tmp[:], tmp[:], -0.5, var[:], ALU.mult, ALU.mult))
            step(v.scalar_tensor_tensor(better[:], tmp[:], 1.5, inv[:], ALU.add, ALU.mult))
            for t in range(NT):
                v.tensor_scalar(normed[:, t, :], y[:, t, :], moments[:, t, 0:1], better[:, t:t + 1],
                                ALU.subtract, ALU.mult).then_inc(normed_done, 1)
            if xT:
                for n in range(3 * KD):
                    k, b, w = n // 3, (0, 512, 1024)[n % 3] , 0
                    dve.wait_ge(hi_done, n + 1)
                    g = n % 3
                    a, m = 4 * g * T, (4 if g < 2 else 2) * T
                    v.tensor_tensor(xT[1][:, k, a:a + m], p_t[:, n % 4, 0:m], xT[0][:, k, a:a + m].bitcast(F32),
                                    ALU.subtract).then_inc(lo_done, 1)

        @block.scalar
        def _(act):
            act.wait_ge(var_done, 1)
            nc.scalar.activation(root[:], var[:], ACT.Sqrt).then_inc(root_done, 1)
            if xT:
                for n in range(3 * KD):
                    k, g = divmod(n, 3)
                    a, m = 4 * g * T, (4 if g < 2 else 2) * T
                    act.wait_ge(turned, n + 1)
                    nc.scalar.activation(xT[0][:, k, a:a + m], p_t[:, n % 4, 0:m], ACT.Copy).then_inc(hi_done, 1)

        @block.tensor
        def _(pe):
            if xT:
                pe.wait_ge(normed_done, NT)
                for n in range(3 * KD):
                    k, g = divmod(n, 3)
                    if n >= 4:
                        pe.wait_ge(lo_done, n - 3)
                    for i in range(4 if g < 2 else 2):
                        t = 4 * g + i
                        last = nc.tensor.transpose(p_t[:, n % 4, i * T:(i + 1) * T], normed[:, t, k * 128:(k + 1) * 128],
                                                   ident[0:T, 0:T])
                    last.then_inc(turned, 1)


def aggregate_last(nc, core, h2, col_src, bias, x2_dram, y2):
    CT = core.CT
    PIECE = D // 3
    STEPS = 2 * NT
    with ExitStack() as ctx:
        sb, pb, sem = core.tools(ctx)
        uv = sb("uv_l", [T, 2, N], F32)
        e = sb("e_l", [T, 3, DH], F32)
        p = sb("p_l", [T, 3, DH], F32)
        sums = sb("sums_l", [T, 2, NH], F32)
        ones = sb("ones_l", [T, 2], F32)
        b_row = sb("b_row_l", [T, D], F32)
        x2 = sb("x2_l", [T, NT, D], F32)
        p_o = pb("p_ol", [T, 8, 512])
        in_sem = sem("in_l")
        ones_set = sem("ones_l")
        v_ready = sem("v_ready_l")
        e_ready = sem("e_ready_l")
        exp_ready = sem("exp_ready_l")
        p_ready = sem("p_ready_l")
        p_used = sem("p_used_l")
        sum_steps = sem("sum_steps_l")
        bank_free = sem("bank_free_l")
        base_ready = sem("base_ready_l")
        y_done = sem("y_done_l")
        block = ctx.enter_context(nc.Block())

        @block.sync
        def _(sp):
            for kind in range(2):
                sp.dma_start(uv[:, kind, :], core.uv_rows[kind, 0:NT, :].rearrange("(o t) p -> o (t p)", o=1)
                             .broadcast_to([T, N])).then_inc(in_sem, 16)
            sp.dma_start(b_row[:], bias.rearrange("(o f) -> o f", o=1).broadcast_to([T, D])).then_inc(in_sem, 16)
            sp.dma_start(x2[:], rows_of(x2_dram)).then_inc(in_sem, 16)

        @block.scalar
        def _(act):
            a = nc.scalar
            act.wait_ge(in_sem, 64)

            def low(g):
                part, s = divmod(g, NT)
                if g >= 3:
                    act.wait_ge(p_ready, g - 2)
                a.activation(e[:, g % 3, :], uv[:, 1, part * DH:(part + 1) * DH], ACT.Identity,
                             bias=col_src[1][:, 0, s:s + 1]).then_inc(v_ready, 1)

            def leave(part):
                act.wait_ge(sum_steps, 2 * part + 2)
                for w in range(15):
                    d, j = divmod(w, 3)
                    last = a.activation(y2[:, part * NH + d, j * PIECE:(j + 1) * PIECE],
                                        p_o[:, w // 2, (w % 2) * 256:(w % 2) * 256 + PIECE], ACT.Copy,
                                        scale=sums[:, 1, d:d + 1])
                    if w % 2 or w == 14:
                        last.then_inc(bank_free, 1)

            low(0)
            for g in range(STEPS):
                if g + 1 < STEPS:
                    low(g + 1)
                act.wait_ge(e_ready, g + 1)
                a.activation(e[:, g % 3, :], e[:, g % 3, :], ACT.Exp).then_inc(exp_ready, 1)
                if g == NT + 1:
                    leave(0)
            leave(1)

        @block.vector
        def _(dve):
            v = nc.vector
            v.memset(ones[:], 1.0).then_inc(ones_set, 1)
            dve.wait_ge(in_sem, 64)

            def upper(g):
                part, s = divmod(g, NT)
                dve.wait_ge(v_ready, g + 1)
                v.scalar_tensor_tensor(e[:, g % 3, :], uv[:, 0, part * DH:(part + 1) * DH], col_src[0][:, 0, s:s + 1],
                                       e[:, g % 3, :], ALU.add, ALU.max).then_inc(e_ready, 1)

            def divisors(part):
                dve.wait_ge(p_used, (part + 1) * NT)
                v.tensor_scalar(sums[:, 0, :], p_o[:, 7, 256:256 + NH], 1e-16, None, ALU.add).then_inc(sum_steps, 1)
                dve.wait_ge(sum_steps, 2 * part + 1)
                v.reciprocal(sums[:, 1, :], sums[:, 0, :]).then_inc(sum_steps, 1)

            def add_base(t):
                dve.wait_ge(bank_free, 8 * (t // NH + 1))
                v.tensor_tensor(y2[:, t, :], y2[:, t, :], b_row[:], ALU.add).then_inc(base_ready, 1)
                dve.wait_ge(base_ready, t + 1)
                v.tensor_tensor(y2[:, t, :], y2[:, t, :], x2[:, t, :], ALU.add).then_inc(y_done, 1)

            upper(0)
            for g in range(STEPS):
                part, s = divmod(g, NT)
                if g + 1 < STEPS:
                    upper(g + 1)
                dve.wait_ge(exp_ready, g + 1)
                if g >= 3:
                    dve.wait_ge(p_used, g - 2)
                v.scalar_tensor_tensor(p[:, g % 3, :], e[:, g % 3, :], 1.0, CT[:, s, part * DH:(part + 1) * DH],
                                       ALU.min, ALU.mult).then_inc(p_ready, 1)
                if g == NT + 1:
                    divisors(0)
                if part and s >= 5:
                    add_base(s - 5)
            divisors(1)
            for t in range(NH, NT):
                add_base(t)

        @block.tensor
        def _(pe):
            pe.wait_ge(ones_set, 1)
            for g in range(STEPS):
                part, s = divmod(g, NT)
                pe.wait_ge(p_ready, g + 1)
                for w in range(15):
                    d, j = divmod(w, 3)
                    if part and s == 0 and w % 2 == 0:
                        pe.wait_ge(bank_free, w // 2 + 1)
                    nc.tensor.matmul(p_o[:, w // 2, (w % 2) * 256:(w % 2) * 256 + PIECE], p[:, g % 3, d * T:(d + 1) * T],
                                     h2[:, s, j * PIECE:(j + 1) * PIECE], start=(s == 0 and w % 2 == 0),
                                     stop=(s == NT - 1), skip_group_check=True)
                for d in range(NH):
                    last = nc.tensor.matmul(p_o[:, 7, 256 + d:257 + d], p[:, g % 3, d * T:(d + 1) * T], ones[:, 0:1],
                                            start=False, stop=(s == NT - 1), skip_group_check=True)
                last.then_inc(p_used, 1)


def gnn_two_layers(nc, src, dst, x, w_ah, b_ah, w_gat0, a_gat0, b_gat0, w_out, b_out, w1, a1, b1, w2, a2, b2, out):
    dram = lambda name, shape: nc.dram_tensor(name, shape, F32, kind="Internal").ap()
    h0_rows = dram("h0_rows", [CONVS * H0, N, HC0])
    h1_rows = dram("h1_rows", [2 * H1, N, HALF1])
    score_rows = dram("score_rows", [CONVS * 2 * H0 * NT, T])
    turned0 = dram("turned0", [KO, 128, N])
    turned1 = dram("turned1", [K1, 128, N])
    x2_rows = dram("x2_rows", [N, D])
    with ExitStack() as ctx:
        core = Core(nc)
        core.uv_rows = dram("uv_rows", [2, CONVS * H0 * NT, T])
        sb, _, sem = core.tools(ctx)
        core.ident = sb("ident", [128, 128], F32)
        core.CT = sb("CT", [T, NT, N], U16)
        core.G = sb("G", [T, NT, N], BF16)
        cols = [sb(f"col{i}", [T, CONVS * H0, NT], F32) for i in range(4)]
        core.ident_ready = sem("ident_ready")
        sem_of_waits[0] = sem("waits")
        nc.gpsimd.memset(core.ident[:], 0.0).then_inc(core.ident_ready, 1)
        nc.gpsimd.wait_ge(core.ident_ready, 1)
        nc.gpsimd.affine_select(out=core.ident[:], in_=core.ident[:], compare_op=ALU.not_equal, fill=1.0, base=0,
                                pattern=[[-1, 128]], channel_multiplier=1).then_inc(core.ident_ready, 1)
        with ExitStack() as inner:
            sb1 = core.tools(inner)[0]
            core.x1T = [sb1(f"x1T{i}", [128, KD, N], F32R) for i in range(2)]
            counts_and_x1(nc, core, src, dst, x, w_ah, b_ah)
            project(nc, core, core.x1T, w_gat0, a_gat0, h0_rows, score_rows, CONVS, PAIR, H0, cols[0:2], *cols[2:4])
        aggregate(nc, core, h0_rows, cols[0:2], b_gat0,
                  turned0, CONVS * 2, 0)
        with ExitStack() as inner:
            sb1 = core.tools(inner)[0]
            y = sb1("y", [T, NT, D], F32)
            from_turned(nc, core, turned0, KO, w_out, y, x=x, bias=b_out)
            x2T = [sb1(f"x2T{i}", [128, KD, N], F32R) for i in range(2)]
            normalize(nc, core, y, x2_rows, x2T)
            project(nc, core, x2T, w1, a1, h1_rows, score_rows, H1, HALF1, 1, cols[0:2], *cols[2:4])
        aggregate(nc, core, h1_rows, cols[0:2], b1,
                  turned1, H1 // 2, 1)
        with ExitStack() as inner:
            sb1 = core.tools(inner)[0]
            h2 = sb1("h2", [T, NT, D], F32)
            from_turned(nc, core, turned1, K1, w2, h2, a_vec=a2, score_rows=score_rows, col_src=cols[0:2])
            y2 = sb1("y2", [T, NT, D], F32)
            aggregate_last(nc, core, h2, cols[0:2], b2, x2_rows, y2)
            normalize(nc, core, y2, out)


def kernel(**inputs):
    import numpy as np
    import concourse.bacc as bacc
    from concourse import mybir as _mybir
    from concourse.bass_utils import run_bass_kernel_spmd

    g = {k: np.asarray(v) for k, v in inputs.items()}
    L0, L1 = "L0_gnn_", "L1_gnn_"
    by_unit = lambda w, width: np.stack([w[:, q:q + width] for q in range(0, w.shape[1], width)])
    a_units = lambda s, d, width: np.stack([s.reshape(-1, width), d.reshape(-1, width)], axis=1)
    by_feature = lambda b, groups: b.reshape(groups, -1, 128).transpose(2, 0, 1)
    arrays = {
        "src": g["src"], "dst": g["dst"], "x": g["x"], "w_ah": g[L0 + "W_ah"], "b_ah": by_feature(g[L0 + "b_ah"], 1)[:, 0],
        "w_gat0": np.concatenate([by_unit(g[f"{L0}W{i}"], PAIR) for i in range(CONVS)]),
        "a_gat0": np.concatenate([a_units(g[f"{L0}a_src{i}"], g[f"{L0}a_dst{i}"], PAIR) for i in range(CONVS)]),
        "b_gat0": by_feature(np.concatenate([g[f"{L0}b{i}"] for i in range(CONVS)]), 2 * CONVS),
        "w_out": g[L0 + "W_out"], "b_out": g[L0 + "b_out"],
        "w1": by_unit(g[L1 + "W1"], HALF1), "a1": a_units(g[L1 + "a1_src"], g[L1 + "a1_dst"], HALF1), "b1": by_feature(g[L1 + "b1"], H1 // 2),
        "w2": g[L1 + "W2"], "a2": np.concatenate([g[L1 + "a2_src"], g[L1 + "a2_dst"]]), "b2": g[L1 + "b2"],
    }
    arrays = {f"in_{k}": np.ascontiguousarray(v) for k, v in arrays.items()}
    nc = bacc.Bacc("TRN2", target_bir_lowering=False, num_devices=1)
    args = [nc.dram_tensor(k, v.shape, _mybir.dt.from_np(v.dtype), kind="ExternalInput").ap() for k, v in arrays.items()]
    out = nc.dram_tensor("out", (N, D), F32, kind="ExternalOutput").ap()
    gnn_two_layers(nc, *args, out)
    return run_bass_kernel_spmd(nc, [arrays], core_ids=[0]).results[0]["out"]
```

```python
import concourse.bass as bass
from concourse import mybir
from contextlib import ExitStack

F32 = mybir.dt.float32
F32R = mybir.dt.float32r
BF16 = mybir.dt.bfloat16
U16 = mybir.dt.uint16
I16 = mybir.dt.int16
I32 = mybir.dt.int32
ALU = mybir.AluOpType
ACT = mybir.ActivationFunctionType
AX = mybir.AxisListType

N = 1250
D = 768
E = 20000
T = 125
NT = N // T
KD = D // 128
EP = E // (2 * T)
SLOPE = 0.2
EPS = 1e-5
NO_EDGE = -3e38

H0, C0 = 4, 192
CONVS = 3
PAIR = 2 * C0
HC0 = C0 + 2
H1, C1 = 4, 512
HALF1 = C1 // 2
DH = N // 2
NH = NT // 2
K1 = H1 * C1 // 128
KO = CONVS * D // 128


class Core:

    def __init__(self, nc):
        self.nc = nc
        self.stages = 0

    def tools(self, ctx):
        nc, n = self.nc, self.stages
        self.stages += 1
        sb = lambda name, shape, dt: ctx.enter_context(nc.sbuf_tensor(f"{name}_{n}", shape, dt))
        pb = lambda name, shape: ctx.enter_context(nc.psum_tensor(f"{name}_{n}", shape, F32))
        sems = []

        def sem(name):
            sems.append(nc.alloc_semaphore(f"{name}_{n}"))
            return sems[-1]

        def clear():
            if sems:
                nc.clear_and_free_semaphores(sems)
                nc.all_engine_barrier()

        ctx.callback(clear)
        return sb, pb, sem


def rows_of(dram_rows):
    return dram_rows.rearrange("(t p) f -> p t f", p=T)


def spread(dram_row, parts):
    return dram_row.partition_broadcast(parts)


def wait_apart(eng, sem, value):
    eng.wait_ge(sem, value)
    eng.sem_inc(sem_of_waits[0], 1)


sem_of_waits = [None]


class Chain:

    def __init__(self, eng, sem):
        self.eng, self.sem, self.n = eng, sem, 0

    def __call__(self, ins):
        self.n += 1
        ins.then_inc(self.sem, 1)
        self.eng.wait_ge(self.sem, self.n)


def counts_and_x1(nc, core, src, dst, x, w_ah, b_ah, w_gat, a_gat):
    ident, CT, G, x1T = core.ident, core.CT, core.G, core.x1T
    BT = 2 * T
    NB = NT // 2
    CH = [(0, 418), (418, 416), (834, 416)]
    with ExitStack() as ctx:
        sb, pb, sem = core.tools(ctx)
        edge_i = sb("edge_i", [EP, 2, 2 * T], I32)
        dst_ends = sb("dst_ends", [EP, 2], F32)
        ends_row = sb("ends_row", [128, 2, EP], F32)
        edge_col = sb("edge_col", [T, 2, 2, 2 * EP], F32)
        spare = CT[0:1, :, :].rearrange("p t n -> p (t n)")[:, 0:2 * 5 * NT * EP].bitcast(F32) \
            .rearrange("p (a t e) -> p a t e", a=5, t=NT)
        meets, meets_b, meets_c = (spare[:, i] for i in range(3))
        tile_lo, pair_no = (spare[:, i].bitcast(I32) for i in (3, 4))
        range_f = sb("range_f", [1, 3, NT], F32)
        ones_row = sb("ones_row", [1, NT], F32)
        range_i = sb("range_i", [1, 3, NT], I32)
        node_no = sb("node_no", [T, N], I16)
        src_hot = sb("src_hot", [T, 2, N], BF16)
        dst_hot = sb("dst_hot", [T, 2, T], BF16)
        band = sb("band", [T, 2 * N - T], BF16)
        ident_b = sb("ident_b", [T, T], BF16)
        zeros_b = sb("zeros_b", [T, T], BF16)
        count_row = sb("count_row", [T, N], F32)
        edge_f = count_row[0:EP, 0:4 * T].rearrange("p (a e) -> p a e", a=2)
        w_raw = sb("w_raw", [128, 2, D], F32)
        w_hi = sb("w_hi", [128, KD, D], F32R)
        w_lo = sb("w_lo", [128, KD, D], F32R)
        bias = sb("bias_ah", [128, KD], F32)
        x_in = sb("x_in", [T, 2, D], F32)
        xT_hi = sb("xT_hi", [128, KD, BT], F32R)
        xT_lo = sb("xT_lo", [128, KD, BT], F32R)
        x1_f = sb("x1_f", [128, 2, 2 * BT], F32)
        p_count = pb("p_count", [T, 3, 512])
        p_turn = pb("p_turn", [128, 3, 512])
        p_x = pb("p_x", [128, 2, 512])

        edges_in = sem("edges_in")
        w_in = [sem(f"w_in{i}") for i in range(2)]
        bias_in = sem("bias_in")
        consts = sem("consts")
        steps = sem("steps")
        edges_turned = sem("edges_turned")
        cols_ready = sem("cols_ready")
        ranges_ready = sem("ranges_ready")
        hot_ready = sem("hot_ready")
        hot_free = sem("hot_free")
        counted = sem("counted")
        row_staged = sem("row_staged")
        mask_done = sem("mask_done")
        row_turned = sem("row_turned")
        ct_done = sem("ct_done")
        w_split = sem("w_split")
        x_loaded = sem("x_loaded")
        x_turned = sem("x_turned")
        xhi_done = sem("xhi_done")
        xlo_done = sem("xlo_done")
        x1_summed = sem("x1_summed")
        x1_relu = sem("x1_relu")
        x1_hi_done = sem("x1_hi_done")
        x1_lo_done = sem("x1_lo_done")

        by_a = WeightsByA(nc, sb, sem, w_gat, a_gat, core.wa0, 1)

        block = ctx.enter_context(nc.Block())

        @block.sync
        def _(sp):
            sp.dma_start(edge_i[:, 0, :], src.rearrange("(p e) -> p e", e=2 * T)).then_inc(edges_in, 16)
            sp.dma_start(edge_i[:, 1, :], dst.rearrange("(p e) -> p e", e=2 * T)).then_inc(edges_in, 16)
            sp.dma_start(x_in[:], rows_of(x)[:, 0:2, :]).then_inc(x_loaded, 16)
            sp.dma_start(bias[:], b_ah).then_inc(bias_in, 16)
            for k in range(KD):
                if k >= 2:
                    sp.wait_ge(w_split, 2 * (k - 1))
                sp.dma_start(w_raw[:, k % 2, :], w_ah[k * 128:(k + 1) * 128, :]).then_inc(w_in[k % 2], 16)
            for b in range(1, NB):
                sp.wait_ge(x_turned, 3 * b)
                sp.dma_start(x_in[:], rows_of(x)[:, 2 * b:2 * b + 2, :]).then_inc(x_loaded, 16)

        @block.gpsimd
        def _(pool):
            pool.iota(node_no[:], [[1, N]], base=0, channel_multiplier=0).then_inc(consts, 1)
            pool.iota(tile_lo, [[T, NT], [0, EP]], base=0, channel_multiplier=0).then_inc(consts, 1)
            pool.iota(pair_no, [[0, NT], [1, EP]], base=0, channel_multiplier=0).then_inc(consts, 1)
            for m in (band, ident_b, zeros_b):
                pool.memset(m[:], 0.0).then_inc(consts, 1)
            pool.wait_ge(consts, 6)
            pool.affine_select(out=ident_b[:], in_=ident_b[:], compare_op=ALU.not_equal, fill=1.0, base=0,
                               pattern=[[-1, T]], channel_multiplier=1).then_inc(consts, 1)
            pool.affine_select(out=band[:], in_=band[:], compare_op=ALU.not_equal, fill=1.0, base=N - T,
                               pattern=[[-1, 2 * N - T]], channel_multiplier=1).then_inc(consts, 1)
            for k in range(KD):
                pool.wait_ge(w_in[k % 2], 16 * (k // 2 + 1))
                pool.tensor_copy(w_hi[:, k, :], w_raw[:, k % 2, :]).then_inc(w_split, 1)
                pool.wait_ge(w_split, 2 * k + 1)
                pool.tensor_tensor(w_lo[:, k, :], w_raw[:, k % 2, :], w_hi[:, k, :].bitcast(F32),
                                   ALU.subtract).then_inc(w_split, 1)
            by_a.program(pool)

        @block.vector
        def _(dve):
            v = nc.vector
            step = Chain(dve, steps)
            dve.wait_ge(edges_in, 32)
            step(v.tensor_copy(edge_f, edge_i[:]))
            step(v.tensor_reduce(out=dst_ends[:, 0:1], in_=edge_f[:, 1, :], axis=AX.X, op=ALU.min))
            step(v.tensor_reduce(out=dst_ends[:, 1:2], in_=edge_f[:, 1, :], axis=AX.X, op=ALU.max))
            dve.wait_ge(edges_turned, 1)
            v.tensor_copy(edge_col[:, :, :, 0:EP],
                          p_turn[0:T, 0, 0:4 * EP].rearrange("p (a b c) -> p a b c", a=2, b=2)).then_inc(cols_ready, 1)
            step(v.tensor_copy(ends_row[:], p_turn[:, 1, 0:2 * EP].rearrange("p (a c) -> p a c", a=2)))
            dve.wait_ge(consts, 3)
            least = ends_row[0:1, 0:1, :].broadcast_to([1, NT, EP])
            most = ends_row[0:1, 1:2, :].broadcast_to([1, NT, EP])
            step(v.tensor_tensor(meets, most, tile_lo, ALU.is_ge))
            step(v.scalar_tensor_tensor(meets_b, tile_lo, float(T), least, ALU.add, ALU.is_gt))
            step(v.tensor_tensor(meets, meets, meets_b, ALU.mult))
            step(v.scalar_tensor_tensor(meets_b, pair_no, float(-EP), meets, ALU.add, ALU.mult))
            step(v.scalar_tensor_tensor(meets_c, pair_no, 1.0, meets, ALU.add, ALU.mult))
            step(v.tensor_reduce(out=range_f[:, 0, :], in_=meets_b, axis=AX.X, op=ALU.min))
            step(v.tensor_reduce(out=range_f[:, 1, :], in_=meets_c, axis=AX.X, op=ALU.max))
            step(v.tensor_scalar(range_f[:, 0, :], range_f[:, 0, :], float(EP), float(EP - 1), ALU.add, ALU.min))
            step(v.tensor_tensor(range_f[:, 1, :], range_f[:, 1, :], range_f[:, 0, :], ALU.subtract))
            step(v.tensor_scalar(range_f[:, 1, :], range_f[:, 1, :], 1.0, None, ALU.max))
            step(v.memset(ones_row[:], 1.0))
            step(v.tensor_tensor_scan(range_f[:, 2, :], ones_row[:], range_f[:, 1, :], 0.0, ALU.mult, ALU.add))
            step(v.tensor_tensor(range_f[:, 2, :], range_f[:, 2, :], range_f[:, 1, :], ALU.subtract))
            v.tensor_copy(range_i[:], range_f[:]).then_inc(ranges_ready, 1)
            dve.wait_ge(ranges_ready, 1)
            dve.wait_ge(cols_ready, 1)

            def one_hots(t):
                first = dve.value_load(range_i[0:1, 0, bass.ds(t, 1)], min_val=0, max_val=EP - 1)
                count = dve.value_load(range_i[0:1, 1, bass.ds(t, 1)], min_val=1, max_val=EP)
                before = dve.value_load(range_i[0:1, 2, bass.ds(t, 1)], min_val=0, max_val=EP * NT)
                with dve.Fori(0, count) as j:
                    for h in range(2):
                        dve.wait_ge(hot_free, (before + j) * 2 + (h + 1))
                        at = bass.ds(first + j, 1)
                        v.tensor_scalar(src_hot[:, h, :], node_no[:], edge_col[:, 0, h, at], None, ALU.is_equal)
                        v.tensor_scalar(dst_hot[:, h, :], node_no[:, bass.ds(t * T, T)], edge_col[:, 1, h, at],
                                        None, ALU.is_equal).then_inc(hot_ready, 1)

            def mask(t):
                dve.wait_ge(row_staged, t + 1)
                v.tensor_scalar(G[:, bass.ds(t, 1), :], count_row[:].rearrange("p (o n) -> p o n", o=1),
                                0.0, NO_EDGE, ALU.is_equal, ALU.mult).then_inc(mask_done, 1)

            with dve.Fori(0, NB) as b:
                for g in range(3):
                    dve.wait_ge(xhi_done, b * 3 + (g + 1))
                    v.tensor_tensor(xT_lo[:, 2 * g:2 * g + 2, :],
                                    p_x[:, g % 2, 0:2 * BT].rearrange("p (k n) -> p k n", k=2),
                                    xT_hi[:, 2 * g:2 * g + 2, :].bitcast(F32), ALU.subtract).then_inc(xlo_done, 1)
                one_hots(b * 2)
                mask(b * 2)
                for g in range(3):
                    dve.wait_ge(x1_hi_done, b * 3 + (g + 1))
                    at = bass.ds(b * BT, BT)
                    v.tensor_tensor(x1T[1][:, 2 * g:2 * g + 2, at],
                                    x1_f[:, g % 2, :].rearrange("p (k n) -> p k n", k=2),
                                    x1T[0][:, 2 * g:2 * g + 2, at].bitcast(F32), ALU.subtract).then_inc(x1_lo_done, 1)
                one_hots(b * 2 + 1)
                mask(b * 2 + 1)

        @block.scalar
        def _(act):
            nc.scalar.sem_inc(x1_lo_done, 1)
            nc.scalar.sem_inc(mask_done, 1)

            act.wait_ge(bias_in, 16)

            def stage_row(t):
                act.wait_ge(counted, t + 1)
                act.wait_ge(mask_done, t + 1)
                act.wait_ge(row_turned, t * 3 + 1)
                for i, (a, w) in enumerate(CH):
                    last = nc.scalar.activation(count_row[:, a:a + w], p_count[:, i, 0:w], ACT.Copy)
                last.then_inc(row_staged, 1)

            def keep_turned(t):
                for i in range(3):
                    k = 4 if i < 2 else 2
                    act.wait_ge(row_turned, t * 3 + (i + 2))
                    nc.scalar.activation(CT[:, 4 * i:4 * i + k, bass.ds(t * T, T)],
                                         p_turn[0:T, i, 0:k * T].rearrange("p (k q) -> p k q", q=T),
                                         ACT.Copy).then_inc(ct_done, 1)

            with act.Fori(0, NB) as b:
                for g in range(3):
                    act.wait_ge(x_turned, b * 3 + (g + 1))
                    nc.scalar.activation(xT_hi[:, 2 * g:2 * g + 2, :],
                                         p_x[:, g % 2, 0:2 * BT].rearrange("p (k n) -> p k n", k=2),
                                         ACT.Copy).then_inc(xhi_done, 1)
                stage_row(b * 2)
                for g in range(3):
                    act.wait_ge(x1_summed, b * 3 + (g + 1))
                    act.wait_ge(x1_lo_done, b * 3 + (g + 1))
                    for m in range(2):
                        last = nc.scalar.activation(x1_f[:, g % 2, m * BT:(m + 1) * BT], p_x[:, g % 2, m * BT:(m + 1) * BT],
                                                    ACT.Relu, bias=bias[:, 2 * g + m:2 * g + m + 1])
                    last.then_inc(x1_relu, 1)
                    act.wait_ge(x1_relu, b * 3 + (g + 1))
                    nc.scalar.activation(x1T[0][:, 2 * g:2 * g + 2, bass.ds(b * BT, BT)],
                                         x1_f[:, g % 2, :].rearrange("p (k n) -> p k n", k=2),
                                         ACT.Copy).then_inc(x1_hi_done, 1)
                keep_turned(b * 2)
                stage_row(b * 2 + 1)
                keep_turned(b * 2 + 1)

        @block.tensor
        def _(pe):
            pe.wait_ge(core.ident_ready, 2)
            pe.wait_ge(steps, 3)
            for a in range(2):
                for h in range(2):
                    nc.tensor.transpose(p_turn[0:T, 0, (2 * a + h) * EP:(2 * a + h + 1) * EP],
                                        edge_f[:, a, h * T:h * T + T], ident[0:EP, 0:EP])
            for a in range(2):
                last = nc.tensor.transpose(p_turn[:, 1, a * EP:(a + 1) * EP],
                                           dst_ends[:, a:a + 1].broadcast_to([EP, 128]), ident[0:EP, 0:EP])
            last.then_inc(edges_turned, 1)
            nc.tensor.sem_inc(hot_free, 2)
            nc.tensor.sem_inc(row_turned, 1)
            nc.tensor.sem_inc(xlo_done, 2)
            pe.wait_ge(consts, 8)
            pe.wait_ge(ranges_ready, 1)
            nc.tensor.sem_inc(ct_done, 1)

            def count(t):
                count_ = pe.value_load(range_i[0:1, 1, bass.ds(t, 1)], min_val=1, max_val=EP)
                before = pe.value_load(range_i[0:1, 2, bass.ds(t, 1)], min_val=0, max_val=EP * NT)
                for i, (a, w) in enumerate(CH):
                    nc.tensor.matmul(p_count[:, i, 0:w], ident_b[:], band[:, bass.ds(t * -T + (N - T + a), w)],
                                     start=True, stop=False, skip_group_check=True)
                with pe.Fori(0, count_) as j:
                    for h in range(2):
                        pe.wait_ge(hot_ready, (before + j) * 2 + (h + 1))
                        for i, (a, w) in enumerate(CH):
                            last = nc.tensor.matmul(p_count[:, i, 0:w], dst_hot[:, h, :], src_hot[:, h, a:a + w],
                                                    start=False, stop=False, skip_group_check=True)
                        last.then_inc(hot_free, 1)
                nc.tensor.matmul(p_count[:, 0, 0:2], zeros_b[:], src_hot[:, 0, 0:2], start=False, stop=True,
                                 skip_group_check=True).then_inc(counted, 1)

            def turn_row(t):
                pe.wait_ge(row_staged, t + 1)
                pe.wait_ge(ct_done, t * 3 + 1)
                for i in range(3):
                    for k in range(4 if i < 2 else 2):
                        q = 4 * i + k
                        last = nc.tensor.transpose(p_turn[0:T, i, k * T:k * T + T], count_row[:, q * T:q * T + T],
                                                   ident[0:T, 0:T])
                    last.then_inc(row_turned, 1)

            for b in range(NB):
                pe.wait_ge(x_loaded, 16 * (b + 1))
                for g in range(3):
                    if g == 2:
                        pe.wait_ge(xlo_done, 3 * b + 3)
                    elif b:
                        pe.wait_ge(x1_relu, 3 * b)
                    for k in (2 * g, 2 * g + 1):
                        for i in range(2):
                            last = nc.tensor.transpose(p_x[:, g % 2, (k % 2) * BT + i * T:(k % 2) * BT + (i + 1) * T],
                                                       x_in[:, i, k * 128:(k + 1) * 128], ident[0:T, 0:T])
                    last.then_inc(x_turned, 1)
                count(2 * b)
                turn_row(2 * b)
                pe.wait_ge(xlo_done, 3 * b + 5)
                if b == 0:
                    pe.wait_ge(w_split, 2 * KD)
                for g in range(3):
                    if g == 2:
                        pe.wait_ge(x1_relu, 3 * b + 1)
                    for m in range(2):
                        for k in range(KD):
                            for n, (wp, xp) in enumerate(((w_hi, xT_hi), (w_hi, xT_lo), (w_lo, xT_hi))):
                                last = nc.tensor.matmul(p_x[:, g % 2, m * BT:(m + 1) * BT],
                                                        wp[:, k, (2 * g + m) * 128:(2 * g + m + 1) * 128], xp[:, k, :],
                                                        start=(m == 0 and k == 0 and n == 0),
                                                        stop=(k == KD - 1 and n == 2), skip_group_check=True)
                    last.then_inc(x1_summed, 1)
                count(2 * b + 1)
                turn_row(2 * b + 1)


class WeightsByA:

    def __init__(self, nc, sb, sem, w, a_vec, wa, units):
        self.nc, self.w, self.a_vec, self.wa = nc, w, a_vec, wa
        self.units, self.groups, self.width = units, w.shape[0] // units, w.shape[2]
        self.heads = wa.shape[3] // self.groups
        self.w_in = sb("by_a_w", [128, 2, units, self.width], F32)
        self.a_in = sb("by_a_a", [128, units, 2, self.width], F32)
        self.prod = sb("by_a_prod", [128, 2, units, self.width], F32)
        self.group = sb("by_a_group", [128, KD, 2, self.heads], F32)
        self.a_loaded = sem("by_a_a_loaded")
        self.w_loaded = [sem(f"by_a_w_loaded{i}") for i in range(2)]
        self.multiplied = sem("by_a_multiplied")
        self.summed = sem("by_a_summed")
        self.kept = sem("by_a_kept")

    def program(self, pool):
        width, heads, units = self.width, self.heads, self.units

        HALVES, left = [], units * width // heads
        while left > 1:
            size = left // 2 if left % 2 == 0 else 1
            HALVES.append((left - size, size))
            left -= size

        def load(g, k):
            pool.dma_start(self.w_in[:, k % 2, :, :],
                           self.w[bass.ds(g * units, units), k * 128:(k + 1) * 128, :].rearrange("u p c -> p u c")
                           ).then_inc(self.w_loaded[k % 2], 16)

        with pool.Fori(0, self.groups) as g:
            pool.dma_start(self.a_in[:].rearrange("p u a c -> p (u a c)"),
                           self.a_vec[bass.ds(g * units, units)].rearrange("(o u) a c -> o (u a c)", o=1)
                           .broadcast_to([128, 2 * units * width])).then_inc(self.a_loaded, 16)
            load(g, 0)
            load(g, 1)
            wait_apart(pool, self.a_loaded, g * 16 + 16)
            for k in range(KD):
                wait_apart(pool, self.w_loaded[k % 2], g * (KD * 8) + (k // 2 + 1) * 16)
                for kind in range(2):
                    last = pool.tensor_tensor(self.prod[:, kind, :, :], self.w_in[:, k % 2, :, :], self.a_in[:, :, kind, :], ALU.mult)
                last.then_inc(self.multiplied, 1)
                wait_apart(pool, self.multiplied, g * KD + (k + 1))
                if k + 2 < KD:
                    load(g, k + 2)
                p = self.prod[:].rearrange("p a u c -> p a (u c)").rearrange("p a (h c) -> p a h c", h=heads)
                for n, (other, size) in enumerate(HALVES):
                    out = self.group[:, k, :, :].rearrange("p a (h o) -> p a h o", o=1) if n == len(HALVES) - 1 else p[:, :, :, 0:size]
                    pool.tensor_tensor(out, p[:, :, :, 0:size], p[:, :, :, other:other + size], ALU.add).then_inc(self.summed, 1)
                    wait_apart(pool, self.summed, g * (KD * len(HALVES)) + (k * len(HALVES) + n + 1))
            pool.tensor_copy(self.wa[:, :, :, bass.ds(g * heads, heads)], self.group[:]).then_inc(self.kept, 1)
            wait_apart(pool, self.kept, g + 1)


def project(nc, core, xT, w, wa, h_rows, score_rows, width, col_src, u_col, v_col):
    iters = w.shape[0] // 2
    heads = wa.shape[3]
    per = heads // (2 * iters) or 1
    cw = width // per
    hw = h_rows.shape[2]
    R = 2 * heads
    HG = 4
    GROUPS = heads // HG
    CH = [(0, 418), (418, 416), (834, 416)]
    ident, G = core.ident, core.G
    with ExitStack() as ctx:
        sb, pb, sem = core.tools(ctx)
        w_raw = sb("pw_raw", [128, 2, KD, width], F32)
        w_hi = sb("pw_hi", [128, 2, KD, width], F32R)
        w_lo = sb("pw_lo", [128, 2, KD, width], F32R)
        wa_hi = sb("wa_hi", [128, KD, R], F32R)
        wa_lo = sb("wa_lo", [128, KD, R], F32R)
        rows = sb("score_rows_in", [R, N], F32)
        junk = sb("max_junk", [T, 2, N], BF16)
        h_out = sb("h_out", [T, 2, NH, per, hw], F32)
        score = sb("score", [T, 2, heads, NT], F32)
        dst_now = sb("dst_now", [T, HG, NT], F32)
        src_row = sb("src_row", [T, 2, N], F32)
        most = sb("most", [T, HG, NT], F32)
        tmp = sb("tmp", [T, HG, NT], F32)
        tmp2 = sb("tmp2", [T, HG, NT], F32)
        turned_uv = src_row[0:heads * NT, 0, 0:2 * T].rearrange("p (a q) -> p a q", a=2)
        p_h = pb("p_h", [T, 4, 512])
        p_r = pb("p_r", [R, 3, 512])
        p_s = pb("p_s", [128, 512])

        w_in = [sem(f"pw_in{u}") for u in range(2)]
        wa_hi_done = sem("wa_hi_done")
        wa_split = sem("wa_split")
        rows_summed = sem("rows_summed")
        rows_kept = sem("rows_kept")
        rows_stored = sem("rows_stored")
        rows_turned = sem("rows_turned")
        score_kept = sem("score_kept")
        max_steps = sem("max_steps")
        maxed = sem("maxed")
        hi_done = sem("hi_done")
        split_done = sem("split_done")
        h_summed = sem("h_summed")
        h_kept = sem("h_kept")
        h_stored = [sem(f"h_stored{u}") for u in range(2)]
        ones_set = sem("ones_set")
        row_in = [sem(f"row_in{u}") for u in range(2)]
        uv_done = sem("uv_done")
        uv_turned = sem("uv_turned")
        uv_kept = sem("uv_kept")
        uv_stored = sem("uv_stored")

        block = ctx.enter_context(nc.Block())

        @block.sync
        def _(sp):
            def load_w(i):
                for u in range(2):
                    q = i * 2 + u
                    wait_apart(sp, split_done, q + 1)
                    sp.dma_start(w_raw[:, u, :, :], w[bass.ds(q, 1)].rearrange("o (k p) c -> p (o k) c", p=128)).then_inc(w_in[u], 16)

            def store(i, heads_to_load):
                for u in range(2):
                    for part_no in range(2):
                        wait_apart(sp, h_kept, i * (2 * NT) + (NT * u + NH * (part_no + 1) + 4))
                        for g in range(per):
                            to = h_rows[bass.ds(i * (2 * per) + (u * per + g), 1), part_no * DH:(part_no + 1) * DH, :]
                            sp.dma_start(to.rearrange("o (t p) c -> p (o t) c", p=T),
                                         h_out[:, part_no, :, g, :]).then_inc(h_stored[part_no], 16)
                        j = 2 * u + part_no
                        if j < heads_to_load:
                            wait_apart(sp, maxed, i * (HG * NT) + ((j + 1) * NT + 2))
                            sp.dma_start(src_row[:, j % 2, :],
                                         score_rows[bass.ds(i * HG + (j + 2), 1), :].broadcast_to([T, N])).then_inc(row_in[j % 2], 16)

            load_w(0)
            if GROUPS > 1:
                with sp.Fori(0, iters - 1) as i:
                    load_w(i + 1)
                    store(i, HG)
                store(iters - 1, HG - 2)
            else:
                load_w(1)
                store(0, HG - 2)
                with sp.Fori(0, iters - 2) as i:
                    load_w(i + 2)
                    store(i + 1, 0)
                store(iters - 1, 0)
            for u in range(2):
                sp.wait_ge(h_stored[u], 16 * per * (2 * iters + 1))
            for kind in range(2):
                sp.wait_ge(uv_kept, kind + 1)
                sp.dma_start(core.uv_rows[kind, 0:heads * NT, :], turned_uv[:, kind, :]).then_inc(uv_stored, 16)
            sp.wait_ge(uv_stored, 32)

        @block.gpsimd
        def _(pool):
            pool.sem_inc(split_done, 2)
            if hw > cw:
                pool.memset(h_out[:, :, :, :, cw:], 0.0).then_inc(ones_set, 1)
                pool.wait_ge(ones_set, 1)
                pool.memset(h_out[:, :, :, :, cw:cw + 1], 1.0).then_inc(ones_set, 1)
            with pool.Fori(0, iters) as i:
                for u in range(2):
                    pool.wait_ge(w_in[u], i * 16 + 16)
                    wait_apart(pool, h_summed, i * (2 * NT) + (u + 1) * NT)
                    pool.tensor_copy(w_hi[:, u, :, :], w_raw[:, u, :, :]).then_inc(hi_done, 1)
                    pool.wait_ge(hi_done, i * 2 + (u + 1))
                    pool.tensor_tensor(w_lo[:, u, :, :], w_raw[:, u, :, :],
                                       w_hi[:, u, :, :].bitcast(F32), ALU.subtract).then_inc(split_done, 1)

        @block.vector
        def _(dve):
            v = nc.vector
            v.sem_inc(maxed, 2)
            wa_flat = wa[:].rearrange("p k a h -> p k (a h)")
            v.tensor_copy(wa_hi[:], wa_flat).then_inc(wa_hi_done, 1)
            dve.wait_ge(wa_hi_done, 1)
            v.tensor_tensor(wa_lo[:], wa_flat, wa_hi[:].bitcast(F32), ALU.subtract).then_inc(wa_split, 1)
            dve.wait_ge(rows_turned, 1)
            v.tensor_copy(score[:], p_s[0:T, 0:NT * R].rearrange("p (t a h) -> p a h t", t=NT, a=2)).then_inc(score_kept, 1)
            dve.wait_ge(score_kept, 1)
            v.tensor_copy(col_src[0][:, 0:heads, :], score[:, 0])
            v.tensor_scalar(col_src[1][:, 0:heads, :], score[:, 0], SLOPE, None, ALU.mult)

            def maxima(q):
                for h in range(HG):
                    wait_apart(dve, row_in[h % 2], q * 32 + 16 * (h // 2 + 1))
                    for t in range(NT):
                        wait_apart(dve, maxed, q * (HG * NT) + (h * NT + t + 1))
                        v.tensor_tensor_reduce(out=junk[:, t % 2, :], in0=src_row[:, h % 2, :], in1=G[:, t, :], scale=1.0,
                                               scalar=NO_EDGE, op0=ALU.add, op1=ALU.max,
                                               accum_out=most[:, h, t:t + 1]).then_inc(maxed, 1)
                hs = bass.ds(q * HG, HG)
                v.tensor_copy(dst_now[:], score[:, 1, hs, :]).then_inc(max_steps, 1)
                dve.wait_ge(max_steps, q * 4 + 1)
                dve.wait_ge(maxed, q * (HG * NT) + (HG * NT + 2))
                v.tensor_tensor(tmp[:], most[:], dst_now[:], ALU.add).then_inc(max_steps, 1)
                dve.wait_ge(max_steps, q * 4 + 2)
                v.scalar_tensor_tensor(tmp2[:], tmp[:], SLOPE, tmp[:], ALU.mult, ALU.max).then_inc(max_steps, 1)
                dve.wait_ge(max_steps, q * 4 + 3)
                v.tensor_tensor(u_col[:, hs, :], dst_now[:], tmp2[:], ALU.subtract)
                v.scalar_tensor_tensor(v_col[:, hs, :], dst_now[:], SLOPE, tmp2[:], ALU.mult, ALU.subtract).then_inc(max_steps, 1)
                dve.wait_ge(max_steps, q * 4 + 4)

            with dve.Fori(0, GROUPS) as q:
                maxima(q)
            v.sem_inc(uv_done, 1)

        @block.scalar
        def _(act):
            a = nc.scalar
            a.sem_inc(h_kept, 4)
            for u in range(2):
                a.sem_inc(h_stored[u], 16 * per)
            act.wait_ge(rows_summed, 1)
            for b, (at, n) in enumerate(CH):
                last = a.activation(rows[:, at:at + n], p_r[:, b, 0:n], ACT.Copy)
            last.then_inc(rows_kept, 1)
            act.wait_ge(rows_kept, 1)
            act.dma_start(score_rows[0:R, :], rows[:]).then_inc(rows_stored, 16)
            act.wait_ge(rows_stored, 16)
            for h in range(2):
                act.dma_start(src_row[:, h, :], score_rows[h:h + 1, :].broadcast_to([T, N])).then_inc(row_in[h], 16)
            if hw > cw:
                act.wait_ge(ones_set, 2)
            with act.Fori(0, iters) as i:
                for u in range(2):
                    for t in range(NT):
                        if t % NH == 0:
                            act.wait_ge(h_stored[t // NH], i * (32 * per) + 16 * per * (u + 1))
                        act.wait_ge(h_summed, i * (2 * NT) + (2 * NT + u * NT + t + 1))
                        a.activation(h_out[:, t // NH, t % NH, :, 0:cw],
                                     p_h[:, (u * NT + t) % 4, 0:width].rearrange("p (g c) -> p g c", g=per),
                                     ACT.Copy).then_inc(h_kept, 1)
            for kind in range(2):
                act.wait_ge(uv_turned, kind + 1)
                a.activation(turned_uv[:, kind, :], p_s[0:heads * NT, 0:T], ACT.Copy).then_inc(uv_kept, 1)

        @block.tensor
        def _(pe):
            nc.tensor.sem_inc(h_summed, 2 * NT)
            pe.wait_ge(wa_split, 1)
            for b, (at, n) in enumerate(CH):
                for k in range(KD):
                    for j, (wp, xp) in enumerate(((wa_hi, xT[0]), (wa_hi, xT[1]), (wa_lo, xT[0]))):
                        last = nc.tensor.matmul(p_r[:, b, 0:n], wp[:, k, :], xp[:, k, at:at + n],
                                                start=(k == 0 and j == 0), stop=(k == KD - 1 and j == 2))
            last.then_inc(rows_summed, 1)
            pe.wait_ge(rows_kept, 1)
            for t in range(NT):
                last = nc.tensor.transpose(p_s[0:T, t * R:(t + 1) * R], rows[:, t * T:(t + 1) * T], ident[0:R, 0:R])
            last.then_inc(rows_turned, 1)
            with pe.Fori(0, iters) as i:
                for u in range(2):
                    pe.wait_ge(split_done, i * 2 + (u + 3))
                    for t in range(NT):
                        pe.wait_ge(h_kept, i * (2 * NT) + (u * NT + t + 1))
                        at = slice(t * T, (t + 1) * T)
                        for k in range(KD):
                            for n, (xp, wp) in enumerate(((xT[0], w_hi), (xT[0], w_lo), (xT[1], w_hi))):
                                last = nc.tensor.matmul(p_h[:, (u * NT + t) % 4, 0:width], xp[:, k, at], wp[:, u, k, :],
                                                        start=(k == 0 and n == 0), stop=(k == KD - 1 and n == 2))
                        last.then_inc(h_summed, 1)
            pe.wait_ge(uv_done, 1)
            for kind, col in enumerate((u_col, v_col)):
                if kind:
                    pe.wait_ge(uv_kept, kind)
                nc.tensor.transpose(p_s[0:heads * NT, 0:T], col[:, 0:heads, :].rearrange("p h t -> p (h t)"),
                                    ident[0:T, 0:T]).then_inc(uv_turned, 1)


def aggregate_layer0(nc, core, h_rows, col_src, bias, turned_rows, w_next, a_next):
    ident, CT = core.ident, core.CT
    ITERS = CONVS * H0 // 2
    STEPS = 2 * NT
    BANKS = 5
    CW = PAIR // 128
    RING = 4
    with ExitStack() as ctx:
        sb, pb, sem = core.tools(ctx)
        uv = sb("uv", [T, 2, 2, N], F32)
        h_in = sb("h_in", [T, 2, NT, HC0], F32)
        e = sb("e", [T, RING, 2, N], F32)
        p = sb("p", [T, RING, N], F32)
        res = sb("res", [T, NT, PAIR], F32)
        sums = sb("sums", [T, 2, NT], F32)
        b_col = sb("b_col", [128, ITERS, CW], F32)
        out_f = sb("out_f", [128, CW, N], F32)
        p_o = pb("p_o", [T, BANKS, 512])
        p_t = pb("p_t", [128, 3, 512])

        uv_in = [sem(f"uv_in{i}") for i in range(2)]
        h_loaded = [sem(f"h_loaded{i}") for i in range(2)]
        bias_in = sem("bias_in")
        exp_ready = sem("exp_ready")
        more_ready = sem("more_ready")
        p_ready = sem("p_ready")
        p_used = sem("p_used")
        sum_steps = sem("sum_steps")
        bank_free = sem("bank_free")
        turned = sem("turned")
        out_ready = sem("out_ready")
        stored = [sem(f"stored{i}") for i in range(CW)]
        by_a = WeightsByA(nc, sb, sem, w_next, a_next, core.wa1, 2)

        block = ctx.enter_context(nc.Block())

        @block.gpsimd
        def _(pool):
            by_a.program(pool)

        def every_iteration(eng, body):
            body(0, True)
            with eng.Fori(0, ITERS - 1) as i:
                body(i + 1, False)

        @block.sync
        def _(sp):
            sp.dma_start(b_col[:], bias).then_inc(bias_in, 16)

            def load(i):
                for s in range(2):
                    wait_apart(sp, exp_ready, i * STEPS + (s + 1) * NT)
                    wait_apart(sp, p_used, i * STEPS + (s + 1) * NT)
                    head = i * 2 + s
                    for kind in range(2):
                        sp.dma_start(uv[:, s, kind, :],
                                     core.uv_rows[kind, bass.ds(head * NT, NT), :].rearrange("(o t) p -> o (t p)", o=1)
                                     .broadcast_to([T, N])).then_inc(uv_in[s], 16)
                    for q in range(2):
                        sp.dma_start(h_in[:, s, q * NH:(q + 1) * NH],
                                     h_rows[bass.ds(head, 1), q * DH:(q + 1) * DH, :].rearrange("o (t p) c -> p (o t) c", p=T)
                                     ).then_inc(h_loaded[s], 16)

            def store(i):
                for c in range(CW):
                    wait_apart(sp, out_ready, i * CW + (c + 1))
                    sp.dma_start(turned_rows[bass.ds(i * CW + c, 1), :, :].rearrange("o p n -> p (o n)"),
                                 out_f[:, c, :]).then_inc(stored[c], 16)

            load(0)
            load(1)
            with sp.Fori(0, ITERS - 2) as i:
                store(i)
                load(i + 2)
            store(ITERS - 2)
            store(ITERS - 1)
            for c in range(CW):
                sp.wait_ge(stored[c], 16 * (1 + ITERS))

        @block.scalar
        def _(act):
            a = nc.scalar
            for c in range(CW):
                a.sem_inc(stored[c], 16)
            a.sem_inc(bank_free, BANKS)
            act.wait_ge(bias_in, 16)

            def leave_head(i, hh):
                act.wait_ge(sum_steps, i * 4 + (2 * hh + 2))
                act.wait_ge(turned, i * CW + CW)
                for d in range(NT):
                    last = a.activation(res[:, d, hh * C0:(hh + 1) * C0], p_o[:, d // 2, (d % 2) * 256:(d % 2) * 256 + C0],
                                        ACT.Copy, scale=sums[:, 1, d:d + 1])
                    if d % 2:
                        last.then_inc(bank_free, 1)

            def keep(i, c):
                act.wait_ge(turned, i * CW + (c + 1 + CW))
                wait_apart(act, stored[c], i * 16 + 16)
                for b, k in ((0, 4), (1, 4), (2, 2)):
                    last = a.activation(out_f[:, c, 4 * b * T:(4 * b + k) * T], p_t[:, b, 0:k * T], ACT.Relu,
                                        bias=b_col[:, bass.ds(i, 1), c])
                last.then_inc(out_ready, 1)

            def body(i, first):
                for g in range(STEPS):
                    hh, s = divmod(g, NT)
                    if s == 0:
                        wait_apart(act, uv_in[hh], i * 32 + 32)
                    wait_apart(act, p_ready, i * STEPS + (g + 1))
                    for kind in range(2):
                        last = a.activation(e[:, g % RING, kind, :], uv[:, hh, kind, :], ACT.Exp,
                                            bias=col_src[kind][:, bass.ds(i * 2 + hh, 1), s])
                    last.then_inc(exp_ready, 1)
                    if g == NT + 3:
                        leave_head(i, 0)
                    if g == 3 and not first:
                        leave_head(i - 1, 1)
                    if g in (5, 7, 9) and not first:
                        keep(i - 1, (g - 5) // 2)

            every_iteration(act, body)
            leave_head(ITERS - 1, 1)
            for c in range(CW):
                keep(ITERS - 1, c)

        @block.vector
        def _(dve):
            v = nc.vector
            v.sem_inc(p_ready, RING)
            v.sem_inc(exp_ready, 2 * NT)

            def divisors(i, hh):
                dve.wait_ge(p_used, i * STEPS + ((hh + 1) * NT + 2 * NT))
                v.tensor_scalar(sums[:, 0, :].rearrange("p (b n) -> p b n", n=2),
                                p_o[:, :, :].rearrange("p b (n c) -> p b n c", n=2)[:, :, :, C0],
                                1e-16, None, ALU.add).then_inc(sum_steps, 1)
                dve.wait_ge(sum_steps, i * 4 + (2 * hh + 1))
                v.reciprocal(sums[:, 1, :], sums[:, 0, :]).then_inc(sum_steps, 1)

            def body(i, first):
                for g in range(STEPS):
                    hh, s = divmod(g, NT)
                    dve.wait_ge(exp_ready, i * STEPS + (g + 1 + 2 * NT))
                    v.tensor_tensor(e[:, g % RING, 0, :], e[:, g % RING, 0, :], e[:, g % RING, 1, :], ALU.max).then_inc(more_ready, 1)
                    dve.wait_ge(more_ready, i * STEPS + (g + 1))
                    dve.wait_ge(p_used, i * STEPS + (g + 1 + 2 * NT - RING))
                    v.scalar_tensor_tensor(p[:, g % RING, :], e[:, g % RING, 0, :], 1.0, CT[:, s, :],
                                           ALU.min, ALU.mult).then_inc(p_ready, 1)
                    if g == NT + 2:
                        divisors(i, 0)
                    if g == 2 and not first:
                        divisors(i - 1, 1)

            every_iteration(dve, body)
            divisors(ITERS - 1, 1)

        @block.tensor
        def _(pe):
            nc.tensor.sem_inc(p_used, 2 * NT)
            nc.tensor.sem_inc(turned, CW)

            def turn(i, c):
                if c:
                    pe.wait_ge(out_ready, i * CW + c)
                else:
                    pe.wait_ge(bank_free, i * (2 * BANKS) + 3 * BANKS)
                for d in range(NT):
                    last = nc.tensor.transpose(p_t[:, d // 4, (d % 4) * T:(d % 4 + 1) * T],
                                               res[:, d, c * 128:(c + 1) * 128], ident[0:T, 0:T])
                last.then_inc(turned, 1)

            def body(i, first):
                for g in range(STEPS):
                    hh, s = divmod(g, NT)
                    if s == 0:
                        pe.wait_ge(h_loaded[hh], i * 32 + 32)
                    pe.wait_ge(p_ready, i * STEPS + (g + 1 + RING))
                    for d in range(NT):
                        b, n = divmod(d, 2)
                        if s == 0 and n == 0:
                            pe.wait_ge(bank_free, i * (2 * BANKS) + (BANKS * hh + b + 1))
                        last = nc.tensor.matmul(p_o[:, b, n * 256:n * 256 + C0 + 1], p[:, g % RING, d * T:(d + 1) * T],
                                                h_in[:, hh, s, 0:C0 + 1], start=(s == 0 and n == 0), stop=(s == NT - 1),
                                                skip_group_check=True)
                    last.then_inc(p_used, 1)
                    if g in (1, 3, 5) and not first:
                        turn(i - 1, (g - 1) // 2)

            every_iteration(pe, body)
            for c in range(CW):
                turn(ITERS - 1, c)


def aggregate_layer1(nc, core, h_rows, col_src, bias, turned_rows):
    ident, CT = core.ident, core.CT
    STEPS = 2 * NT
    BANKS = NH
    CW = C1 // 128
    ROW = (NH - 1) * T
    RING = 4
    with ExitStack() as ctx:
        sb, pb, sem = core.tools(ctx)
        uv = sb("uv", [T, 2, 2, DH], F32)
        h_raw = sb("h_raw", [T, NT, C1], F32)
        h_hi = sb("h_hi", [T, NT, C1], F32R)
        h_lo = sb("h_lo", [T, NT, C1], F32R)
        e = sb("e", [T, RING, 2, DH], F32)
        p_hi = sb("p_hi", [T, RING, DH], F32R)
        p_lo = sb("p_lo", [T, RING, DH], F32R)
        ones_f = sb("ones_f", [T, 128], F32)
        ones = sb("ones", [T, 128], F32R)
        res = sb("res", [T, NH, C1], F32)
        sum_row = sb("sum_row", [1, ROW], F32)
        sums = sb("sums", [T, 2, NH + 1], F32)
        b_col = sb("b_col", [128, H1, CW], F32)
        z = sb("z", [128, 2, 3, DH], F32)
        out_f = sb("out_f", [128, 2, DH], F32)
        p_o = pb("p_o", [T, BANKS, 512])
        p_sum = pb("p_sum", [128, 512])
        p_t = pb("p_t", [128, 2, 512])

        uv_in = [sem(f"uv_in{i}") for i in range(2)]
        h_loaded = [sem(f"h_loaded{i}") for i in range(2)]
        bias_in = sem("bias_in")
        ones_set = sem("ones_set")
        h_hi_done = sem("h_hi_done")
        h_split = sem("h_split")
        exp_ready = sem("exp_ready")
        more_ready = sem("more_ready")
        p_ready = sem("p_ready")
        p_hi_ready = sem("p_hi_ready")
        p_split = sem("p_split")
        p_used = sem("p_used")
        sum_steps = sem("sum_steps")
        sums_turned = sem("sums_turned")
        bank_free = sem("bank_free")
        turned = sem("turned")
        kept = sem("kept")
        elu_low = sem("elu_low")
        elu_up = sem("elu_up")
        elu_exped = sem("elu_exped")
        out_ready = sem("out_ready")
        stored = [sem(f"stored{i}") for i in range(2)]

        block = ctx.enter_context(nc.Block())

        def chunk_of(i, part, back, c):
            return i * (2 * CW) + ((part - back) * CW + c)

        def every_iteration(eng, body):
            body(0, True)
            with eng.Fori(0, H1 - 1) as i:
                body(i + 1, False)

        @block.sync
        def _(sp):
            sp.dma_start(b_col[:], bias).then_inc(bias_in, 16)

            def load_uv(i, part):
                wait_apart(sp, exp_ready, i * STEPS + (part + 1) * NT)
                for kind in range(2):
                    sp.dma_start(uv[:, part, kind, :],
                                 core.uv_rows[kind, bass.ds(i * NT + part * NH, NH), :].rearrange("(o t) p -> o (t p)", o=1)
                                 .broadcast_to([T, DH])).then_inc(uv_in[part], 16)

            def load_h(i):
                wait_apart(sp, h_split, i * NT + NT)
                for part in range(2):
                    for q in range(2):
                        sp.dma_start(h_raw[:, part * NH:(part + 1) * NH, q * HALF1:(q + 1) * HALF1],
                                     h_rows[bass.ds(i * 2 + q, 1), part * DH:(part + 1) * DH, :].rearrange("o (t p) c -> p (o t) c", p=T)
                                     ).then_inc(h_loaded[part], 16)

            def store(i, part, back, c):
                wait_apart(sp, out_ready, chunk_of(i, part, back, c) + 3)
                head, half = i + (part - back) // 2, (part - back) % 2
                sp.dma_start(turned_rows[bass.ds(head * CW + c, 1), :, half * DH:(half + 1) * DH].rearrange("o p n -> p (o n)"),
                             out_f[:, c % 2, :]).then_inc(stored[c % 2], 16)

            def stores(i, part, groups):
                if groups >= 2:
                    for c in range(1, CW):
                        store(i, part, 2, c)
                if groups >= 1:
                    store(i, part, 1, 0)

            load_uv(0, 0)
            load_h(0)
            load_uv(0, 1)
            load_h(1)
            load_uv(1, 0)
            stores(0, 1, 1)
            with sp.Fori(0, H1 - 2) as i:
                load_uv(i + 1, 1)
                load_h(i + 2)
                stores(i + 1, 0, 2)
                load_uv(i + 2, 0)
                stores(i + 1, 1, 2)
            load_uv(H1 - 1, 1)
            stores(H1 - 1, 0, 2)
            stores(H1 - 1, 1, 2)
            stores(H1, 0, 2)
            for c in range(1, CW):
                store(H1, 1, 2, c)
            for s in range(2):
                sp.wait_ge(stored[s], 16 * (1 + H1 * CW))

        @block.gpsimd
        def _(pool):
            pool.sem_inc(h_split, NT)

            def split(i, s):
                if s % NH == 0:
                    pool.wait_ge(h_loaded[s // NH], i * 32 + 32)
                wait_apart(pool, p_used, i * STEPS + (s + 1 + NT))
                pool.tensor_copy(h_hi[:, s, :], h_raw[:, s, :]).then_inc(h_hi_done, 1)
                pool.wait_ge(h_hi_done, i * NT + (s + 1))
                pool.tensor_tensor(h_lo[:, s, :], h_raw[:, s, :], h_hi[:, s, :].bitcast(F32), ALU.subtract).then_inc(h_split, 1)

            with pool.Fori(0, H1) as i:
                for s in range(NT):
                    split(i, s)

        @block.scalar
        def _(act):
            a = nc.scalar
            for s in range(2):
                a.sem_inc(stored[s], 16)
            a.sem_inc(bank_free, BANKS)
            act.wait_ge(ones_set, 1)
            a.activation(ones[:], ones_f[:], ACT.Copy).then_inc(ones_set, 1)
            act.wait_ge(bias_in, 16)

            def leave(i, part):
                act.wait_ge(sum_steps, i * 6 + 3 * part)
                act.wait_ge(turned, i * (2 * CW) + part * CW)
                for d in range(NH):
                    at = 0 if d == NH - 1 else d + 2
                    a.activation(res[:, d, :], p_o[:, d, :], ACT.Copy, scale=sums[:, 1, at:at + 1]).then_inc(bank_free, 1)

            def keep(i, part, back, c):
                act.wait_ge(turned, chunk_of(i, part, back, c) + (1 + CW))
                wait_apart(act, out_ready, chunk_of(i, part, back, c) + 1)
                head = i + (part - back) // 2
                for b, k in ((0, 4), (1, 1)):
                    last = a.activation(z[:, c % 2, 0, 4 * b * T:(4 * b + k) * T], p_t[:, b, 0:k * T], ACT.Identity,
                                        bias=b_col[:, bass.ds(head, 1), c])
                last.then_inc(kept, 1)

            def elu_exp(i, part, back, c):
                act.wait_ge(elu_low, chunk_of(i, part, back, c) + 1)
                a.activation(z[:, c % 2, 1, :], z[:, c % 2, 1, :], ACT.Exp).then_inc(elu_exped, 1)

            def out_work(i, part, s, groups):
                if groups >= 2 and s in (1, 3):
                    keep(i, part, 2, (s + 3) // 2)
                if groups >= 2 and s in (1, 3, 5):
                    elu_exp(i, part, 2, (s + 1) // 2)
                if groups >= 1 and s == 5:
                    leave(i, part)
                if groups >= 1 and s in (7, 9):
                    keep(i, part, 1, (s - 7) // 2)
                if groups >= 1 and s == 9:
                    elu_exp(i, part, 1, 0)

            def round_p(i, g):
                act.wait_ge(p_ready, i * STEPS + (g + 1))
                wait_apart(act, p_used, i * STEPS + (g + 1 + 2 * NT - RING))
                a.activation(p_hi[:, g % RING, :], e[:, g % RING, 0, :], ACT.Copy).then_inc(p_hi_ready, 1)

            def body(i, first):
                for g in range(STEPS):
                    part, s = divmod(g, NT)
                    if s == 0:
                        wait_apart(act, uv_in[part], i * 32 + 32)
                    wait_apart(act, p_split, i * STEPS + (g + 1))
                    for kind in range(2):
                        last = a.activation(e[:, g % RING, kind, :], uv[:, part, kind, :], ACT.Exp,
                                            bias=col_src[kind][:, bass.ds(i, 1), s])
                    last.then_inc(exp_ready, 1)
                    if g >= 2 or not first:
                        round_p(i, g - 2)
                    out_work(i, part, s, part if first else 2)

            every_iteration(act, body)
            for g in (STEPS - 2, STEPS - 1):
                round_p(H1 - 1, g)
            for s in range(NT):
                out_work(H1, 0, s, 2)
            for c in (2, 3):
                keep(H1, 1, 2, c)
                elu_exp(H1, 1, 2, c - 1)
            elu_exp(H1, 1, 2, 3)

        @block.vector
        def _(dve):
            v = nc.vector
            v.sem_inc(p_split, RING)
            v.sem_inc(exp_ready, 2 * NT)
            v.sem_inc(out_ready, 2)
            v.memset(ones_f[:], 1.0).then_inc(ones_set, 1)

            def divisors(i, part):
                dve.wait_ge(p_used, i * STEPS + (part * NT + 2 * NT))
                v.tensor_copy(sum_row[:], p_sum[0:1, 0:ROW]).then_inc(sum_steps, 1)
                dve.wait_ge(sums_turned, i * 2 + part)
                v.tensor_scalar(sums[:, 0, :], p_sum[0:T, ROW:ROW + NH + 1], 1e-16, None, ALU.add).then_inc(sum_steps, 1)
                dve.wait_ge(sum_steps, i * 6 + (3 * part - 1))
                v.reciprocal(sums[:, 1, :], sums[:, 0, :]).then_inc(sum_steps, 1)

            def low(i, part, back, c):
                dve.wait_ge(kept, chunk_of(i, part, back, c) + 1)
                v.tensor_scalar(z[:, c % 2, 1, :], z[:, c % 2, 0, :], 0.0, None, ALU.min).then_inc(elu_low, 1)
                v.tensor_scalar(z[:, c % 2, 2, :], z[:, c % 2, 0, :], 0.0, None, ALU.max).then_inc(elu_up, 1)

            def elu(i, part, back, c):
                dve.wait_ge(elu_up, chunk_of(i, part, back, c) + 1)
                dve.wait_ge(elu_exped, chunk_of(i, part, back, c) + 1)
                dve.wait_ge(stored[c % 2], i * (16 * CW) + ((part - back) * 2 + c // 2 + 1) * 16)
                v.scalar_tensor_tensor(out_f[:, c % 2, :], z[:, c % 2, 1, :], -1.0, z[:, c % 2, 2, :],
                                       ALU.add, ALU.add).then_inc(out_ready, 1)

            def out_work(i, part, s, groups):
                if groups >= 2 and s in (1, 3):
                    low(i, part, 2, (s + 3) // 2)
                if groups >= 2 and s in (1, 3, 5):
                    elu(i, part, 2, (s + 1) // 2)
                if groups >= 1 and s == 4:
                    divisors(i, part)
                if groups >= 1 and s in (7, 9):
                    low(i, part, 1, (s - 7) // 2)
                if groups >= 1 and s == 9:
                    elu(i, part, 1, 0)

            def rest_of_p(i, g):
                dve.wait_ge(p_hi_ready, i * STEPS + (g + 1))
                v.tensor_tensor(p_lo[:, g % RING, :], e[:, g % RING, 0, :], p_hi[:, g % RING, :].bitcast(F32),
                                ALU.subtract).then_inc(p_split, 1)

            def body(i, first):
                for g in range(STEPS):
                    part, s = divmod(g, NT)
                    dve.wait_ge(exp_ready, i * STEPS + (g + 1 + 2 * NT))
                    v.tensor_tensor(e[:, g % RING, 0, :], e[:, g % RING, 0, :], e[:, g % RING, 1, :], ALU.max).then_inc(more_ready, 1)
                    dve.wait_ge(more_ready, i * STEPS + (g + 1))
                    v.scalar_tensor_tensor(e[:, g % RING, 0, :], e[:, g % RING, 0, :], 1.0, CT[:, s, part * DH:(part + 1) * DH],
                                           ALU.min, ALU.mult).then_inc(p_ready, 1)
                    if g or not first:
                        rest_of_p(i, g - 1)
                    out_work(i, part, s, part if first else 2)

            every_iteration(dve, body)
            rest_of_p(H1 - 1, STEPS - 1)
            for s in range(NT):
                out_work(H1, 0, s, 2)
            for c in (2, 3):
                low(H1, 1, 2, c)
                elu(H1, 1, 2, c - 1)
            elu(H1, 1, 2, 3)

        @block.tensor
        def _(pe):
            nc.tensor.sem_inc(p_used, 2 * NT)
            nc.tensor.sem_inc(turned, CW)
            pe.wait_ge(ones_set, 2)

            def turn(i, part, c, first_ever=False):
                if c == 0:
                    pe.wait_ge(bank_free, i * (2 * BANKS) + BANKS * (part + 1))
                if not first_ever:
                    pe.wait_ge(kept, chunk_of(i, part, 1, c))
                for d in range(NH):
                    last = nc.tensor.transpose(p_t[:, d // 4, (d % 4) * T:(d % 4 + 1) * T],
                                               res[:, d, c * 128:(c + 1) * 128], ident[0:T, 0:T])
                last.then_inc(turned, 1)

            def body(i, first):
                for g in range(STEPS):
                    part, s = divmod(g, NT)
                    if part == 0:
                        pe.wait_ge(h_split, i * NT + (s + 1 + NT))
                    pe.wait_ge(p_split, i * STEPS + (g + 1 + RING))
                    for d in range(NH):
                        if s == 0:
                            pe.wait_ge(bank_free, i * (2 * BANKS) + (BANKS * part + d + 1))
                        cols = slice(d * T, (d + 1) * T)
                        begin = s == 0
                        for pp, moving in ((p_hi, (h_hi, h_lo)), (p_lo, (h_hi,))):
                            for hp in moving:
                                for half in (slice(0, HALF1), slice(HALF1, C1)):
                                    nc.tensor.matmul(p_o[:, d, half], pp[:, g % RING, cols], hp[:, s, half],
                                                     start=(begin and pp is p_hi and hp is h_hi and half.start == 0),
                                                     stop=(s == NT - 1 and pp is p_lo), skip_group_check=True)
                    for pp in (p_hi, p_lo):
                        nc.tensor.matmul(p_sum[:, 0:ROW], ones[:], pp[:, g % RING, 0:ROW],
                                         start=(begin and pp is p_hi), stop=False, skip_group_check=True)
                    for pp in (p_hi, p_lo):
                        last = nc.tensor.matmul(p_sum[0:T, ROW:ROW + 2], pp[:, g % RING, ROW:DH], ones[:, 0:2],
                                                start=False, stop=(s == NT - 1 and pp is p_lo), skip_group_check=True)
                    last.then_inc(p_used, 1)
                    if s == NT - 1:
                        wait_apart(pe, sum_steps, i * 6 + (3 * part + 1))
                        for d in range(NH - 1):
                            last = nc.tensor.transpose(p_sum[0:T, ROW + 2 + d:ROW + 3 + d], sum_row[:, d * T:(d + 1) * T],
                                                       ident[0:1, 0:1])
                        last.then_inc(sums_turned, 1)
                    if s in (1, 3, 5, 7) and (part or not first):
                        turn(i, part, (s - 1) // 2, first_ever=first and s == 1)

            every_iteration(pe, body)
            for c in range(CW):
                turn(H1, 0, c)


def from_turned(nc, core, turned_rows, K, w, out_rows, x=None, bias=None, stats=None, a_vec=None, score_rows=None,
                col_src=None):
    ident, G = core.ident, core.G
    CW = D // 2
    PARTS = 6 if K % 3 == 0 else 8
    KP, KH = K // PARTS, K // 2
    PARTS_WITH = ((0,), range(1, PARTS // 2 + 1), range(PARTS // 2 + 1, PARTS))
    extra = a_vec is not None
    with ExitStack() as ctx:
        sb, pb, sem = core.tools(ctx)
        w_raw = sb("fw_raw", [128, K, CW], F32)
        w_hi = sb("fw_hi", [128, K, CW], F32R)
        w_lo = sb("fw_lo", [128, K, CW], F32R)
        f_raw = sb("f_raw", [128, 2, KH, T], F32)
        f_hi = sb("f_hi", [128, 2, KH, T], F32R)
        f_lo = sb("f_lo", [128, 2, KH, T], F32R)
        biased = sb("biased", [T, 2, CW], F32) if x is not None else None
        b_row = sb("b_row", [T, D], F32) if x is not None else None
        p_y = pb("p_y", [T, 2, 512])
        if extra:
            a_row = sb("a_row", [T, 2, CW], F32)
            part_now = sb("part_now", [T, 2, NT], F32)
            junk = sb("score_junk", [T, 2, CW], BF16)
            junk_b = sb("max2_junk", [T, 2, N], BF16)
            part = sb("part2", [T, 2, 2, NT], F32)
            score = sb("score2", [T, 2, NT], F32)
            turned = sb("turned2", [4 * NT, T], F32)
            turned_b = sb("turned2b", [4 * NT, T], F32)
            src_row = sb("src_row2", [T, N], F32)
            uv = sb("uv_col2", [T, 2, NT], F32)
            most = sb("most2", [T, NT], F32)
            tmp = sb("tmp_a", [T, NT], F32)
            tmp2 = sb("tmp_b", [T, NT], F32)
            p_s = pb("p_s2", [128, 512])

        w_in = [sem(f"fw_in{i}") for i in range(PARTS)]
        small_in = sem("small_in")
        f_in = [sem(f"f_in{i}") for i in range(2)]
        hi_done = sem("w_hi_done")
        w_split = sem("w_split")
        a_in = sem("a_in2")
        scored = sem("scored2")
        part_kept = sem("part_kept2")
        maxed = sem("maxed2")
        f_hi_done = sem("f_hi_done")
        f_lo_done = sem("f_lo_done")
        piece_used = sem("piece_used")
        y_left = sem("y_left")
        y_biased = sem("y_biased")
        steps = sem("fsteps")
        turned_done = sem("turned_done")
        turned_kept = sem("turned_kept2")
        rows_stored = sem("rows_stored2")
        row_in = sem("row_in2")

        block = ctx.enter_context(nc.Block())

        @block.sync
        def _(sp):
            def load_w(half, parts):
                for part_no in parts:
                    sp.wait_ge(w_split, half * PARTS + (part_no + 1))
                    ks = slice(part_no * KP, (part_no + 1) * KP)
                    sp.dma_start(w_raw[:, ks, :],
                                 w.rearrange("(k p) c -> p k c", p=128)[:, ks, half * CW:(half + 1) * CW]).then_inc(w_in[part_no], 16)

            def load_f(half, t, kh):
                sp.wait_ge(f_lo_done, half * (2 * NT) + (2 * t + kh + 1))
                sp.dma_start(f_raw[:, kh, :, :],
                             turned_rows[kh * KH:(kh + 1) * KH, :, t * T:(t + 1) * T].rearrange("k p n -> p k n")).then_inc(f_in[kh], 16)

            def load_a(half):
                sp.wait_ge(scored, half * (2 * NT) + 4)
                for kind in range(2):
                    sp.dma_start(a_row[:, kind, :], a_vec[kind:kind + 1, half * CW:(half + 1) * CW].broadcast_to([T, CW])).then_inc(a_in, 16)

            for kh in range(2):
                load_w(0, PARTS_WITH[kh])
                load_f(0, 0, kh)
            load_w(0, PARTS_WITH[2])
            for half in range(2):
                if extra:
                    load_a(half)
                for t in range(1 - half, NT):
                    for kh in range(2):
                        load_f(half, t, kh)
                    if half == 0 and t == 2:
                        load_w(1, range(PARTS))
            if extra:
                sp.wait_ge(turned_kept, 1)
                sp.dma_start(score_rows[0:2 * NT, :], turned[0:2 * NT, :]).then_inc(rows_stored, 16)
                sp.wait_ge(rows_stored, 16)
                sp.dma_start(src_row[:], score_rows[0:NT, :].rearrange("(o t) p -> o (t p)", o=1).broadcast_to([T, N])).then_inc(row_in, 16)
                sp.wait_ge(turned_kept, 2)
                sp.dma_start(core.uv_rows[0, 0:NT, :], turned_b[0:NT, :]).then_inc(rows_stored, 16)
                sp.dma_start(core.uv_rows[1, 0:NT, :], turned_b[NT:2 * NT, :]).then_inc(rows_stored, 16)
                sp.wait_ge(rows_stored, 48)

        @block.gpsimd
        def _(pool):
            if x is not None:
                pool.wait_ge(hi_done, PARTS - 2)
                pool.dma_start(out_rows[:], rows_of(x)).then_inc(small_in, 16)
                pool.dma_start(b_row[:], bias.rearrange("(o f) -> o f", o=1).broadcast_to([T, D])).then_inc(small_in, 16)

        @block.vector
        def _(dve):
            v = nc.vector
            v.sem_inc(f_lo_done, 2)
            if x is not None:
                v.sem_inc(y_left, 2)
            else:
                v.sem_inc(scored, 4)
            with dve.Fori(0, 2) as half:
                def rest_of_f(t, kh):
                    dve.wait_ge(f_hi_done, half * (2 * NT) + (2 * t + kh + 1))
                    v.tensor_tensor(f_lo[:, kh], f_raw[:, kh], f_hi[:, kh].bitcast(F32), ALU.subtract).then_inc(f_lo_done, 1)

                def rest_of_w(part_no):
                    ks = slice(part_no * KP, (part_no + 1) * KP)
                    dve.wait_ge(hi_done, half * PARTS + (part_no + 1))
                    v.tensor_tensor(w_lo[:, ks, :], w_raw[:, ks, :], w_hi[:, ks, :].bitcast(F32),
                                    ALU.subtract).then_inc(w_split, 1)

                def score_of(t):
                    wait_apart(dve, y_left, half * NT + (t + 1))
                    if t == 0:
                        wait_apart(dve, a_in, half * 32 + 32)
                    for kind in range(2):
                        wait_apart(dve, scored, half * (2 * NT) + (2 * t + kind + 1 + 2))
                        v.tensor_tensor_reduce(out=junk[:, kind, :], in0=p_y[:, t % 2, 0:CW], in1=a_row[:, kind, :],
                                               scale=1.0, scalar=0.0, op0=ALU.mult, op1=ALU.add,
                                               accum_out=part_now[:, kind, t:t + 1]).then_inc(scored, 1)

                def statistics(t):
                    wait_apart(dve, y_biased, half * NT + (t + 1))
                    v.bn_stats(stats[:, t, bass.ds(half, 1), :].rearrange("p o s -> p (o s)"), out_rows[:, t, bass.ds(half * CW, CW)])

                def leave(t):
                    if t:
                        statistics(t - 1)
                    else:
                        wait_apart(dve, small_in, 32)
                    dve.wait_ge(piece_used, half * (2 * NT) + (2 * t + 2 + 2 * NT))
                    cols = bass.ds(half * CW, CW)
                    v.tensor_tensor(biased[:, t % 2, :], p_y[:, t % 2, 0:CW], b_row[:, cols], ALU.add).then_inc(y_left, 1)
                    dve.wait_ge(y_left, half * NT + (t + 3))
                    v.scalar_tensor_tensor(out_rows[:, t, cols], biased[:, t % 2, :], 0.0, out_rows[:, t, cols],
                                           ALU.max, ALU.add).then_inc(y_biased, 1)

                for t in range(NT):
                    for kh in range(2):
                        if t == 0:
                            for part_no in PARTS_WITH[kh]:
                                rest_of_w(part_no)
                        rest_of_f(t, kh)
                    if t == 0:
                        for part_no in PARTS_WITH[2]:
                            rest_of_w(part_no)
                    if t:
                        leave(t - 1) if x is not None else score_of(t - 1)
                if x is not None:
                    leave(NT - 1)
                    statistics(NT - 1)
                else:
                    score_of(NT - 1)
                    dve.wait_ge(scored, half * (2 * NT) + (2 * NT + 4))
                    v.tensor_copy(part[:, :, bass.ds(half, 1), :], part_now[:].rearrange("p k (o t) -> p k o t", o=1)).then_inc(part_kept, 1)
            if extra:
                step = Chain(dve, steps)
                dve.wait_ge(part_kept, 2)
                step(v.tensor_tensor(score[:], part[:, :, 0], part[:, :, 1], ALU.add))
                v.tensor_copy(col_src[0][:, 0, :], score[:, 0])
                step(v.tensor_scalar(col_src[1][:, 0, :], score[:, 0], SLOPE, None, ALU.mult))
                dve.wait_ge(row_in, 16)
                for t in range(NT):
                    if t >= 2:
                        dve.wait_ge(maxed, t - 1)
                    v.tensor_tensor_reduce(out=junk_b[:, t % 2, :], in0=src_row[:], in1=G[:, t, :], scale=1.0, scalar=NO_EDGE,
                                           op0=ALU.add, op1=ALU.max, accum_out=most[:, t:t + 1]).then_inc(maxed, 1)
                dve.wait_ge(maxed, NT)
                step(v.tensor_tensor(tmp[:], most[:], score[:, 1], ALU.add))
                step(v.scalar_tensor_tensor(tmp2[:], tmp[:], SLOPE, tmp[:], ALU.mult, ALU.max))
                v.tensor_tensor(uv[:, 0], score[:, 1], tmp2[:], ALU.subtract)
                step(v.scalar_tensor_tensor(uv[:, 1], score[:, 1], SLOPE, tmp2[:], ALU.mult, ALU.subtract))

        @block.scalar
        def _(act):
            a = nc.scalar
            a.sem_inc(w_split, PARTS)
            with act.Fori(0, 2) as half:
                def round_w(part_no):
                    ks = slice(part_no * KP, (part_no + 1) * KP)
                    act.wait_ge(w_in[part_no], half * 16 + 16)
                    wait_apart(act, piece_used, half * (2 * NT) + 2 * NT)
                    a.activation(w_hi[:, ks, :], w_raw[:, ks, :], ACT.Copy).then_inc(hi_done, 1)

                def leave(t):
                    act.wait_ge(piece_used, half * (2 * NT) + (2 * t + 2 + 2 * NT))
                    a.activation(out_rows[:, t, bass.ds(half * CW, CW)], p_y[:, t % 2, 0:CW], ACT.Copy).then_inc(y_left, 1)

                for t in range(NT):
                    for kh in range(2):
                        if t == 0:
                            for part_no in PARTS_WITH[kh]:
                                round_w(part_no)
                        act.wait_ge(f_in[kh], half * (16 * NT) + 16 * (t + 1))
                        act.wait_ge(piece_used, half * (2 * NT) + (2 * t + kh + 2 * NT - 1))
                        a.activation(f_hi[:, kh], f_raw[:, kh], ACT.Copy).then_inc(f_hi_done, 1)
                    if t == 0:
                        for part_no in PARTS_WITH[2]:
                            round_w(part_no)
                    if extra and t:
                        leave(t - 1)
                if extra:
                    leave(NT - 1)
            if extra:
                for n, to in enumerate((turned, turned_b)):
                    act.wait_ge(turned_done, n + 1)
                    a.activation(to[0:2 * NT, :], p_s[0:2 * NT, 0:T], ACT.Copy).then_inc(turned_kept, 1)

        @block.tensor
        def _(pe):
            nc.tensor.sem_inc(piece_used, 2 * NT)
            with pe.Fori(0, 2) as half:
                for t in range(NT):
                    if extra:
                        pe.wait_ge(scored, half * (2 * NT) + (2 * t + 2))
                    else:
                        pe.wait_ge(y_left, half * NT + (t + 1))
                    for kh in range(2):
                        pe.wait_ge(f_lo_done, half * (2 * NT) + (2 * t + kh + 3))
                        for kk in range(KH):
                            k = kh * KH + kk
                            if t == 0 and k % KP == 0:
                                pe.wait_ge(w_split, half * PARTS + (k // KP + 1 + PARTS))
                            for n, (fp, wp) in enumerate(((f_hi, w_hi), (f_hi, w_lo), (f_lo, w_hi))):
                                last = nc.tensor.matmul(p_y[:, t % 2, 0:CW], fp[:, kh, kk, :], wp[:, k, :],
                                                        start=(k == 0 and n == 0), stop=(k == K - 1 and n == 2))
                        last.then_inc(piece_used, 1)
            if extra:
                pe.wait_ge(steps, 1)
                nc.tensor.transpose(p_s[0:2 * NT, 0:T], score[:].rearrange("p a t -> p (a t)"), ident[0:T, 0:T]).then_inc(turned_done, 1)
                pe.wait_ge(steps, 5)
                pe.wait_ge(turned_kept, 1)
                nc.tensor.transpose(p_s[0:2 * NT, 0:T], uv[:].rearrange("p a t -> p (a t)"), ident[0:T, 0:T]).then_inc(turned_done, 1)


def normalize(nc, core, y, stats, to_dram, xT=None):
    ident = core.ident
    with ExitStack() as ctx:
        sb, pb, sem = core.tools(ctx)
        moments = sb("ln_moments", [T, NT, 2], F32)
        var = sb("ln_var", [T, NT], F32)
        root = sb("ln_root", [T, NT], F32)
        inv = sb("ln_inv", [T, NT], F32)
        tmp = sb("ln_tmp", [T, NT], F32)
        better = sb("ln_better", [T, NT], F32)
        normed = sb("normed", [T, NT, D], F32)
        p_t = pb("ln_p", [128, 4, 512]) if xT else None
        steps = sem("ln_steps")
        var_done = sem("var_done")
        root_done = sem("root_done")
        normed_done = sem("normed_done")
        stored = sem("ln_stored")
        turned = sem("ln_turned")
        hi_done = sem("ln_hi")
        lo_done = sem("ln_lo")
        block = ctx.enter_context(nc.Block())
        HT = NH

        @block.sync
        def _(sp):
            for q in range(2):
                sp.wait_ge(normed_done, HT * (q + 1))
                sp.dma_start(rows_of(to_dram)[:, q * HT:(q + 1) * HT, :], normed[:, q * HT:(q + 1) * HT, :]).then_inc(stored, 16)
            sp.wait_ge(stored, 32)

        @block.vector
        def _(dve):
            v = nc.vector
            step = Chain(dve, steps)
            for t in range(NT):
                last = v.bn_aggr(moments[:, t, :], stats[:, t, :, :])
            step(last)
            v.tensor_scalar(var[:], moments[:, :, 1], EPS, None, ALU.add).then_inc(var_done, 1)
            dve.wait_ge(root_done, 1)
            step(v.reciprocal(inv[:], root[:]))
            step(v.tensor_tensor(tmp[:], inv[:], inv[:], ALU.mult))
            step(v.scalar_tensor_tensor(tmp[:], tmp[:], -0.5, var[:], ALU.mult, ALU.mult))
            step(v.scalar_tensor_tensor(better[:], tmp[:], 1.5, inv[:], ALU.add, ALU.mult))
            for t in range(NT):
                v.tensor_scalar(normed[:, t, :], y[:, t, :], moments[:, t, 0:1], better[:, t:t + 1],
                                ALU.subtract, ALU.mult).then_inc(normed_done, 1)
            if xT:
                for n in range(3 * KD):
                    k = n // 3
                    dve.wait_ge(hi_done, n + 1)
                    g = n % 3
                    a, m = 4 * g * T, (4 if g < 2 else 2) * T
                    v.tensor_tensor(xT[1][:, k, a:a + m], p_t[:, n % 4, 0:m], xT[0][:, k, a:a + m].bitcast(F32),
                                    ALU.subtract).then_inc(lo_done, 1)

        @block.scalar
        def _(act):
            act.wait_ge(var_done, 1)
            nc.scalar.activation(root[:], var[:], ACT.Sqrt).then_inc(root_done, 1)
            if xT:
                for n in range(3 * KD):
                    k, g = divmod(n, 3)
                    a, m = 4 * g * T, (4 if g < 2 else 2) * T
                    act.wait_ge(turned, n + 1)
                    nc.scalar.activation(xT[0][:, k, a:a + m], p_t[:, n % 4, 0:m], ACT.Copy).then_inc(hi_done, 1)

        @block.tensor
        def _(pe):
            if xT:
                pe.wait_ge(normed_done, NT)
                for n in range(3 * KD):
                    k, g = divmod(n, 3)
                    if n >= 4:
                        pe.wait_ge(lo_done, n - 3)
                    for i in range(4 if g < 2 else 2):
                        t = 4 * g + i
                        last = nc.tensor.transpose(p_t[:, n % 4, i * T:(i + 1) * T], normed[:, t, k * 128:(k + 1) * 128],
                                                   ident[0:T, 0:T])
                    last.then_inc(turned, 1)


def aggregate_last(nc, core, h2, col_src, bias, x2_dram, y2, stats):
    CT = core.CT
    PIECE = D // 3
    STEPS = 2 * NT
    RING = 4
    ORDER = tuple(reversed(range(NH)))
    OPENS = (12, 14, 9, 10, 6, 3, 4, 0)
    with ExitStack() as ctx:
        sb, pb, sem = core.tools(ctx)
        uv = sb("uv_l", [T, 2, N], F32)
        h_hi = sb("h_hi_l", [T, NT, D], F32R)
        e = sb("e_l", [T, RING, 2, DH], F32)
        p_hi = sb("p_hi_l", [T, RING, DH], F32R)
        p_lo = sb("p_lo_l", [T, RING, DH], F32R)
        sums = sb("sums_l", [T, 2, NH], F32)
        ones_f = sb("ones_fl", [T, 2], F32)
        ones = sb("ones_l", [T, 2], F32R)
        b_row = sb("b_row_l", [T, D], F32)
        mean = sb("mean_l", [T, 2, D], F32)
        p_o = pb("p_ol", [T, 8, 512])
        in_sem = sem("in_l")
        base_in = sem("base_in_l")
        ones_set = sem("ones_set_l")
        h_hi_done = sem("h_hi_done_l")
        h_split = sem("h_split_l")
        exp_ready = sem("exp_ready_l")
        more_ready = sem("more_ready_l")
        p_ready = sem("p_ready_l")
        p_hi_ready = sem("p_hi_ready_l")
        p_split = sem("p_split_l")
        p_used = sem("p_used_l")
        sum_steps = sem("sum_steps_l")
        mean_out = sem("mean_out_l")
        biased = sem("biased_l")
        mean_biased = sem("mean_biased_l")
        block = ctx.enter_context(nc.Block())
        h_lo = h2[:].bitcast(F32R)

        @block.sync
        def _(sp):
            for kind in range(2):
                sp.dma_start(uv[:, kind, :], core.uv_rows[kind, 0:NT, :].rearrange("(o t) p -> o (t p)", o=1)
                             .broadcast_to([T, N])).then_inc(in_sem, 16)
            sp.dma_start(b_row[:], bias.rearrange("(o f) -> o f", o=1).broadcast_to([T, D])).then_inc(base_in, 16)
            sp.dma_start(y2[:], rows_of(x2_dram)).then_inc(base_in, 16)

        @block.gpsimd
        def _(pool):
            for s in range(NT):
                pool.tensor_copy(h_hi[:, s, :], h2[:, s, :]).then_inc(h_hi_done, 1)
                pool.wait_ge(h_hi_done, s + 1)
                pool.tensor_tensor(h_lo[:, s, :], h2[:, s, :], h_hi[:, s, :].bitcast(F32), ALU.subtract).then_inc(h_split, 1)

        @block.scalar
        def _(act):
            a = nc.scalar
            act.wait_ge(ones_set, 1)
            a.activation(ones[:], ones_f[:], ACT.Copy).then_inc(ones_set, 1)
            act.wait_ge(in_sem, 32)

            def leave(part):
                act.wait_ge(sum_steps, 2 * part + 2)
                for n, d in enumerate(ORDER, part * NH):
                    if n >= 2:
                        act.wait_ge(biased, n - 1)
                    for j in range(3):
                        w = 3 * d + j
                        last = a.activation(mean[:, n % 2, j * PIECE:(j + 1) * PIECE],
                                            p_o[:, w // 2, (w % 2) * 256:(w % 2) * 256 + PIECE], ACT.Copy,
                                            scale=sums[:, 1, d:d + 1])
                    last.then_inc(mean_out, 1)

            def round_p(g):
                act.wait_ge(p_ready, g + 1)
                if g >= RING:
                    act.wait_ge(p_used, g - RING + 1)
                a.activation(p_hi[:, g % RING, :], e[:, g % RING, 0, :], ACT.Copy).then_inc(p_hi_ready, 1)

            for g in range(STEPS):
                part, s = divmod(g, NT)
                if g >= RING:
                    act.wait_ge(p_split, g - RING + 1)
                for kind in range(2):
                    last = a.activation(e[:, g % RING, kind, :], uv[:, kind, part * DH:(part + 1) * DH], ACT.Exp,
                                        bias=col_src[kind][:, 0, s:s + 1])
                last.then_inc(exp_ready, 1)
                if g >= 2:
                    round_p(g - 2)
                if g == NT + 5:
                    leave(0)
            round_p(STEPS - 2)
            round_p(STEPS - 1)
            leave(1)

        @block.vector
        def _(dve):
            v = nc.vector
            v.memset(ones_f[:], 1.0).then_inc(ones_set, 1)

            def divisors(part):
                dve.wait_ge(p_used, (part + 1) * NT)
                v.tensor_scalar(sums[:, 0, :], p_o[:, 7, 256:256 + 2 * NH].rearrange("p (d a) -> p d a", a=2)[:, :, 0],
                                1e-16, None, ALU.add).then_inc(sum_steps, 1)
                dve.wait_ge(sum_steps, 2 * part + 1)
                v.reciprocal(sums[:, 1, :], sums[:, 0, :]).then_inc(sum_steps, 1)

            def add_base(part):
                for n, d in enumerate(ORDER, part * NH):
                    t = part * NH + d
                    dve.wait_ge(mean_out, n + 1)
                    v.tensor_tensor(mean[:, n % 2, :], mean[:, n % 2, :], b_row[:], ALU.add).then_inc(mean_biased, 1)
                    dve.wait_ge(mean_biased, n + 1)
                    v.tensor_tensor(y2[:, t, :], y2[:, t, :], mean[:, n % 2, :], ALU.add).then_inc(biased, 1)
                    dve.wait_ge(biased, n + 1)
                    for q in range(2):
                        v.bn_stats(stats[:, t, q, :], y2[:, t, q * (D // 2):(q + 1) * (D // 2)])

            def rest_of_p(g):
                dve.wait_ge(p_hi_ready, g + 1)
                v.tensor_tensor(p_lo[:, g % RING, :], e[:, g % RING, 0, :], p_hi[:, g % RING, :].bitcast(F32),
                                ALU.subtract).then_inc(p_split, 1)

            for g in range(STEPS):
                part, s = divmod(g, NT)
                dve.wait_ge(exp_ready, g + 1)
                v.tensor_tensor(e[:, g % RING, 0, :], e[:, g % RING, 0, :], e[:, g % RING, 1, :], ALU.max).then_inc(more_ready, 1)
                dve.wait_ge(more_ready, g + 1)
                v.scalar_tensor_tensor(e[:, g % RING, 0, :], e[:, g % RING, 0, :], 1.0, CT[:, s, part * DH:(part + 1) * DH],
                                       ALU.min, ALU.mult).then_inc(p_ready, 1)
                if g:
                    rest_of_p(g - 1)
                if g == NT + 4:
                    divisors(0)
                    dve.wait_ge(base_in, 32)
                    add_base(0)
            rest_of_p(STEPS - 1)
            divisors(1)
            add_base(1)

        @block.tensor
        def _(pe):
            pe.wait_ge(ones_set, 2)
            for g in range(STEPS):
                part, s = divmod(g, NT)
                if part == 0:
                    pe.wait_ge(h_split, s + 1)
                pe.wait_ge(p_split, g + 1)
                for d in ORDER:
                    if part and s == 0 and d in (4, 3, 1):
                        pe.wait_ge(mean_out, {4: 1, 3: 3, 1: 5}[d])
                    for pp, moving in ((p_hi, (h_hi, h_lo)), (p_lo, (h_hi,))):
                        stationary = pp[:, g % RING, d * T:(d + 1) * T]
                        for hp in moving:
                            for j in range(3):
                                w = 3 * d + j
                                nc.tensor.matmul(p_o[:, w // 2, (w % 2) * 256:(w % 2) * 256 + PIECE], stationary,
                                                 hp[:, s, j * PIECE:(j + 1) * PIECE],
                                                 start=(s == 0 and w in OPENS and pp is p_hi and hp is h_hi),
                                                 stop=(s == NT - 1 and pp is p_lo), skip_group_check=True)
                        last = nc.tensor.matmul(p_o[:, 7, 256 + 2 * d:258 + 2 * d], stationary, ones[:], start=False,
                                                stop=(s == NT - 1 and pp is p_lo), skip_group_check=True)
                last.then_inc(p_used, 1)


def gnn_two_layers(nc, src, dst, x, w_ah, b_ah, w_gat0, a_gat0, b_gat0, w_out, b_out, w1, a1, b1, w2, a2, b2, out):
    dram = lambda name, shape: nc.dram_tensor(name, shape, F32, kind="Internal").ap()
    h0_rows = dram("h0_rows", [CONVS * H0, N, HC0])
    h1_rows = dram("h1_rows", [2 * H1, N, HALF1])
    score_rows = dram("score_rows", [CONVS * 2 * H0, N])
    score_rows2 = dram("score_rows2", [2 * NT, T])
    turned0 = dram("turned0", [KO, 128, N])
    turned1 = dram("turned1", [K1, 128, N])
    x2_rows = dram("x2_rows", [N, D])
    with ExitStack() as ctx:
        core = Core(nc)
        core.uv_rows = dram("uv_rows", [2, CONVS * H0 * NT, T])
        sb, _, sem = core.tools(ctx)
        core.ident = sb("ident", [128, 128], F32)
        core.wa1 = sb("wa1", [128, KD, 2, H1], F32)
        stats = sb("stats", [T, NT, 2, 6], F32)
        core.CT = sb("CT", [T, NT, N], U16)
        core.G = sb("G", [T, NT, N], BF16)
        cols = [sb(f"col{i}", [T, CONVS * H0, NT], F32) for i in range(4)]
        core.ident_ready = sem("ident_ready")
        sem_of_waits[0] = sem("waits")
        nc.gpsimd.memset(core.ident[:], 0.0).then_inc(core.ident_ready, 1)
        nc.gpsimd.wait_ge(core.ident_ready, 1)
        nc.gpsimd.affine_select(out=core.ident[:], in_=core.ident[:], compare_op=ALU.not_equal, fill=1.0, base=0,
                                pattern=[[-1, 128]], channel_multiplier=1).then_inc(core.ident_ready, 1)
        with ExitStack() as inner:
            sb1 = core.tools(inner)[0]
            core.wa0 = sb1("wa0", [128, KD, 2, CONVS * H0], F32)
            core.x1T = [sb1(f"x1T{i}", [128, KD, N], F32R) for i in range(2)]
            counts_and_x1(nc, core, src, dst, x, w_ah, b_ah, w_gat0, a_gat0)
            project(nc, core, core.x1T, w_gat0, core.wa0, h0_rows, score_rows, PAIR, cols[0:2], *cols[2:4])
        aggregate_layer0(nc, core, h0_rows, cols[0:2], b_gat0, turned0, w1, a1)
        with ExitStack() as inner:
            sb1 = core.tools(inner)[0]
            y = sb1("y", [T, NT, D], F32)
            from_turned(nc, core, turned0, KO, w_out, y, x=x, bias=b_out, stats=stats)
            x2T = [sb1(f"x2T{i}", [128, KD, N], F32R) for i in range(2)]
            normalize(nc, core, y, stats, x2_rows, x2T)
            project(nc, core, x2T, w1, core.wa1, h1_rows, score_rows, HALF1, cols[0:2], *cols[2:4])
        aggregate_layer1(nc, core, h1_rows, cols[0:2], b1, turned1)
        with ExitStack() as inner:
            sb1 = core.tools(inner)[0]
            h2 = sb1("h2", [T, NT, D], F32)
            from_turned(nc, core, turned1, K1, w2, h2, a_vec=a2, score_rows=score_rows2, col_src=cols[0:2])
            y2 = sb1("y2", [T, NT, D], F32)
            aggregate_last(nc, core, h2, cols[0:2], b2, x2_rows, y2, stats)
            normalize(nc, core, y2, stats, out)


def kernel(**inputs):
    import numpy as np
    import concourse.bacc as bacc
    from concourse import mybir as _mybir
    from concourse.bass_utils import run_bass_kernel_spmd

    g = {k: np.asarray(v) for k, v in inputs.items()}
    L0, L1 = "L0_gnn_", "L1_gnn_"
    by_unit = lambda w, width: np.stack([w[:, q:q + width] for q in range(0, w.shape[1], width)])
    a_units = lambda s, d, width: np.stack([s.reshape(-1, width), d.reshape(-1, width)], axis=1)
    by_feature = lambda b, groups: b.reshape(groups, -1, 128).transpose(2, 0, 1)
    arrays = {
        "src": g["src"], "dst": g["dst"], "x": g["x"], "w_ah": g[L0 + "W_ah"], "b_ah": by_feature(g[L0 + "b_ah"], 1)[:, 0],
        "w_gat0": np.concatenate([by_unit(g[f"{L0}W{i}"], PAIR) for i in range(CONVS)]),
        "a_gat0": np.concatenate([a_units(g[f"{L0}a_src{i}"], g[f"{L0}a_dst{i}"], PAIR) for i in range(CONVS)]),
        "b_gat0": by_feature(np.concatenate([g[f"{L0}b{i}"] for i in range(CONVS)]), 2 * CONVS),
        "w_out": g[L0 + "W_out"], "b_out": g[L0 + "b_out"],
        "w1": by_unit(g[L1 + "W1"], HALF1), "a1": a_units(g[L1 + "a1_src"], g[L1 + "a1_dst"], HALF1), "b1": by_feature(g[L1 + "b1"], H1),
        "w2": g[L1 + "W2"], "a2": np.concatenate([g[L1 + "a2_src"], g[L1 + "a2_dst"]]), "b2": g[L1 + "b2"],
    }
    arrays = {f"in_{k}": np.ascontiguousarray(v) for k, v in arrays.items()}
    nc = bacc.Bacc("TRN2", target_bir_lowering=False, num_devices=1)
    args = [nc.dram_tensor(k, v.shape, _mybir.dt.from_np(v.dtype), kind="ExternalInput").ap() for k, v in arrays.items()]
    out = nc.dram_tensor("out", (N, D), F32, kind="ExternalOutput").ap()
    gnn_two_layers(nc, *args, out)
    return run_bass_kernel_spmd(nc, [arrays], core_ids=[0]).results[0]["out"]
```

```python
import concourse.bass as bass
from concourse import mybir
from contextlib import ExitStack

F32 = mybir.dt.float32
F32R = mybir.dt.float32r
BF16 = mybir.dt.bfloat16
U16 = mybir.dt.uint16
I16 = mybir.dt.int16
I32 = mybir.dt.int32
ALU = mybir.AluOpType
ACT = mybir.ActivationFunctionType
AX = mybir.AxisListType

N = 1250
D = 768
E = 20000
T = 125
NT = N // T
KD = D // 128
RUN = 4
ER = E // (RUN * T)
SLOPE = 0.2
EPS = 1e-5
NO_EDGE = -3e38

H0, C0 = 4, 192
CONVS = 3
PAIR = 2 * C0
HC0 = C0 + 2
H1, C1 = 4, 512
HALF1 = C1 // 2
DH = N // 2
NH = NT // 2
K1 = H1 * C1 // 128
KO = CONVS * D // 128


class Core:

    def __init__(self, nc):
        self.nc = nc
        self.stages = 0

    def tools(self, ctx):
        nc, n = self.nc, self.stages
        self.stages += 1
        sb = lambda name, shape, dt: ctx.enter_context(nc.sbuf_tensor(f"{name}_{n}", shape, dt))
        pb = lambda name, shape: ctx.enter_context(nc.psum_tensor(f"{name}_{n}", shape, F32))
        sems = []

        def sem(name):
            sems.append(nc.alloc_semaphore(f"{name}_{n}"))
            return sems[-1]

        def clear():
            if sems:
                nc.clear_and_free_semaphores(sems)
                nc.all_engine_barrier()

        ctx.callback(clear)
        return sb, pb, sem


def rows_of(dram_rows):
    return dram_rows.rearrange("(t p) f -> p t f", p=T)


def wait_apart(eng, sem, value):
    eng.wait_ge(sem, value)
    eng.sem_inc(waits_done[0], 1)


waits_done = [None]


class Chain:

    def __init__(self, eng, sem):
        self.eng, self.sem, self.n = eng, sem, 0

    def __call__(self, ins):
        self.n += 1
        ins.then_inc(self.sem, 1)
        self.eng.wait_ge(self.sem, self.n)


def counts_and_x1(nc, core, src, dst, x, w_ah, b_ah, w_gat, a_gat):
    ident, CT, G, x1T = core.ident, core.CT, core.G, core.x1T
    BT = 2 * T
    NB = NT // 2
    CH = [(0, 418), (418, 416), (834, 416)]
    with ExitStack() as ctx:
        sb, pb, sem = core.tools(ctx)
        dst_ends = sb("dst_ends", [ER, 2], F32)
        ends_row = sb("ends_row", [128, 2, ER], F32)
        edge_col = sb("edge_col", [T, 2, RUN, 2 * ER], F32)
        spare = CT[0:1, :, :].rearrange("p t n -> p (t n)")[:, 0:2 * 5 * NT * ER].bitcast(F32) \
            .rearrange("p (a t e) -> p a t e", a=5, t=NT)
        meets, meets_b, meets_c = (spare[:, i] for i in range(3))
        tile_lo, run_no = (spare[:, i].bitcast(I32) for i in (3, 4))
        range_f = sb("range_f", [1, 3, NT], F32)
        ones_row = sb("ones_row", [1, NT], F32)
        range_i = sb("range_i", [1, 3, NT], I32)
        node_no = sb("node_no", [T, N], I16)
        src_hot = sb("src_hot", [T, RUN, N], BF16)
        dst_hot = sb("dst_hot", [T, RUN, T], BF16)
        band = sb("band", [T, 2 * N - T], BF16)
        ident_b = sb("ident_b", [T, T], BF16)
        zeros_b = sb("zeros_b", [T, T], BF16)
        count_row = sb("count_row", [T, N], F32)
        edge_f = count_row[0:ER, 0:2 * RUN * T].rearrange("p (a e) -> p a e", a=2)
        w_raw = core.G_room[:, NT - 3:NT, :].rearrange("p t n -> p (t n)")[:, 0:4 * D].bitcast(F32).rearrange("p (a d) -> p a d", a=2)
        w_hi = sb("w_hi", [128, KD, D], F32R)
        w_lo = sb("w_lo", [128, KD, D], F32R)
        bias = sb("bias_ah", [128, KD], F32)
        x_in = sb("x_in", [T, 2, D], F32)
        xT_hi = sb("xT_hi", [128, KD, BT], F32R)
        xT_lo = sb("xT_lo", [128, KD, BT], F32R)
        x1_f = sb("x1_f", [128, 2, 2 * BT], F32)
        edge_i = x1_f[0:ER].rearrange("p a n -> p (a n)")[:, 0:2 * RUN * T].bitcast(I32).rearrange("p (a e) -> p a e", a=2)
        p_count = pb("p_count", [T, 3, 512])
        p_turn = pb("p_turn", [128, 3, 512])
        p_x = pb("p_x", [128, 2, 512])

        edges_in = sem("edges_in")
        w_in = [sem(f"w_in{i}") for i in range(2)]
        bias_in = sem("bias_in")
        consts = sem("consts")
        steps = sem("steps")
        edges_turned = sem("edges_turned")
        cols_ready = sem("cols_ready")
        ranges_ready = sem("ranges_ready")
        hot_ready = sem("hot_ready")
        hot_free = sem("hot_free")
        counted = sem("counted")
        row_staged = sem("row_staged")
        mask_done = sem("mask_done")
        row_turned = sem("row_turned")
        ct_done = sem("ct_done")
        w_split = sem("w_split")
        x_loaded = sem("x_loaded")
        x_turned = sem("x_turned")
        xhi_done = sem("xhi_done")
        xlo_done = sem("xlo_done")
        x1_summed = sem("x1_summed")
        x1_relu = sem("x1_relu")
        x1_hi_done = sem("x1_hi_done")
        x1_lo_done = sem("x1_lo_done")

        by_a = WeightsByA(nc, sb, sem, w_gat, a_gat, core.wa0, 1)

        block = ctx.enter_context(nc.Block())

        @block.sync
        def _(sp):
            sp.dma_start(edge_i[:, 0, :], src.rearrange("(p e) -> p e", e=RUN * T)).then_inc(edges_in, 16)
            sp.dma_start(edge_i[:, 1, :], dst.rearrange("(p e) -> p e", e=RUN * T)).then_inc(edges_in, 16)
            sp.dma_start(x_in[:], rows_of(x)[:, 0:2, :]).then_inc(x_loaded, 16)
            sp.dma_start(bias[:], b_ah).then_inc(bias_in, 16)
            for k in range(KD):
                if k >= 2:
                    sp.wait_ge(w_split, 2 * (k - 1))
                sp.dma_start(w_raw[:, k % 2, :], w_ah[k * 128:(k + 1) * 128, :]).then_inc(w_in[k % 2], 16)
            for b in range(1, NB):
                sp.wait_ge(x_turned, 3 * b)
                sp.dma_start(x_in[:], rows_of(x)[:, 2 * b:2 * b + 2, :]).then_inc(x_loaded, 16)

        @block.gpsimd
        def _(pool):
            pool.iota(node_no[:], [[1, N]], base=0, channel_multiplier=0).then_inc(consts, 1)
            pool.iota(tile_lo, [[T, NT], [0, ER]], base=0, channel_multiplier=0).then_inc(consts, 1)
            pool.iota(run_no, [[0, NT], [1, ER]], base=0, channel_multiplier=0).then_inc(consts, 1)
            for m in (band, ident_b, zeros_b):
                pool.memset(m[:], 0.0).then_inc(consts, 1)
            pool.wait_ge(consts, 6)
            pool.affine_select(out=ident_b[:], in_=ident_b[:], compare_op=ALU.not_equal, fill=1.0, base=0,
                               pattern=[[-1, T]], channel_multiplier=1).then_inc(consts, 1)
            pool.affine_select(out=band[:], in_=band[:], compare_op=ALU.not_equal, fill=1.0, base=N - T,
                               pattern=[[-1, 2 * N - T]], channel_multiplier=1).then_inc(consts, 1)
            for k in range(KD):
                pool.wait_ge(w_in[k % 2], 16 * (k // 2 + 1))
                pool.tensor_copy(w_hi[:, k, :], w_raw[:, k % 2, :]).then_inc(w_split, 1)
                pool.wait_ge(w_split, 2 * k + 1)
                pool.tensor_tensor(w_lo[:, k, :], w_raw[:, k % 2, :], w_hi[:, k, :].bitcast(F32),
                                   ALU.subtract).then_inc(w_split, 1)
            by_a_group = by_a.program(pool)
            with pool.Fori(0, by_a.groups) as g:
                by_a_group(g)

        @block.vector
        def _(dve):
            v = nc.vector
            step = Chain(dve, steps)
            dve.wait_ge(edges_in, 32)
            step(v.tensor_copy(edge_f, edge_i))
            step(v.tensor_reduce(out=dst_ends[:, 0:1], in_=edge_f[:, 1, :], axis=AX.X, op=ALU.min))
            step(v.tensor_reduce(out=dst_ends[:, 1:2], in_=edge_f[:, 1, :], axis=AX.X, op=ALU.max))
            dve.wait_ge(edges_turned, 1)
            v.tensor_copy(edge_col[:, :, :, 0:ER],
                          p_turn[0:T, 0, 0:2 * RUN * ER].rearrange("p (a b c) -> p a b c", a=2, b=RUN)).then_inc(cols_ready, 1)
            step(v.tensor_copy(ends_row[:], p_turn[:, 1, 0:2 * ER].rearrange("p (a c) -> p a c", a=2)))
            dve.wait_ge(consts, 3)
            least = ends_row[0:1, 0:1, :].broadcast_to([1, NT, ER])
            most = ends_row[0:1, 1:2, :].broadcast_to([1, NT, ER])
            step(v.tensor_tensor(meets, most, tile_lo, ALU.is_ge))
            step(v.scalar_tensor_tensor(meets_b, tile_lo, float(T), least, ALU.add, ALU.is_gt))
            step(v.tensor_tensor(meets, meets, meets_b, ALU.mult))
            step(v.scalar_tensor_tensor(meets_b, run_no, float(-ER), meets, ALU.add, ALU.mult))
            step(v.scalar_tensor_tensor(meets_c, run_no, 1.0, meets, ALU.add, ALU.mult))
            step(v.tensor_reduce(out=range_f[:, 0, :], in_=meets_b, axis=AX.X, op=ALU.min))
            step(v.tensor_reduce(out=range_f[:, 1, :], in_=meets_c, axis=AX.X, op=ALU.max))
            step(v.tensor_scalar(range_f[:, 0, :], range_f[:, 0, :], float(ER), float(ER - 1), ALU.add, ALU.min))
            step(v.tensor_tensor(range_f[:, 1, :], range_f[:, 1, :], range_f[:, 0, :], ALU.subtract))
            step(v.tensor_scalar(range_f[:, 1, :], range_f[:, 1, :], 1.0, None, ALU.max))
            step(v.memset(ones_row[:], 1.0))
            step(v.tensor_tensor_scan(range_f[:, 2, :], ones_row[:], range_f[:, 1, :], 0.0, ALU.mult, ALU.add))
            step(v.tensor_tensor(range_f[:, 2, :], range_f[:, 2, :], range_f[:, 1, :], ALU.subtract))
            v.tensor_copy(range_i[:], range_f[:]).then_inc(ranges_ready, 1)
            dve.wait_ge(ranges_ready, 1)
            dve.wait_ge(cols_ready, 1)

            def one_hots(t):
                first = dve.value_load(range_i[0:1, 0, bass.ds(t, 1)], min_val=0, max_val=ER - 1)
                count = dve.value_load(range_i[0:1, 1, bass.ds(t, 1)], min_val=1, max_val=ER)
                before = dve.value_load(range_i[0:1, 2, bass.ds(t, 1)], min_val=0, max_val=ER * NT)
                with dve.Fori(0, count) as j:
                    for h in range(RUN):
                        dve.wait_ge(hot_free, (before + j) * RUN + (h + 1))
                        at = bass.ds(first + j, 1)
                        v.tensor_scalar(src_hot[:, h, :], node_no[:], edge_col[:, 0, h, at], None, ALU.is_equal)
                        v.tensor_scalar(dst_hot[:, h, :], node_no[:, bass.ds(t * T, T)], edge_col[:, 1, h, at],
                                        None, ALU.is_equal).then_inc(hot_ready, 1)

            def mask(t):
                dve.wait_ge(row_staged, t + 1)
                v.tensor_scalar(G[:, bass.ds(t, 1), :], count_row[:].rearrange("p (o n) -> p o n", o=1),
                                0.0, NO_EDGE, ALU.is_equal, ALU.mult).then_inc(mask_done, 1)

            with dve.Fori(0, NB) as b:
                for g in range(3):
                    dve.wait_ge(xhi_done, b * 3 + (g + 1))
                    v.tensor_tensor(xT_lo[:, 2 * g:2 * g + 2, :],
                                    p_x[:, g % 2, 0:2 * BT].rearrange("p (k n) -> p k n", k=2),
                                    xT_hi[:, 2 * g:2 * g + 2, :].bitcast(F32), ALU.subtract).then_inc(xlo_done, 1)
                one_hots(b * 2)
                mask(b * 2)
                for g in range(3):
                    dve.wait_ge(x1_hi_done, b * 3 + (g + 1))
                    at = bass.ds(b * BT, BT)
                    v.tensor_tensor(x1T[1][:, 2 * g:2 * g + 2, at],
                                    x1_f[:, g % 2, :].rearrange("p (k n) -> p k n", k=2),
                                    x1T[0][:, 2 * g:2 * g + 2, at].bitcast(F32), ALU.subtract).then_inc(x1_lo_done, 1)
                one_hots(b * 2 + 1)
                mask(b * 2 + 1)

        @block.scalar
        def _(act):
            nc.scalar.sem_inc(x1_lo_done, 1)
            nc.scalar.sem_inc(mask_done, 1)

            act.wait_ge(bias_in, 16)

            def stage_row(t):
                act.wait_ge(counted, t + 1)
                act.wait_ge(mask_done, t + 1)
                act.wait_ge(row_turned, t * 3 + 1)
                for i, (a, w) in enumerate(CH):
                    last = nc.scalar.activation(count_row[:, a:a + w], p_count[:, i, 0:w], ACT.Copy)
                last.then_inc(row_staged, 1)

            def keep_turned(t):
                for i in range(3):
                    k = 4 if i < 2 else 2
                    act.wait_ge(row_turned, t * 3 + (i + 2))
                    nc.scalar.activation(CT[:, 4 * i:4 * i + k, bass.ds(t * T, T)],
                                         p_turn[0:T, i, 0:k * T].rearrange("p (k q) -> p k q", q=T),
                                         ACT.Copy).then_inc(ct_done, 1)

            with act.Fori(0, NB) as b:
                for g in range(3):
                    act.wait_ge(x_turned, b * 3 + (g + 1))
                    nc.scalar.activation(xT_hi[:, 2 * g:2 * g + 2, :],
                                         p_x[:, g % 2, 0:2 * BT].rearrange("p (k n) -> p k n", k=2),
                                         ACT.Copy).then_inc(xhi_done, 1)
                stage_row(b * 2)
                for g in range(3):
                    act.wait_ge(x1_summed, b * 3 + (g + 1))
                    act.wait_ge(x1_lo_done, b * 3 + (g + 1))
                    for m in range(2):
                        last = nc.scalar.activation(x1_f[:, g % 2, m * BT:(m + 1) * BT], p_x[:, g % 2, m * BT:(m + 1) * BT],
                                                    ACT.Relu, bias=bias[:, 2 * g + m:2 * g + m + 1])
                    last.then_inc(x1_relu, 1)
                    act.wait_ge(x1_relu, b * 3 + (g + 1))
                    nc.scalar.activation(x1T[0][:, 2 * g:2 * g + 2, bass.ds(b * BT, BT)],
                                         x1_f[:, g % 2, :].rearrange("p (k n) -> p k n", k=2),
                                         ACT.Copy).then_inc(x1_hi_done, 1)
                keep_turned(b * 2)
                stage_row(b * 2 + 1)
                keep_turned(b * 2 + 1)

        @block.tensor
        def _(pe):
            pe.wait_ge(core.ident_ready, 2)
            pe.wait_ge(steps, 3)
            for a in range(2):
                for h in range(RUN):
                    nc.tensor.transpose(p_turn[0:T, 0, (RUN * a + h) * ER:(RUN * a + h + 1) * ER],
                                        edge_f[:, a, h * T:h * T + T], ident[0:ER, 0:ER])
            for a in range(2):
                last = nc.tensor.transpose(p_turn[:, 1, a * ER:(a + 1) * ER],
                                           dst_ends[:, a:a + 1].broadcast_to([ER, 128]), ident[0:ER, 0:ER])
            last.then_inc(edges_turned, 1)
            nc.tensor.sem_inc(hot_free, RUN)
            nc.tensor.sem_inc(row_turned, 1)
            nc.tensor.sem_inc(xlo_done, 2)
            pe.wait_ge(consts, 8)
            pe.wait_ge(ranges_ready, 1)
            nc.tensor.sem_inc(ct_done, 1)

            def count(t):
                count_ = pe.value_load(range_i[0:1, 1, bass.ds(t, 1)], min_val=1, max_val=ER)
                before = pe.value_load(range_i[0:1, 2, bass.ds(t, 1)], min_val=0, max_val=ER * NT)
                for i, (a, w) in enumerate(CH):
                    nc.tensor.matmul(p_count[:, i, 0:w], ident_b[:], band[:, bass.ds(t * -T + (N - T + a), w)],
                                     start=True, stop=False, skip_group_check=True)
                with pe.Fori(0, count_) as j:
                    for h in range(RUN):
                        pe.wait_ge(hot_ready, (before + j) * RUN + (h + 1))
                        for i, (a, w) in enumerate(CH):
                            last = nc.tensor.matmul(p_count[:, i, 0:w], dst_hot[:, h, :], src_hot[:, h, a:a + w],
                                                    start=False, stop=False, skip_group_check=True)
                        last.then_inc(hot_free, 1)
                nc.tensor.matmul(p_count[:, 0, 0:2], zeros_b[:], src_hot[:, 0, 0:2], start=False, stop=True,
                                 skip_group_check=True).then_inc(counted, 1)

            def turn_row(t):
                pe.wait_ge(row_staged, t + 1)
                pe.wait_ge(ct_done, t * 3 + 1)
                for i in range(3):
                    for k in range(4 if i < 2 else 2):
                        q = 4 * i + k
                        last = nc.tensor.transpose(p_turn[0:T, i, k * T:k * T + T], count_row[:, q * T:q * T + T],
                                                   ident[0:T, 0:T])
                    last.then_inc(row_turned, 1)

            for b in range(NB):
                pe.wait_ge(x_loaded, 16 * (b + 1))
                for g in range(3):
                    if g == 2:
                        pe.wait_ge(xlo_done, 3 * b + 3)
                    elif b:
                        pe.wait_ge(x1_relu, 3 * b)
                    for k in (2 * g, 2 * g + 1):
                        for i in range(2):
                            last = nc.tensor.transpose(p_x[:, g % 2, (k % 2) * BT + i * T:(k % 2) * BT + (i + 1) * T],
                                                       x_in[:, i, k * 128:(k + 1) * 128], ident[0:T, 0:T])
                    last.then_inc(x_turned, 1)
                count(2 * b)
                turn_row(2 * b)
                pe.wait_ge(xlo_done, 3 * b + 5)
                if b == 0:
                    pe.wait_ge(w_split, 2 * KD)
                for g in range(3):
                    if g == 2:
                        pe.wait_ge(x1_relu, 3 * b + 1)
                    for m in range(2):
                        for k in range(KD):
                            for n, (wp, xp) in enumerate(((w_hi, xT_hi), (w_hi, xT_lo), (w_lo, xT_hi))):
                                last = nc.tensor.matmul(p_x[:, g % 2, m * BT:(m + 1) * BT],
                                                        wp[:, k, (2 * g + m) * 128:(2 * g + m + 1) * 128], xp[:, k, :],
                                                        start=(m == 0 and k == 0 and n == 0),
                                                        stop=(k == KD - 1 and n == 2), skip_group_check=True)
                    last.then_inc(x1_summed, 1)
                count(2 * b + 1)
                turn_row(2 * b + 1)


class WeightsByA:

    def __init__(self, nc, sb, sem, w, a_vec, wa, units, at_once=1, name="by_a"):
        self.nc, self.w, self.a_vec, self.wa = nc, w, a_vec, wa
        self.units, self.groups, self.width = units, w.shape[0] // units, w.shape[2]
        self.chunks = w.shape[1] // 128
        self.heads = wa.shape[3] // self.groups
        self.at_once = at_once
        self.w_in = sb(f"{name}_w", [128, 2, at_once, units, self.width], F32)
        self.a_in = sb(f"{name}_a", [128, units, 2, self.width], F32)
        self.prod = sb(f"{name}_prod", [128, 2, units, self.width], F32)
        self.group = sb(f"{name}_group", [128, self.chunks, 2, self.heads], F32)
        self.a_loaded = sem(f"{name}_a_loaded")
        self.w_loaded = [sem(f"{name}_w_loaded{i}") for i in range(2)]
        self.multiplied = sem(f"{name}_multiplied")
        self.summed = sem(f"{name}_summed")
        self.kept = sem(f"{name}_kept")

    def program(self, pool):
        width, heads, units, at_once = self.width, self.heads, self.units, self.at_once
        loads = self.chunks // at_once

        HALVES, left = [], units * width // heads
        while left > 1:
            size = left // 2 if left % 2 == 0 else 1
            HALVES.append((left - size, size))
            left -= size

        def load(g, n):
            rows = self.w[bass.ds(g * units, units), n * at_once * 128:(n + 1) * at_once * 128, :]
            pool.dma_start(self.w_in[:, n % 2].rearrange("p k u c -> p (k u) c"),
                           rows.rearrange("u (k p) c -> p (u k) c", p=128) if units == 1 else rows.rearrange("u p c -> p u c")
                           ).then_inc(self.w_loaded[n % 2], 16)

        def group(g):
            pool.dma_start(self.a_in[:].rearrange("p u a c -> p (u a c)"),
                           self.a_vec[bass.ds(g * units, units)].rearrange("(o u) a c -> o (u a c)", o=1)
                           .broadcast_to([128, 2 * units * width])).then_inc(self.a_loaded, 16)
            load(g, 0)
            load(g, 1)
            wait_apart(pool, self.a_loaded, g * 16 + 16)
            for k in range(self.chunks):
                n, j = divmod(k, at_once)
                if j == 0:
                    wait_apart(pool, self.w_loaded[n % 2], g * (loads * 8) + (n // 2 + 1) * 16)
                for kind in range(2):
                    last = pool.tensor_tensor(self.prod[:, kind, :, :], self.w_in[:, n % 2, j, :, :], self.a_in[:, :, kind, :], ALU.mult)
                last.then_inc(self.multiplied, 1)
                wait_apart(pool, self.multiplied, g * self.chunks + (k + 1))
                if j == at_once - 1 and n + 2 < loads:
                    load(g, n + 2)
                p = self.prod[:].rearrange("p a u c -> p a (u c)").rearrange("p a (h c) -> p a h c", h=heads)
                for step, (other, size) in enumerate(HALVES):
                    out = self.group[:, k, :, :].rearrange("p a (h o) -> p a h o", o=1) if step == len(HALVES) - 1 else p[:, :, :, 0:size]
                    pool.tensor_tensor(out, p[:, :, :, 0:size], p[:, :, :, other:other + size], ALU.add).then_inc(self.summed, 1)
                    wait_apart(pool, self.summed, g * (self.chunks * len(HALVES)) + (k * len(HALVES) + step + 1))
            pool.tensor_copy(self.wa[:, :, :, bass.ds(g * heads, heads)], self.group[:]).then_inc(self.kept, 1)
            wait_apart(pool, self.kept, g + 1)

        return group


def project(nc, core, xT, w, wa, h_rows, score_rows, width, col_src, u_col, v_col):
    iters = w.shape[0] // 2
    heads = wa.shape[3]
    per = heads // (2 * iters) or 1
    cw = width // per
    hw = h_rows.shape[2]
    R = 2 * heads
    HG = 4
    GROUPS = heads // HG
    CH = [(0, 418), (418, 416), (834, 416)]
    ident, G = core.ident, core.G
    with ExitStack() as ctx:
        sb, pb, sem = core.tools(ctx)
        w_raw = sb("pw_raw", [128, 2, KD, width], F32)
        w_hi = sb("pw_hi", [128, 2, KD, width], F32R)
        w_lo = sb("pw_lo", [128, 2, KD, width], F32R)
        wa_hi = sb("wa_hi", [128, KD, R], F32R)
        wa_lo = sb("wa_lo", [128, KD, R], F32R)
        rows = sb("score_rows_in", [R, N], F32)
        junk = sb("max_junk", [T, 2, N], BF16)
        h_out = sb("h_out", [T, 2, NH, per, hw], F32)
        score = sb("score", [T, 2, heads, NT], F32)
        dst_now = sb("dst_now", [T, HG, NT], F32)
        src_row = sb("src_row", [T, 2, N], F32)
        most = sb("most", [T, HG, NT], F32)
        tmp = sb("tmp", [T, HG, NT], F32)
        tmp2 = sb("tmp2", [T, HG, NT], F32)
        turned_uv = src_row[0:heads * NT, 0, 0:2 * T].rearrange("p (a q) -> p a q", a=2)
        p_h = pb("p_h", [T, 4, 512])
        p_r = pb("p_r", [R, 3, 512])
        p_s = pb("p_s", [128, 512])

        w_in = [sem(f"pw_in{u}") for u in range(2)]
        wa_hi_done = sem("wa_hi_done")
        wa_split = sem("wa_split")
        rows_summed = sem("rows_summed")
        rows_kept = sem("rows_kept")
        rows_stored = sem("rows_stored")
        rows_turned = sem("rows_turned")
        score_kept = sem("score_kept")
        max_steps = sem("max_steps")
        maxed = sem("maxed")
        hi_done = sem("hi_done")
        split_done = sem("split_done")
        h_summed = sem("h_summed")
        h_kept = sem("h_kept")
        h_stored = [sem(f"h_stored{u}") for u in range(2)]
        ones_set = sem("ones_set")
        row_in = [sem(f"row_in{u}") for u in range(2)]
        uv_done = sem("uv_done")
        uv_turned = sem("uv_turned")
        uv_kept = sem("uv_kept")
        uv_stored = sem("uv_stored")

        block = ctx.enter_context(nc.Block())

        @block.sync
        def _(sp):
            def load_w(i):
                for u in range(2):
                    q = i * 2 + u
                    wait_apart(sp, split_done, q + 1)
                    sp.dma_start(w_raw[:, u, :, :], w[bass.ds(q, 1)].rearrange("o (k p) c -> p (o k) c", p=128)).then_inc(w_in[u], 16)

            def store(i, heads_to_load):
                for u in range(2):
                    for part_no in range(2):
                        wait_apart(sp, h_kept, i * (2 * NT) + (NT * u + NH * (part_no + 1) + 4))
                        for g in range(per):
                            to = h_rows[bass.ds(i * (2 * per) + (u * per + g), 1), part_no * DH:(part_no + 1) * DH, :]
                            sp.dma_start(to.rearrange("o (t p) c -> p (o t) c", p=T),
                                         h_out[:, part_no, :, g, :]).then_inc(h_stored[part_no], 16)
                        j = 2 * u + part_no
                        if j < heads_to_load:
                            wait_apart(sp, maxed, i * (HG * NT) + ((j + 1) * NT + 2))
                            sp.dma_start(src_row[:, j % 2, :],
                                         score_rows[bass.ds(i * HG + (j + 2), 1), :].broadcast_to([T, N])).then_inc(row_in[j % 2], 16)

            load_w(0)
            if GROUPS > 1:
                with sp.Fori(0, iters - 1) as i:
                    load_w(i + 1)
                    store(i, HG)
                store(iters - 1, HG - 2)
            else:
                load_w(1)
                store(0, HG - 2)
                with sp.Fori(0, iters - 2) as i:
                    load_w(i + 2)
                    store(i + 1, 0)
                store(iters - 1, 0)
            for u in range(2):
                sp.wait_ge(h_stored[u], 16 * per * (2 * iters + 1))
            for kind in range(2):
                sp.wait_ge(uv_kept, kind + 1)
                sp.dma_start(core.uv_rows[kind, 0:heads * NT, :], turned_uv[:, kind, :]).then_inc(uv_stored, 16)
            sp.wait_ge(uv_stored, 32)

        @block.gpsimd
        def _(pool):
            pool.sem_inc(split_done, 2)
            if hw > cw:
                pool.memset(h_out[:, :, :, :, cw:], 0.0).then_inc(ones_set, 1)
                pool.wait_ge(ones_set, 1)
                pool.memset(h_out[:, :, :, :, cw:cw + 1], 1.0).then_inc(ones_set, 1)
            with pool.Fori(0, iters) as i:
                for u in range(2):
                    pool.wait_ge(w_in[u], i * 16 + 16)
                    wait_apart(pool, h_summed, i * (2 * NT) + (u + 1) * NT)
                    pool.tensor_copy(w_hi[:, u, :, :], w_raw[:, u, :, :]).then_inc(hi_done, 1)
                    pool.wait_ge(hi_done, i * 2 + (u + 1))
                    pool.tensor_tensor(w_lo[:, u, :, :], w_raw[:, u, :, :],
                                       w_hi[:, u, :, :].bitcast(F32), ALU.subtract).then_inc(split_done, 1)

        @block.vector
        def _(dve):
            v = nc.vector
            v.sem_inc(maxed, 2)
            wa_flat = wa[:].rearrange("p k a h -> p k (a h)")
            v.tensor_copy(wa_hi[:], wa_flat).then_inc(wa_hi_done, 1)
            dve.wait_ge(wa_hi_done, 1)
            v.tensor_tensor(wa_lo[:], wa_flat, wa_hi[:].bitcast(F32), ALU.subtract).then_inc(wa_split, 1)
            dve.wait_ge(rows_turned, 1)
            v.tensor_copy(score[:], p_s[0:T, 0:NT * R].rearrange("p (t a h) -> p a h t", t=NT, a=2)).then_inc(score_kept, 1)
            dve.wait_ge(score_kept, 1)
            v.tensor_copy(col_src[0][:, 0:heads, :], score[:, 0])
            v.tensor_scalar(col_src[1][:, 0:heads, :], score[:, 0], SLOPE, None, ALU.mult)

            def maxima(q):
                for h in range(HG):
                    wait_apart(dve, row_in[h % 2], q * 32 + 16 * (h // 2 + 1))
                    for t in range(NT):
                        wait_apart(dve, maxed, q * (HG * NT) + (h * NT + t + 1))
                        v.tensor_tensor_reduce(out=junk[:, t % 2, :], in0=src_row[:, h % 2, :], in1=G[:, t, :], scale=1.0,
                                               scalar=NO_EDGE, op0=ALU.add, op1=ALU.max,
                                               accum_out=most[:, h, t:t + 1]).then_inc(maxed, 1)
                hs = bass.ds(q * HG, HG)
                v.tensor_copy(dst_now[:], score[:, 1, hs, :]).then_inc(max_steps, 1)
                dve.wait_ge(max_steps, q * 4 + 1)
                dve.wait_ge(maxed, q * (HG * NT) + (HG * NT + 2))
                v.tensor_tensor(tmp[:], most[:], dst_now[:], ALU.add).then_inc(max_steps, 1)
                dve.wait_ge(max_steps, q * 4 + 2)
                v.scalar_tensor_tensor(tmp2[:], tmp[:], SLOPE, tmp[:], ALU.mult, ALU.max).then_inc(max_steps, 1)
                dve.wait_ge(max_steps, q * 4 + 3)
                v.tensor_tensor(u_col[:, hs, :], dst_now[:], tmp2[:], ALU.subtract)
                v.scalar_tensor_tensor(v_col[:, hs, :], dst_now[:], SLOPE, tmp2[:], ALU.mult, ALU.subtract).then_inc(max_steps, 1)
                dve.wait_ge(max_steps, q * 4 + 4)

            with dve.Fori(0, GROUPS) as q:
                maxima(q)
            v.sem_inc(uv_done, 1)

        @block.scalar
        def _(act):
            a = nc.scalar
            a.sem_inc(h_kept, 4)
            for u in range(2):
                a.sem_inc(h_stored[u], 16 * per)
            act.wait_ge(rows_summed, 1)
            for b, (at, n) in enumerate(CH):
                last = a.activation(rows[:, at:at + n], p_r[:, b, 0:n], ACT.Copy)
            last.then_inc(rows_kept, 1)
            act.wait_ge(rows_kept, 1)
            act.dma_start(score_rows[0:R, :], rows[:]).then_inc(rows_stored, 16)
            act.wait_ge(rows_stored, 16)
            for h in range(2):
                act.dma_start(src_row[:, h, :], score_rows[h:h + 1, :].broadcast_to([T, N])).then_inc(row_in[h], 16)
            if hw > cw:
                act.wait_ge(ones_set, 2)
            with act.Fori(0, iters) as i:
                for u in range(2):
                    for t in range(NT):
                        if t % NH == 0:
                            act.wait_ge(h_stored[t // NH], i * (32 * per) + 16 * per * (u + 1))
                        act.wait_ge(h_summed, i * (2 * NT) + (2 * NT + u * NT + t + 1))
                        a.activation(h_out[:, t // NH, t % NH, :, 0:cw],
                                     p_h[:, (u * NT + t) % 4, 0:width].rearrange("p (g c) -> p g c", g=per),
                                     ACT.Copy).then_inc(h_kept, 1)
            for kind in range(2):
                act.wait_ge(uv_turned, kind + 1)
                a.activation(turned_uv[:, kind, :], p_s[0:heads * NT, 0:T], ACT.Copy).then_inc(uv_kept, 1)

        @block.tensor
        def _(pe):
            nc.tensor.sem_inc(h_summed, 2 * NT)
            pe.wait_ge(wa_split, 1)
            for b, (at, n) in enumerate(CH):
                for k in range(KD):
                    for j, (wp, xp) in enumerate(((wa_hi, xT[0]), (wa_hi, xT[1]), (wa_lo, xT[0]))):
                        last = nc.tensor.matmul(p_r[:, b, 0:n], wp[:, k, :], xp[:, k, at:at + n],
                                                start=(k == 0 and j == 0), stop=(k == KD - 1 and j == 2))
            last.then_inc(rows_summed, 1)
            pe.wait_ge(rows_kept, 1)
            for t in range(NT):
                last = nc.tensor.transpose(p_s[0:T, t * R:(t + 1) * R], rows[:, t * T:(t + 1) * T], ident[0:R, 0:R])
            last.then_inc(rows_turned, 1)
            with pe.Fori(0, iters) as i:
                for u in range(2):
                    pe.wait_ge(split_done, i * 2 + (u + 3))
                    for t in range(NT):
                        pe.wait_ge(h_kept, i * (2 * NT) + (u * NT + t + 1))
                        at = slice(t * T, (t + 1) * T)
                        for k in range(KD):
                            for n, (xp, wp) in enumerate(((xT[0], w_hi), (xT[0], w_lo), (xT[1], w_hi))):
                                last = nc.tensor.matmul(p_h[:, (u * NT + t) % 4, 0:width], xp[:, k, at], wp[:, u, k, :],
                                                        start=(k == 0 and n == 0), stop=(k == KD - 1 and n == 2))
                        last.then_inc(h_summed, 1)
            pe.wait_ge(uv_done, 1)
            for kind, col in enumerate((u_col, v_col)):
                if kind:
                    pe.wait_ge(uv_kept, kind)
                nc.tensor.transpose(p_s[0:heads * NT, 0:T], col[:, 0:heads, :].rearrange("p h t -> p (h t)"),
                                    ident[0:T, 0:T]).then_inc(uv_turned, 1)


def aggregate_layer0(nc, core, h_rows, col_src, bias, turned_rows, w1, a1, w2, a2):
    ident, CT = core.ident, core.CT
    ITERS = CONVS * H0 // 2
    STEPS = 2 * NT
    BANKS = 5
    CW = PAIR // 128
    RING = 4
    with ExitStack() as ctx:
        sb, pb, sem = core.tools(ctx)
        uv = sb("uv", [T, 2, 2, N], F32)
        h_in = sb("h_in", [T, 2, NT, HC0], F32)
        e = sb("e", [T, RING, 2, N], F32)
        p = sb("p", [T, RING, N], F32)
        res = sb("res", [T, NT, PAIR], F32)
        sums = sb("sums", [T, 2, NT], F32)
        b_col = sb("b_col", [128, ITERS, CW], F32)
        out_f = sb("out_f", [128, CW, N], F32)
        p_o = pb("p_o", [T, BANKS, 512])
        p_t = pb("p_t", [128, 3, 512])

        uv_in = [sem(f"uv_in{i}") for i in range(2)]
        h_loaded = [sem(f"h_loaded{i}") for i in range(2)]
        bias_in = sem("bias_in")
        exp_ready = sem("exp_ready")
        more_ready = sem("more_ready")
        p_ready = sem("p_ready")
        p_used = sem("p_used")
        sum_steps = sem("sum_steps")
        bank_free = sem("bank_free")
        turned = sem("turned")
        out_ready = sem("out_ready")
        stored = [sem(f"stored{i}") for i in range(CW)]
        all_by_a = (WeightsByA(nc, sb, sem, w1, a1, core.wa1, 2, 1, "by_a1"),
                    WeightsByA(nc, sb, sem, w2, a2, core.wa2, 1, 4, "by_a2"))

        block = ctx.enter_context(nc.Block())

        @block.gpsimd
        def _(pool):
            for by_a in all_by_a:
                by_a_group = by_a.program(pool)
                with pool.Fori(0, by_a.groups) as g:
                    by_a_group(g)

        def every_iteration(eng, body):
            body(0, True)
            with eng.Fori(0, ITERS - 1) as i:
                body(i + 1, False)

        @block.sync
        def _(sp):
            sp.dma_start(b_col[:], bias).then_inc(bias_in, 16)

            def load(i):
                for s in range(2):
                    wait_apart(sp, exp_ready, i * STEPS + (s + 1) * NT)
                    wait_apart(sp, p_used, i * STEPS + (s + 1) * NT)
                    head = i * 2 + s
                    for kind in range(2):
                        sp.dma_start(uv[:, s, kind, :],
                                     core.uv_rows[kind, bass.ds(head * NT, NT), :].rearrange("(o t) p -> o (t p)", o=1)
                                     .broadcast_to([T, N])).then_inc(uv_in[s], 16)
                    for q in range(2):
                        sp.dma_start(h_in[:, s, q * NH:(q + 1) * NH],
                                     h_rows[bass.ds(head, 1), q * DH:(q + 1) * DH, :].rearrange("o (t p) c -> p (o t) c", p=T)
                                     ).then_inc(h_loaded[s], 16)

            def store(i):
                for c in range(CW):
                    wait_apart(sp, out_ready, i * CW + (c + 1))
                    sp.dma_start(turned_rows[bass.ds(i * CW + c, 1), :, :].rearrange("o p n -> p (o n)"),
                                 out_f[:, c, :]).then_inc(stored[c], 16)

            load(0)
            load(1)
            with sp.Fori(0, ITERS - 2) as i:
                store(i)
                load(i + 2)
            store(ITERS - 2)
            store(ITERS - 1)
            for c in range(CW):
                sp.wait_ge(stored[c], 16 * (1 + ITERS))

        @block.scalar
        def _(act):
            a = nc.scalar
            for c in range(CW):
                a.sem_inc(stored[c], 16)
            a.sem_inc(bank_free, BANKS)
            act.wait_ge(bias_in, 16)

            def leave_head(i, hh):
                act.wait_ge(sum_steps, i * 4 + (2 * hh + 2))
                act.wait_ge(turned, i * CW + CW)
                for d in range(NT):
                    last = a.activation(res[:, d, hh * C0:(hh + 1) * C0], p_o[:, d // 2, (d % 2) * 256:(d % 2) * 256 + C0],
                                        ACT.Copy, scale=sums[:, 1, d:d + 1])
                    if d % 2:
                        last.then_inc(bank_free, 1)

            def keep(i, c):
                act.wait_ge(turned, i * CW + (c + 1 + CW))
                wait_apart(act, stored[c], i * 16 + 16)
                for b, k in ((0, 4), (1, 4), (2, 2)):
                    last = a.activation(out_f[:, c, 4 * b * T:(4 * b + k) * T], p_t[:, b, 0:k * T], ACT.Relu,
                                        bias=b_col[:, bass.ds(i, 1), c])
                last.then_inc(out_ready, 1)

            def body(i, first):
                for g in range(STEPS):
                    hh, s = divmod(g, NT)
                    if s == 0:
                        wait_apart(act, uv_in[hh], i * 32 + 32)
                    wait_apart(act, p_ready, i * STEPS + (g + 1))
                    for kind in range(2):
                        last = a.activation(e[:, g % RING, kind, :], uv[:, hh, kind, :], ACT.Exp,
                                            bias=col_src[kind][:, bass.ds(i * 2 + hh, 1), s])
                    last.then_inc(exp_ready, 1)
                    if g == NT + 3:
                        leave_head(i, 0)
                    if g == 3 and not first:
                        leave_head(i - 1, 1)
                    if g in (5, 7, 9) and not first:
                        keep(i - 1, (g - 5) // 2)

            every_iteration(act, body)
            leave_head(ITERS - 1, 1)
            for c in range(CW):
                keep(ITERS - 1, c)

        @block.vector
        def _(dve):
            v = nc.vector
            v.sem_inc(p_ready, RING)
            v.sem_inc(exp_ready, 2 * NT)

            def divisors(i, hh):
                dve.wait_ge(p_used, i * STEPS + ((hh + 1) * NT + 2 * NT))
                v.tensor_scalar(sums[:, 0, :].rearrange("p (b n) -> p b n", n=2),
                                p_o[:, :, :].rearrange("p b (n c) -> p b n c", n=2)[:, :, :, C0],
                                1e-16, None, ALU.add).then_inc(sum_steps, 1)
                dve.wait_ge(sum_steps, i * 4 + (2 * hh + 1))
                v.reciprocal(sums[:, 1, :], sums[:, 0, :]).then_inc(sum_steps, 1)

            def body(i, first):
                for g in range(STEPS):
                    hh, s = divmod(g, NT)
                    dve.wait_ge(exp_ready, i * STEPS + (g + 1 + 2 * NT))
                    v.tensor_tensor(e[:, g % RING, 0, :], e[:, g % RING, 0, :], e[:, g % RING, 1, :], ALU.max).then_inc(more_ready, 1)
                    dve.wait_ge(more_ready, i * STEPS + (g + 1))
                    dve.wait_ge(p_used, i * STEPS + (g + 1 + 2 * NT - RING))
                    v.scalar_tensor_tensor(p[:, g % RING, :], e[:, g % RING, 0, :], 1.0, CT[:, s, :],
                                           ALU.min, ALU.mult).then_inc(p_ready, 1)
                    if g == NT + 2:
                        divisors(i, 0)
                    if g == 2 and not first:
                        divisors(i - 1, 1)

            every_iteration(dve, body)
            divisors(ITERS - 1, 1)

        @block.tensor
        def _(pe):
            nc.tensor.sem_inc(p_used, 2 * NT)
            nc.tensor.sem_inc(turned, CW)

            def turn(i, c):
                if c:
                    pe.wait_ge(out_ready, i * CW + c)
                else:
                    pe.wait_ge(bank_free, i * (2 * BANKS) + 3 * BANKS)
                for d in range(NT):
                    last = nc.tensor.transpose(p_t[:, d // 4, (d % 4) * T:(d % 4 + 1) * T],
                                               res[:, d, c * 128:(c + 1) * 128], ident[0:T, 0:T])
                last.then_inc(turned, 1)

            def body(i, first):
                for g in range(STEPS):
                    hh, s = divmod(g, NT)
                    if s == 0:
                        pe.wait_ge(h_loaded[hh], i * 32 + 32)
                    pe.wait_ge(p_ready, i * STEPS + (g + 1 + RING))
                    for d in range(NT):
                        b, n = divmod(d, 2)
                        if s == 0 and n == 0:
                            pe.wait_ge(bank_free, i * (2 * BANKS) + (BANKS * hh + b + 1))
                        last = nc.tensor.matmul(p_o[:, b, n * 256:n * 256 + C0 + 1], p[:, g % RING, d * T:(d + 1) * T],
                                                h_in[:, hh, s, 0:C0 + 1], start=(s == 0 and n == 0), stop=(s == NT - 1),
                                                skip_group_check=True)
                    last.then_inc(p_used, 1)
                    if g in (1, 3, 5) and not first:
                        turn(i - 1, (g - 1) // 2)

            every_iteration(pe, body)
            for c in range(CW):
                turn(ITERS - 1, c)


def aggregate_layer1(nc, core, h_rows, col_src, bias, turned_rows):
    ident, CT = core.ident, core.CT
    STEPS = 2 * NT
    BANKS = NH
    CW = C1 // 128
    ROW = (NH - 1) * T
    RING = 4
    with ExitStack() as ctx:
        sb, pb, sem = core.tools(ctx)
        uv = sb("uv", [T, 2, 2, DH], F32)
        h_raw = sb("h_raw", [T, NT, C1], F32)
        h_hi = sb("h_hi", [T, NT, C1], F32R)
        h_lo = sb("h_lo", [T, NT, C1], F32R)
        e = sb("e", [T, RING, 2, DH], F32)
        p_hi = sb("p_hi", [T, RING, DH], F32R)
        p_lo = sb("p_lo", [T, RING, DH], F32R)
        ones_f = sb("ones_f", [T, 128], F32)
        ones = sb("ones", [T, 128], F32R)
        res = sb("res", [T, NH, C1], F32)
        sum_row = sb("sum_row", [1, ROW], F32)
        sums = sb("sums", [T, 2, NH + 1], F32)
        b_col = sb("b_col", [128, H1, CW], F32)
        z = sb("z", [128, 2, 3, DH], F32)
        out_f = sb("out_f", [128, 2, DH], F32)
        p_o = pb("p_o", [T, BANKS, 512])
        p_sum = pb("p_sum", [128, 512])
        p_t = pb("p_t", [128, 2, 512])

        uv_in = [sem(f"uv_in{i}") for i in range(2)]
        h_loaded = [sem(f"h_loaded{i}") for i in range(2)]
        bias_in = sem("bias_in")
        ones_set = sem("ones_set")
        h_hi_done = sem("h_hi_done")
        h_split = sem("h_split")
        exp_ready = sem("exp_ready")
        more_ready = sem("more_ready")
        p_ready = sem("p_ready")
        p_hi_ready = sem("p_hi_ready")
        p_split = sem("p_split")
        p_used = sem("p_used")
        sum_steps = sem("sum_steps")
        sums_turned = sem("sums_turned")
        divided = sem("divided")
        bank_free = sem("bank_free")
        turned = sem("turned")
        kept = sem("kept")
        elu_low = sem("elu_low")
        elu_up = sem("elu_up")
        elu_exped = sem("elu_exped")
        out_ready = sem("out_ready")
        stored = [sem(f"stored{i}") for i in range(2)]

        block = ctx.enter_context(nc.Block())

        def chunk_of(i, part, back, c):
            return i * (2 * CW) + ((part - back) * CW + c)

        def every_iteration(eng, body):
            body(0, True)
            with eng.Fori(0, H1 - 1) as i:
                body(i + 1, False)

        @block.sync
        def _(sp):
            sp.dma_start(b_col[:], bias).then_inc(bias_in, 16)

            def load_uv(i, part):
                wait_apart(sp, exp_ready, i * STEPS + (part + 1) * NT)
                for kind in range(2):
                    sp.dma_start(uv[:, part, kind, :],
                                 core.uv_rows[kind, bass.ds(i * NT + part * NH, NH), :].rearrange("(o t) p -> o (t p)", o=1)
                                 .broadcast_to([T, DH])).then_inc(uv_in[part], 16)

            def load_h(i):
                wait_apart(sp, h_split, i * NT + NT)
                for part in range(2):
                    for q in range(2):
                        sp.dma_start(h_raw[:, part * NH:(part + 1) * NH, q * HALF1:(q + 1) * HALF1],
                                     h_rows[bass.ds(i * 2 + q, 1), part * DH:(part + 1) * DH, :].rearrange("o (t p) c -> p (o t) c", p=T)
                                     ).then_inc(h_loaded[part], 16)

            def store(i, part, back, c):
                wait_apart(sp, out_ready, chunk_of(i, part, back, c) + 3)
                head, half = i + (part - back) // 2, (part - back) % 2
                sp.dma_start(turned_rows[bass.ds(head * CW + c, 1), :, half * DH:(half + 1) * DH].rearrange("o p n -> p (o n)"),
                             out_f[:, c % 2, :]).then_inc(stored[c % 2], 16)

            def stores(i, part, groups):
                if groups >= 2:
                    for c in range(1, CW):
                        store(i, part, 2, c)
                if groups >= 1:
                    store(i, part, 1, 0)

            load_uv(0, 0)
            load_h(0)
            load_uv(0, 1)
            load_h(1)
            load_uv(1, 0)
            stores(0, 1, 1)
            with sp.Fori(0, H1 - 2) as i:
                load_uv(i + 1, 1)
                load_h(i + 2)
                stores(i + 1, 0, 2)
                load_uv(i + 2, 0)
                stores(i + 1, 1, 2)
            load_uv(H1 - 1, 1)
            stores(H1 - 1, 0, 2)
            stores(H1 - 1, 1, 2)
            stores(H1, 0, 2)
            for c in range(1, CW):
                store(H1, 1, 2, c)
            for s in range(2):
                sp.wait_ge(stored[s], 16 * (1 + H1 * CW))

        @block.gpsimd
        def _(pool):
            pool.sem_inc(h_split, NT)

            def split(i, s):
                if s % NH == 0:
                    pool.wait_ge(h_loaded[s // NH], i * 32 + 32)
                wait_apart(pool, p_used, i * STEPS + (s + 1 + NT))
                pool.tensor_copy(h_hi[:, s, :], h_raw[:, s, :]).then_inc(h_hi_done, 1)
                pool.wait_ge(h_hi_done, i * NT + (s + 1))
                pool.tensor_tensor(h_lo[:, s, :], h_raw[:, s, :], h_hi[:, s, :].bitcast(F32), ALU.subtract).then_inc(h_split, 1)

            with pool.Fori(0, H1) as i:
                for s in range(NT):
                    split(i, s)

        @block.scalar
        def _(act):
            a = nc.scalar
            for s in range(2):
                a.sem_inc(stored[s], 16)
            a.sem_inc(bank_free, BANKS)
            act.wait_ge(ones_set, 1)
            a.activation(ones[:], ones_f[:], ACT.Copy).then_inc(ones_set, 1)
            act.wait_ge(bias_in, 16)

            def leave(i, part):
                act.wait_ge(p_used, i * STEPS + (part * NT + 2 * NT))
                act.wait_ge(turned, i * (2 * CW) + part * CW)
                for d in range(NH):
                    a.activation(res[:, d, :], p_o[:, d, :], ACT.Copy).then_inc(bank_free, 1)

            def keep(i, part, back, c):
                act.wait_ge(turned, chunk_of(i, part, back, c) + (1 + CW))
                wait_apart(act, out_ready, chunk_of(i, part, back, c) + 1)
                head = i + (part - back) // 2
                for b, k in ((0, 4), (1, 1)):
                    last = a.activation(z[:, c % 2, 0, 4 * b * T:(4 * b + k) * T], p_t[:, b, 0:k * T], ACT.Identity,
                                        bias=b_col[:, bass.ds(head, 1), c])
                last.then_inc(kept, 1)

            def elu_exp(i, part, back, c):
                act.wait_ge(elu_low, chunk_of(i, part, back, c) + 1)
                a.activation(z[:, c % 2, 1, :], z[:, c % 2, 1, :], ACT.Exp).then_inc(elu_exped, 1)

            def out_work(i, part, s, groups):
                if groups >= 2 and s in (1, 3):
                    keep(i, part, 2, (s + 3) // 2)
                if groups >= 2 and s in (1, 3, 5):
                    elu_exp(i, part, 2, (s + 1) // 2)
                if groups >= 1 and s == 4:
                    leave(i, part)
                if groups >= 1 and s in (7, 9):
                    keep(i, part, 1, (s - 7) // 2)
                if groups >= 1 and s == 9:
                    elu_exp(i, part, 1, 0)

            def round_p(i, g):
                act.wait_ge(p_ready, i * STEPS + (g + 1))
                wait_apart(act, p_used, i * STEPS + (g + 1 + 2 * NT - RING))
                a.activation(p_hi[:, g % RING, :], e[:, g % RING, 0, :], ACT.Copy).then_inc(p_hi_ready, 1)

            def body(i, first):
                for g in range(STEPS):
                    part, s = divmod(g, NT)
                    if s == 0:
                        wait_apart(act, uv_in[part], i * 32 + 32)
                    wait_apart(act, p_split, i * STEPS + (g + 1))
                    for kind in range(2):
                        last = a.activation(e[:, g % RING, kind, :], uv[:, part, kind, :], ACT.Exp,
                                            bias=col_src[kind][:, bass.ds(i, 1), s])
                    last.then_inc(exp_ready, 1)
                    if g >= 2 or not first:
                        round_p(i, g - 2)
                    out_work(i, part, s, part if first else 2)

            every_iteration(act, body)
            for g in (STEPS - 2, STEPS - 1):
                round_p(H1 - 1, g)
            for s in range(NT):
                out_work(H1, 0, s, 2)
            for c in (2, 3):
                keep(H1, 1, 2, c)
                elu_exp(H1, 1, 2, c - 1)
            elu_exp(H1, 1, 2, 3)

        @block.vector
        def _(dve):
            v = nc.vector
            v.sem_inc(p_split, RING)
            v.sem_inc(exp_ready, 2 * NT)
            v.sem_inc(out_ready, 2)
            v.memset(ones_f[:], 1.0).then_inc(ones_set, 1)

            def divisors(i, part):
                dve.wait_ge(p_used, i * STEPS + (part * NT + 2 * NT))
                v.tensor_copy(sum_row[:], p_sum[0:1, 0:ROW]).then_inc(sum_steps, 1)
                dve.wait_ge(sums_turned, i * 2 + part)
                v.tensor_scalar(sums[:, 0, :], p_sum[0:T, ROW:ROW + NH + 1], 1e-16, None, ALU.add).then_inc(sum_steps, 1)
                dve.wait_ge(sum_steps, i * 6 + (3 * part - 1))
                v.reciprocal(sums[:, 1, :], sums[:, 0, :]).then_inc(sum_steps, 1)

            def divide(i, part):
                dve.wait_ge(sum_steps, i * 6 + 3 * part)
                for d in range(NH):
                    dve.wait_ge(bank_free, i * (2 * BANKS) + (BANKS * part + d + 1))
                    at = 0 if d == NH - 1 else d + 2
                    last = v.tensor_scalar(res[:, d, :], res[:, d, :], sums[:, 1, at:at + 1], None, ALU.mult)
                last.then_inc(divided, 1)

            def low(i, part, back, c):
                dve.wait_ge(kept, chunk_of(i, part, back, c) + 1)
                v.tensor_scalar(z[:, c % 2, 1, :], z[:, c % 2, 0, :], 0.0, None, ALU.min).then_inc(elu_low, 1)
                v.tensor_scalar(z[:, c % 2, 2, :], z[:, c % 2, 0, :], 0.0, None, ALU.max).then_inc(elu_up, 1)

            def elu(i, part, back, c):
                dve.wait_ge(elu_up, chunk_of(i, part, back, c) + 1)
                dve.wait_ge(elu_exped, chunk_of(i, part, back, c) + 1)
                dve.wait_ge(stored[c % 2], i * (16 * CW) + ((part - back) * 2 + c // 2 + 1) * 16)
                v.scalar_tensor_tensor(out_f[:, c % 2, :], z[:, c % 2, 1, :], -1.0, z[:, c % 2, 2, :],
                                       ALU.add, ALU.add).then_inc(out_ready, 1)

            def out_work(i, part, s, groups):
                if groups >= 2 and s in (1, 3):
                    low(i, part, 2, (s + 3) // 2)
                if groups >= 2 and s in (1, 3, 5):
                    elu(i, part, 2, (s + 1) // 2)
                if groups >= 1 and s == 3:
                    divisors(i, part)
                if groups >= 1 and s == 5:
                    divide(i, part)
                if groups >= 1 and s in (7, 9):
                    low(i, part, 1, (s - 7) // 2)
                if groups >= 1 and s == 9:
                    elu(i, part, 1, 0)

            def rest_of_p(i, g):
                dve.wait_ge(p_hi_ready, i * STEPS + (g + 1))
                v.tensor_tensor(p_lo[:, g % RING, :], e[:, g % RING, 0, :], p_hi[:, g % RING, :].bitcast(F32),
                                ALU.subtract).then_inc(p_split, 1)

            def body(i, first):
                for g in range(STEPS):
                    part, s = divmod(g, NT)
                    dve.wait_ge(exp_ready, i * STEPS + (g + 1 + 2 * NT))
                    v.tensor_tensor(e[:, g % RING, 0, :], e[:, g % RING, 0, :], e[:, g % RING, 1, :], ALU.max).then_inc(more_ready, 1)
                    dve.wait_ge(more_ready, i * STEPS + (g + 1))
                    v.scalar_tensor_tensor(e[:, g % RING, 0, :], e[:, g % RING, 0, :], 1.0, CT[:, s, part * DH:(part + 1) * DH],
                                           ALU.min, ALU.mult).then_inc(p_ready, 1)
                    if g or not first:
                        rest_of_p(i, g - 1)
                    out_work(i, part, s, part if first else 2)

            every_iteration(dve, body)
            rest_of_p(H1 - 1, STEPS - 1)
            for s in range(NT):
                out_work(H1, 0, s, 2)
            for c in (2, 3):
                low(H1, 1, 2, c)
                elu(H1, 1, 2, c - 1)
            elu(H1, 1, 2, 3)

        @block.tensor
        def _(pe):
            nc.tensor.sem_inc(p_used, 2 * NT)
            nc.tensor.sem_inc(turned, CW)
            pe.wait_ge(ones_set, 2)

            def turn(i, part, c, first_ever=False):
                if c == 0:
                    pe.wait_ge(divided, i * 2 + part)
                if not first_ever:
                    pe.wait_ge(kept, chunk_of(i, part, 1, c))
                for d in range(NH):
                    last = nc.tensor.transpose(p_t[:, d // 4, (d % 4) * T:(d % 4 + 1) * T],
                                               res[:, d, c * 128:(c + 1) * 128], ident[0:T, 0:T])
                last.then_inc(turned, 1)

            def turn_sums(i, part):
                wait_apart(pe, sum_steps, i * 6 + (3 * part - 2))
                for d in range(NH - 1):
                    last = nc.tensor.transpose(p_sum[0:T, ROW + 2 + d:ROW + 3 + d], sum_row[:, d * T:(d + 1) * T],
                                               ident[0:1, 0:1])
                last.then_inc(sums_turned, 1)

            def body(i, first):
                for g in range(STEPS):
                    part, s = divmod(g, NT)
                    if part == 0:
                        pe.wait_ge(h_split, i * NT + (s + 1 + NT))
                    pe.wait_ge(p_split, i * STEPS + (g + 1 + RING))
                    for d in range(NH):
                        if s == 0:
                            pe.wait_ge(bank_free, i * (2 * BANKS) + (BANKS * part + d + 1))
                        cols = slice(d * T, (d + 1) * T)
                        begin = s == 0
                        for pp, moving in ((p_hi, (h_hi, h_lo)), (p_lo, (h_hi,))):
                            for hp in moving:
                                for half in (slice(0, HALF1), slice(HALF1, C1)):
                                    nc.tensor.matmul(p_o[:, d, half], pp[:, g % RING, cols], hp[:, s, half],
                                                     start=(begin and pp is p_hi and hp is h_hi and half.start == 0),
                                                     stop=(s == NT - 1 and pp is p_lo), skip_group_check=True)
                    if s == 0 and (part or not first):
                        turn_sums(i, part)
                        pe.wait_ge(sum_steps, i * 6 + (3 * part - 1))
                    for pp in (p_hi, p_lo):
                        nc.tensor.matmul(p_sum[:, 0:ROW], ones[:], pp[:, g % RING, 0:ROW],
                                         start=(begin and pp is p_hi), stop=False, skip_group_check=True)
                    for pp in (p_hi, p_lo):
                        last = nc.tensor.matmul(p_sum[0:T, ROW:ROW + 2], pp[:, g % RING, ROW:DH], ones[:, 0:2],
                                                start=False, stop=(s == NT - 1 and pp is p_lo), skip_group_check=True)
                    last.then_inc(p_used, 1)
                    if s in (2, 4, 6, 8) and (part or not first):
                        turn(i, part, (s - 2) // 2, first_ever=first and s == 2)

            every_iteration(pe, body)
            turn_sums(H1, 0)
            for c in range(CW):
                turn(H1, 0, c)


def from_turned(nc, core, turned_rows, K, w, out_rows, x=None, bias=None, stats=None, wa_parts=None, score_rows=None,
                col_src=None):
    ident, G = core.ident, core.G
    CW = D // 2
    PARTS = 6 if K % 3 == 0 else 8
    KP, KH = K // PARTS, K // 2
    PARTS_WITH = ((0,), range(1, PARTS // 2 + 1), range(PARTS // 2 + 1, PARTS))
    extra = 2 if wa_parts is not None else 0
    with ExitStack() as ctx:
        sb, pb, sem = core.tools(ctx)
        w_raw = sb("fw_raw", [128, K, CW], F32)
        w_hi = sb("fw_hi", [128, K, CW + extra], F32R)
        w_lo = sb("fw_lo", [128, K, CW + extra], F32R)
        f_raw = sb("f_raw", [128, 2, KH, T], F32)
        f_hi = sb("f_hi", [128, 2, KH, T], F32R)
        f_lo = sb("f_lo", [128, 2, KH, T], F32R)
        biased = sb("biased", [T, 2, CW], F32) if x is not None else None
        b_row = sb("b_row", [T, D], F32) if x is not None else None
        p_y = pb("p_y", [T, 2, 512])
        if extra:
            wa = sb("wa_now", [128, K, 2], F32)
            junk_b = sb("max2_junk", [T, 2, N], BF16)
            scores = sb("score2", [T, 2, 2, NT], F32)
            score = scores[:, :, 0, :]
            score_now = sb("score_now", [T, 2, NT], F32)
            turned = sb("turned2", [4 * NT, T], F32)
            turned_b = sb("turned2b", [4 * NT, T], F32)
            src_row = sb("src_row2", [T, N], F32)
            uv = sb("uv_col2", [T, 2, NT], F32)
            most = sb("most2", [T, NT], F32)
            tmp = sb("tmp_a", [T, NT], F32)
            tmp2 = sb("tmp_b", [T, NT], F32)
            p_s = pb("p_s2", [128, 512])

        w_in = [sem(f"fw_in{i}") for i in range(PARTS)]
        small_in = sem("small_in")
        f_in = [sem(f"f_in{i}") for i in range(2)]
        hi_done = sem("w_hi_done")
        w_split = sem("w_split")
        wa_steps = sem("wa_steps2")
        score_kept = sem("score_kept2")
        maxed = sem("maxed2")
        f_hi_done = sem("f_hi_done")
        f_lo_done = sem("f_lo_done")
        piece_used = sem("piece_used")
        y_left = sem("y_left")
        y_biased = sem("y_biased")
        steps = sem("fsteps")
        turned_done = sem("turned_done")
        turned_kept = sem("turned_kept2")
        rows_stored = sem("rows_stored2")
        row_in = sem("row_in2")

        block = ctx.enter_context(nc.Block())

        def over_halves(eng, body):
            if extra:
                body(0)
                body(1)
            else:
                with eng.Fori(0, 2) as half:
                    body(half)

        @block.sync
        def _(sp):
            def load_w(half, parts):
                for part_no in parts:
                    sp.wait_ge(w_split, half * PARTS + (part_no + 1))
                    ks = slice(part_no * KP, (part_no + 1) * KP)
                    sp.dma_start(w_raw[:, ks, :],
                                 w[half].rearrange("(k p) c -> p k c", p=128)[:, ks, :]).then_inc(w_in[part_no], 16)

            def load_f(half, t, kh):
                sp.wait_ge(f_lo_done, half * (2 * NT) + (2 * t + kh + 1))
                sp.dma_start(f_raw[:, kh, :, :],
                             turned_rows[kh * KH:(kh + 1) * KH, :, t * T:(t + 1) * T].rearrange("k p n -> p k n")).then_inc(f_in[kh], 16)

            def spread_scores():
                sp.wait_ge(turned_kept, 1)
                sp.dma_start(score_rows[0:2 * NT, :], turned[0:2 * NT, :]).then_inc(rows_stored, 16)
                sp.wait_ge(rows_stored, 16)
                sp.dma_start(src_row[:], score_rows[0:NT, :].rearrange("(o t) p -> o (t p)", o=1).broadcast_to([T, N])).then_inc(row_in, 16)

            for kh in range(2):
                load_w(0, PARTS_WITH[kh])
                load_f(0, 0, kh)
            load_w(0, PARTS_WITH[2])
            for half in range(2):
                for t in range(1 - half, NT):
                    for kh in range(2):
                        load_f(half, t, kh)
                    if extra and half and t == 4:
                        spread_scores()
                    if half == 0 and t == 2:
                        load_w(1, range(PARTS))
            if extra:
                sp.wait_ge(turned_kept, 2)
                sp.dma_start(core.uv_rows[0, 0:NT, :], turned_b[0:NT, :]).then_inc(rows_stored, 16)
                sp.dma_start(core.uv_rows[1, 0:NT, :], turned_b[NT:2 * NT, :]).then_inc(rows_stored, 16)
                sp.wait_ge(rows_stored, 48)

        @block.gpsimd
        def _(pool):
            if x is not None:
                pool.wait_ge(hi_done, PARTS - 2)
                pool.dma_start(out_rows[:], rows_of(x)).then_inc(small_in, 16)
                pool.dma_start(b_row[:], bias.rearrange("(o f) -> o f", o=1).broadcast_to([T, D])).then_inc(small_in, 16)

        @block.vector
        def _(dve):
            v = nc.vector
            v.sem_inc(f_lo_done, 2)
            v.sem_inc(y_left, 2)
            if extra:
                step = Chain(dve, wa_steps)
                for kh in range(2):
                    last = v.tensor_tensor(wa[:, kh * KH:(kh + 1) * KH, :], wa_parts[:, :, :, kh], wa_parts[:, :, :, 2 + kh], ALU.add)
                step(last)
                step(v.tensor_copy(w_hi[:, :, CW:], wa[:]))
                step(v.tensor_tensor(w_lo[:, :, CW:], wa[:], w_hi[:, :, CW:].bitcast(F32), ALU.subtract))

            def keep_turned(n, to):
                dve.wait_ge(turned_done, n + 1)
                v.tensor_copy(to[0:2 * NT, :], p_s[0:2 * NT, 0:T]).then_inc(turned_kept, 1)

            def half_of_rows(half):
                def rest_of_f(t, kh):
                    dve.wait_ge(f_hi_done, half * (2 * NT) + (2 * t + kh + 1))
                    v.tensor_tensor(f_lo[:, kh], f_raw[:, kh], f_hi[:, kh].bitcast(F32), ALU.subtract).then_inc(f_lo_done, 1)

                def rest_of_w(part_no):
                    ks = slice(part_no * KP, (part_no + 1) * KP)
                    dve.wait_ge(hi_done, half * PARTS + (part_no + 1))
                    v.tensor_tensor(w_lo[:, ks, 0:CW], w_raw[:, ks, :], w_hi[:, ks, 0:CW].bitcast(F32),
                                    ALU.subtract).then_inc(w_split, 1)

                def maximum(t):
                    if t == 0:
                        dve.wait_ge(row_in, 16)
                    if t >= 2:
                        dve.wait_ge(maxed, t - 1)
                    v.tensor_tensor_reduce(out=junk_b[:, t % 2, :], in0=src_row[:], in1=G[:, t, :], scale=1.0, scalar=NO_EDGE,
                                           op0=ALU.add, op1=ALU.max, accum_out=most[:, t:t + 1]).then_inc(maxed, 1)

                def statistics(t):
                    wait_apart(dve, y_biased, half * NT + (t + 1))
                    v.bn_stats(stats[:, t, bass.ds(half, 1), :].rearrange("p o s -> p (o s)"), out_rows[:, t, bass.ds(half * CW, CW)])

                def leave(t):
                    if t:
                        statistics(t - 1)
                    else:
                        wait_apart(dve, small_in, 32)
                    dve.wait_ge(piece_used, half * (2 * NT) + (2 * t + 2 + 2 * NT))
                    cols = bass.ds(half * CW, CW)
                    v.tensor_tensor(biased[:, t % 2, :], p_y[:, t % 2, 0:CW], b_row[:, cols], ALU.add).then_inc(y_left, 1)
                    dve.wait_ge(y_left, half * NT + (t + 3))
                    v.scalar_tensor_tensor(out_rows[:, t, cols], biased[:, t % 2, :], 0.0, out_rows[:, t, cols],
                                           ALU.max, ALU.add).then_inc(y_biased, 1)

                for t in range(NT):
                    for kh in range(2):
                        if t == 0:
                            for part_no in PARTS_WITH[kh]:
                                rest_of_w(part_no)
                        rest_of_f(t, kh)
                    if t == 0:
                        for part_no in PARTS_WITH[2]:
                            rest_of_w(part_no)
                    if x is not None and t:
                        leave(t - 1)
                    if extra and half and t == 1:
                        dve.wait_ge(y_left, NT + 2)
                        v.tensor_copy(score_now[:], score).then_inc(score_kept, 1)
                        v.tensor_copy(col_src[0][:, 0, :], score[:, 0])
                        v.tensor_scalar(col_src[1][:, 0, :], score[:, 0], SLOPE, None, ALU.mult)
                    if extra and half and t == 3:
                        keep_turned(0, turned)
                    if extra and half and t >= NH:
                        for n in range(2):
                            maximum(2 * (t - NH) + n)
                if x is not None:
                    leave(NT - 1)
                    statistics(NT - 1)

            over_halves(dve, half_of_rows)
            if extra:
                step = Chain(dve, steps)
                dve.wait_ge(maxed, NT)
                step(v.tensor_tensor(tmp[:], most[:], score[:, 1], ALU.add))
                step(v.scalar_tensor_tensor(tmp2[:], tmp[:], SLOPE, tmp[:], ALU.mult, ALU.max))
                v.tensor_tensor(uv[:, 0], score[:, 1], tmp2[:], ALU.subtract)
                step(v.scalar_tensor_tensor(uv[:, 1], score[:, 1], SLOPE, tmp2[:], ALU.mult, ALU.subtract))
                keep_turned(1, turned_b)

        @block.scalar
        def _(act):
            a = nc.scalar
            a.sem_inc(w_split, PARTS)
            with act.Fori(0, 2) as half:
                def round_w(part_no):
                    ks = slice(part_no * KP, (part_no + 1) * KP)
                    act.wait_ge(w_in[part_no], half * 16 + 16)
                    wait_apart(act, piece_used, half * (2 * NT) + 2 * NT)
                    a.activation(w_hi[:, ks, 0:CW], w_raw[:, ks, :], ACT.Copy).then_inc(hi_done, 1)

                def leave(t):
                    act.wait_ge(piece_used, half * (2 * NT) + (2 * t + 2 + 2 * NT))
                    a.activation(out_rows[:, t, bass.ds(half * CW, CW)], p_y[:, t % 2, 0:CW], ACT.Copy)
                    a.activation(scores[:, :, bass.ds(half, 1), t], p_y[:, t % 2, CW:CW + 2].rearrange("p (a o) -> p a o", o=1),
                                 ACT.Copy).then_inc(y_left, 1)

                for t in range(NT):
                    for kh in range(2):
                        if t == 0:
                            for part_no in PARTS_WITH[kh]:
                                round_w(part_no)
                        act.wait_ge(f_in[kh], half * (16 * NT) + 16 * (t + 1))
                        act.wait_ge(piece_used, half * (2 * NT) + (2 * t + kh + 2 * NT - 1))
                        a.activation(f_hi[:, kh], f_raw[:, kh], ACT.Copy).then_inc(f_hi_done, 1)
                    if t == 0:
                        for part_no in PARTS_WITH[2]:
                            round_w(part_no)
                    if extra and t:
                        leave(t - 1)
                if extra:
                    leave(NT - 1)

        @block.tensor
        def _(pe):
            nc.tensor.sem_inc(piece_used, 2 * NT)
            if extra:
                pe.wait_ge(wa_steps, 3)

            def half_of_rows(half):
                for t in range(NT):
                    pe.wait_ge(y_left, half * NT + (t + 1))
                    for kh in range(2):
                        pe.wait_ge(f_lo_done, half * (2 * NT) + (2 * t + kh + 3))
                        for kk in range(KH):
                            k = kh * KH + kk
                            if t == 0 and k % KP == 0:
                                pe.wait_ge(w_split, half * PARTS + (k // KP + 1 + PARTS))
                            for n, (fp, wp) in enumerate(((f_hi, w_hi), (f_hi, w_lo), (f_lo, w_hi))):
                                last = nc.tensor.matmul(p_y[:, t % 2, 0:CW + extra], fp[:, kh, kk, :], wp[:, k, :],
                                                        start=(k == 0 and n == 0), stop=(k == K - 1 and n == 2))
                        last.then_inc(piece_used, 1)
                    if extra and half and t == 1:
                        pe.wait_ge(score_kept, 1)
                        nc.tensor.transpose(p_s[0:2 * NT, 0:T], score_now[:].rearrange("p a t -> p (a t)"), ident[0:T, 0:T]).then_inc(turned_done, 1)

            over_halves(pe, half_of_rows)
            if extra:
                pe.wait_ge(steps, 3)
                pe.wait_ge(turned_kept, 1)
                nc.tensor.transpose(p_s[0:2 * NT, 0:T], uv[:].rearrange("p a t -> p (a t)"), ident[0:T, 0:T]).then_inc(turned_done, 1)


def normalize(nc, core, y, stats, to_dram, xT=None):
    ident = core.ident
    with ExitStack() as ctx:
        sb, pb, sem = core.tools(ctx)
        moments = sb("ln_moments", [T, NT, 2], F32)
        var = sb("ln_var", [T, NT], F32)
        root = sb("ln_root", [T, NT], F32)
        inv = sb("ln_inv", [T, NT], F32)
        tmp = sb("ln_tmp", [T, NT], F32)
        better = sb("ln_better", [T, NT], F32)
        shift = sb("ln_shift", [T, NT], F32)
        normed = sb("normed", [T, NT, D], F32)
        p_t = pb("ln_p", [128, 4, 512]) if xT else None
        steps = sem("ln_steps")
        var_done = sem("var_done")
        root_done = sem("root_done")
        normed_even = sem("normed_even")
        normed_odd = sem("normed_odd")
        stored = sem("ln_stored")
        turned = sem("ln_turned")
        hi_done = sem("ln_hi")
        lo_done = sem("ln_lo")
        block = ctx.enter_context(nc.Block())
        HT = NH
        LN_STEPS = 6

        @block.sync
        def _(sp):
            for q in range(2):
                sp.wait_ge(normed_even, (3, 5)[q])
                sp.wait_ge(normed_odd, (2, 5)[q])
                sp.dma_start(rows_of(to_dram)[:, q * HT:(q + 1) * HT, :], normed[:, q * HT:(q + 1) * HT, :]).then_inc(stored, 16)
            sp.wait_ge(stored, 32)

        @block.vector
        def _(dve):
            v = nc.vector
            step = Chain(dve, steps)
            for t in range(NT):
                last = v.bn_aggr(moments[:, t, :], stats[:, t, :, :])
            step(last)
            v.tensor_scalar(var[:], moments[:, :, 1], EPS, None, ALU.add).then_inc(var_done, 1)
            dve.wait_ge(root_done, 1)
            step(v.reciprocal(inv[:], root[:]))
            step(v.tensor_tensor(tmp[:], inv[:], inv[:], ALU.mult))
            step(v.scalar_tensor_tensor(tmp[:], tmp[:], -0.5, var[:], ALU.mult, ALU.mult))
            step(v.scalar_tensor_tensor(better[:], tmp[:], 1.5, inv[:], ALU.add, ALU.mult))
            step(v.scalar_tensor_tensor(shift[:], moments[:, :, 0], -1.0, better[:], ALU.mult, ALU.mult))
            for t in range(0, NT, 2):
                v.tensor_scalar(normed[:, t, :], y[:, t, :], moments[:, t, 0:1], better[:, t:t + 1],
                                ALU.subtract, ALU.mult).then_inc(normed_even, 1)
            if xT:
                for n in range(3 * KD):
                    k = n // 3
                    dve.wait_ge(hi_done, n + 1)
                    g = n % 3
                    a, m = 4 * g * T, (4 if g < 2 else 2) * T
                    v.tensor_tensor(xT[1][:, k, a:a + m], p_t[:, n % 4, 0:m], xT[0][:, k, a:a + m].bitcast(F32),
                                    ALU.subtract).then_inc(lo_done, 1)

        @block.scalar
        def _(act):
            act.wait_ge(var_done, 1)
            nc.scalar.activation(root[:], var[:], ACT.Sqrt).then_inc(root_done, 1)
            act.wait_ge(steps, LN_STEPS)
            for t in range(1, NT, 2):
                nc.scalar.activation(normed[:, t, :], y[:, t, :], ACT.Identity, scale=better[:, t:t + 1],
                                     bias=shift[:, t:t + 1]).then_inc(normed_odd, 1)
            if xT:
                for n in range(3 * KD):
                    k, g = divmod(n, 3)
                    a, m = 4 * g * T, (4 if g < 2 else 2) * T
                    act.wait_ge(turned, n + 1)
                    nc.scalar.activation(xT[0][:, k, a:a + m], p_t[:, n % 4, 0:m], ACT.Copy).then_inc(hi_done, 1)

        @block.tensor
        def _(pe):
            if xT:
                pe.wait_ge(normed_even, NT // 2)
                pe.wait_ge(normed_odd, NT // 2)
                for n in range(3 * KD):
                    k, g = divmod(n, 3)
                    if n >= 4:
                        pe.wait_ge(lo_done, n - 3)
                    for i in range(4 if g < 2 else 2):
                        t = 4 * g + i
                        last = nc.tensor.transpose(p_t[:, n % 4, i * T:(i + 1) * T], normed[:, t, k * 128:(k + 1) * 128],
                                                   ident[0:T, 0:T])
                    last.then_inc(turned, 1)


def aggregate_last(nc, core, h2, col_src, bias, x2_dram, y2, stats):
    CT = core.CT
    PIECE = D // 3
    STEPS = 2 * NT
    RING = 4
    ORDER = tuple(reversed(range(NH)))
    OPENS = (12, 14, 9, 10, 6, 3, 4, 0)
    with ExitStack() as ctx:
        sb, pb, sem = core.tools(ctx)
        uv = sb("uv_l", [T, 2, N], F32)
        h_hi = sb("h_hi_l", [T, NT, D], F32R)
        e = sb("e_l", [T, RING, 2, DH], F32)
        p_hi = sb("p_hi_l", [T, RING, DH], F32R)
        p_lo = sb("p_lo_l", [T, RING, DH], F32R)
        sums = sb("sums_l", [T, 2, NH], F32)
        ones_f = sb("ones_fl", [T, 2], F32)
        ones = sb("ones_l", [T, 2], F32R)
        b_row = sb("b_row_l", [T, D], F32)
        p_o = pb("p_ol", [T, 8, 512])
        in_sem = sem("in_l")
        base_in = sem("base_in_l")
        ones_set = sem("ones_set_l")
        h_hi_done = sem("h_hi_done_l")
        h_split = sem("h_split_l")
        exp_ready = sem("exp_ready_l")
        more_ready = sem("more_ready_l")
        p_ready = sem("p_ready_l")
        p_hi_ready = sem("p_hi_ready_l")
        p_split = sem("p_split_l")
        p_used = sem("p_used_l")
        sum_steps = sem("sum_steps_l")
        left = sem("left_l")
        base_done = sem("base_done_l")
        block = ctx.enter_context(nc.Block())
        h_lo = h2[:].bitcast(F32R)

        @block.sync
        def _(sp):
            for kind in range(2):
                sp.dma_start(uv[:, kind, :], core.uv_rows[kind, 0:NT, :].rearrange("(o t) p -> o (t p)", o=1)
                             .broadcast_to([T, N])).then_inc(in_sem, 16)
            sp.dma_start(b_row[:], bias.rearrange("(o f) -> o f", o=1).broadcast_to([T, D])).then_inc(base_in, 16)
            sp.dma_start(y2[:], rows_of(x2_dram)).then_inc(base_in, 16)

        @block.gpsimd
        def _(pool):
            for s in range(NT):
                pool.tensor_copy(h_hi[:, s, :], h2[:, s, :]).then_inc(h_hi_done, 1)
                pool.wait_ge(h_hi_done, s + 1)
                pool.tensor_tensor(h_lo[:, s, :], h2[:, s, :], h_hi[:, s, :].bitcast(F32), ALU.subtract).then_inc(h_split, 1)
            pool.wait_ge(base_in, 32)
            for t in range(NT):
                pool.tensor_tensor(y2[:, t, :], y2[:, t, :], b_row[:], ALU.add).then_inc(base_done, 1)

        @block.scalar
        def _(act):
            a = nc.scalar
            act.wait_ge(ones_set, 1)
            a.activation(ones[:], ones_f[:], ACT.Copy).then_inc(ones_set, 1)
            act.wait_ge(in_sem, 32)

            def round_p(g):
                act.wait_ge(p_ready, g + 1)
                if g >= RING:
                    act.wait_ge(p_used, g - RING + 1)
                a.activation(p_hi[:, g % RING, :], e[:, g % RING, 0, :], ACT.Copy).then_inc(p_hi_ready, 1)

            for g in range(STEPS):
                part, s = divmod(g, NT)
                if g >= RING:
                    act.wait_ge(p_split, g - RING + 1)
                for kind in range(2):
                    last = a.activation(e[:, g % RING, kind, :], uv[:, kind, part * DH:(part + 1) * DH], ACT.Exp,
                                        bias=col_src[kind][:, 0, s:s + 1])
                last.then_inc(exp_ready, 1)
                if g >= 2:
                    round_p(g - 2)
            round_p(STEPS - 2)
            round_p(STEPS - 1)

        @block.vector
        def _(dve):
            v = nc.vector
            v.memset(ones_f[:], 1.0).then_inc(ones_set, 1)

            def divisors(part):
                dve.wait_ge(p_used, (part + 1) * NT)
                v.tensor_scalar(sums[:, 0, :], p_o[:, 7, 256:256 + 2 * NH].rearrange("p (d a) -> p d a", a=2)[:, :, 0],
                                1e-16, None, ALU.add).then_inc(sum_steps, 1)
                dve.wait_ge(sum_steps, 2 * part + 1)
                v.reciprocal(sums[:, 1, :], sums[:, 0, :]).then_inc(sum_steps, 1)

            def leave(part):
                dve.wait_ge(sum_steps, 2 * part + 2)
                dve.wait_ge(base_done, NT)
                for d in ORDER:
                    for j in range(3):
                        w = 3 * d + j
                        y_piece = y2[:, part * NH + d, j * PIECE:(j + 1) * PIECE]
                        last = v.scalar_tensor_tensor(y_piece, p_o[:, w // 2, (w % 2) * 256:(w % 2) * 256 + PIECE],
                                                      sums[:, 1, d:d + 1], y_piece, ALU.mult, ALU.add)
                    last.then_inc(left, 1)
                for n, d in enumerate(ORDER, part * NH):
                    dve.wait_ge(left, n + 1)
                    t = part * NH + d
                    for q in range(2):
                        v.bn_stats(stats[:, t, q, :], y2[:, t, q * (D // 2):(q + 1) * (D // 2)])

            def rest_of_p(g):
                dve.wait_ge(p_hi_ready, g + 1)
                v.tensor_tensor(p_lo[:, g % RING, :], e[:, g % RING, 0, :], p_hi[:, g % RING, :].bitcast(F32),
                                ALU.subtract).then_inc(p_split, 1)

            for g in range(STEPS):
                part, s = divmod(g, NT)
                dve.wait_ge(exp_ready, g + 1)
                v.tensor_tensor(e[:, g % RING, 0, :], e[:, g % RING, 0, :], e[:, g % RING, 1, :], ALU.max).then_inc(more_ready, 1)
                dve.wait_ge(more_ready, g + 1)
                v.scalar_tensor_tensor(e[:, g % RING, 0, :], e[:, g % RING, 0, :], 1.0, CT[:, s, part * DH:(part + 1) * DH],
                                       ALU.min, ALU.mult).then_inc(p_ready, 1)
                if g:
                    rest_of_p(g - 1)
                if g == NT + 4:
                    divisors(0)
                    leave(0)
            rest_of_p(STEPS - 1)
            divisors(1)
            leave(1)

        @block.tensor
        def _(pe):
            pe.wait_ge(ones_set, 2)
            for g in range(STEPS):
                part, s = divmod(g, NT)
                if part == 0:
                    pe.wait_ge(h_split, s + 1)
                pe.wait_ge(p_split, g + 1)
                for d in ORDER:
                    if part and s == 0 and d in (4, 3, 1):
                        pe.wait_ge(left, {4: 1, 3: 3, 1: 5}[d])
                    for pp, moving in ((p_hi, (h_hi, h_lo)), (p_lo, (h_hi,))):
                        stationary = pp[:, g % RING, d * T:(d + 1) * T]
                        for hp in moving:
                            for j in range(3):
                                w = 3 * d + j
                                nc.tensor.matmul(p_o[:, w // 2, (w % 2) * 256:(w % 2) * 256 + PIECE], stationary,
                                                 hp[:, s, j * PIECE:(j + 1) * PIECE],
                                                 start=(s == 0 and w in OPENS and pp is p_hi and hp is h_hi),
                                                 stop=(s == NT - 1 and pp is p_lo), skip_group_check=True)
                        last = nc.tensor.matmul(p_o[:, 7, 256 + 2 * d:258 + 2 * d], stationary, ones[:], start=False,
                                                stop=(s == NT - 1 and pp is p_lo), skip_group_check=True)
                last.then_inc(p_used, 1)


def gnn_two_layers(nc, src, dst, x, w_ah, b_ah, w_gat0, a_gat0, b_gat0, w_out, b_out, w1, a1, b1, w2, a2, b2, out):
    dram = lambda name, shape: nc.dram_tensor(name, shape, F32, kind="Internal").ap()
    h0_rows = dram("h0_rows", [CONVS * H0, N, HC0])
    h1_rows = dram("h1_rows", [2 * H1, N, HALF1])
    score_rows = dram("score_rows", [CONVS * 2 * H0, N])
    score_rows2 = dram("score_rows2", [2 * NT, T])
    turned0 = dram("turned0", [KO, 128, N])
    turned1 = dram("turned1", [K1, 128, N])
    x2_rows = dram("x2_rows", [N, D])
    with ExitStack() as ctx:
        core = Core(nc)
        core.uv_rows = dram("uv_rows", [2, CONVS * H0 * NT, T])
        sb, _, sem = core.tools(ctx)
        core.ident = sb("ident", [128, 128], F32)
        core.wa1 = sb("wa1", [128, KD, 2, H1], F32)
        core.wa2 = sb("wa2", [128, K1 // 2, 2, 4], F32)
        stats = sb("stats", [T, NT, 2, 6], F32)
        core.CT = sb("CT", [T, NT, N], U16)
        core.G_room = sb("G", [128, NT, N], BF16)
        core.G = core.G_room[0:T]
        cols = [sb(f"col{i}", [T, CONVS * H0, NT], F32) for i in range(4)]
        core.ident_ready = sem("ident_ready")
        waits_done[0] = sem("waits")
        nc.gpsimd.memset(core.ident[:], 0.0).then_inc(core.ident_ready, 1)
        nc.gpsimd.wait_ge(core.ident_ready, 1)
        nc.gpsimd.affine_select(out=core.ident[:], in_=core.ident[:], compare_op=ALU.not_equal, fill=1.0, base=0,
                                pattern=[[-1, 128]], channel_multiplier=1).then_inc(core.ident_ready, 1)
        with ExitStack() as inner:
            sb1 = core.tools(inner)[0]
            core.wa0 = sb1("wa0", [128, KD, 2, CONVS * H0], F32)
            core.x1T = [sb1(f"x1T{i}", [128, KD, N], F32R) for i in range(2)]
            counts_and_x1(nc, core, src, dst, x, w_ah, b_ah, w_gat0, a_gat0)
            project(nc, core, core.x1T, w_gat0, core.wa0, h0_rows, score_rows, PAIR, cols[0:2], *cols[2:4])
        aggregate_layer0(nc, core, h0_rows, cols[0:2], b_gat0, turned0, w1, a1, w2, a2)
        with ExitStack() as inner:
            sb1 = core.tools(inner)[0]
            y = sb1("y", [T, NT, D], F32)
            from_turned(nc, core, turned0, KO, w_out, y, x=x, bias=b_out, stats=stats)
            x2T = [sb1(f"x2T{i}", [128, KD, N], F32R) for i in range(2)]
            normalize(nc, core, y, stats, x2_rows, x2T)
            project(nc, core, x2T, w1, core.wa1, h1_rows, score_rows, HALF1, cols[0:2], *cols[2:4])
        aggregate_layer1(nc, core, h1_rows, cols[0:2], b1, turned1)
        with ExitStack() as inner:
            sb1 = core.tools(inner)[0]
            h2 = sb1("h2", [T, NT, D], F32)
            from_turned(nc, core, turned1, K1, w2.rearrange("(u g) r c -> u (g r) c", u=2), h2, wa_parts=core.wa2, score_rows=score_rows2, col_src=cols[0:2])
            y2 = sb1("y2", [T, NT, D], F32)
            aggregate_last(nc, core, h2, cols[0:2], b2, x2_rows, y2, stats)
            normalize(nc, core, y2, stats, out)


def kernel(**inputs):
    import numpy as np
    import concourse.bacc as bacc
    from concourse import mybir as _mybir
    from concourse.bass_utils import run_bass_kernel_spmd

    g = {k: np.asarray(v) for k, v in inputs.items()}
    L0, L1 = "L0_gnn_", "L1_gnn_"
    by_unit = lambda w, width: np.stack([w[:, q:q + width] for q in range(0, w.shape[1], width)])
    a_units = lambda s, d, width: np.stack([s.reshape(-1, width), d.reshape(-1, width)], axis=1)
    by_feature = lambda b, groups: b.reshape(groups, -1, 128).transpose(2, 0, 1)
    arrays = {
        "src": g["src"], "dst": g["dst"], "x": g["x"], "w_ah": g[L0 + "W_ah"], "b_ah": by_feature(g[L0 + "b_ah"], 1)[:, 0],
        "w_gat0": np.concatenate([by_unit(g[f"{L0}W{i}"], PAIR) for i in range(CONVS)]),
        "a_gat0": np.concatenate([a_units(g[f"{L0}a_src{i}"], g[f"{L0}a_dst{i}"], PAIR) for i in range(CONVS)]),
        "b_gat0": by_feature(np.concatenate([g[f"{L0}b{i}"] for i in range(CONVS)]), 2 * CONVS),
        "w_out": by_unit(g[L0 + "W_out"], D // 2), "b_out": g[L0 + "b_out"],
        "w1": by_unit(g[L1 + "W1"], HALF1), "a1": a_units(g[L1 + "a1_src"], g[L1 + "a1_dst"], HALF1), "b1": by_feature(g[L1 + "b1"], H1),
        "w2": by_unit(g[L1 + "W2"], D // 2).reshape(4, -1, D // 2),
        "a2": np.repeat(a_units(g[L1 + "a2_src"], g[L1 + "a2_dst"], D // 2), 2, axis=0), "b2": g[L1 + "b2"],
    }
    arrays = {f"in_{k}": np.ascontiguousarray(v) for k, v in arrays.items()}
    nc = bacc.Bacc("TRN2", target_bir_lowering=False, num_devices=1)
    args = [nc.dram_tensor(k, v.shape, _mybir.dt.from_np(v.dtype), kind="ExternalInput").ap() for k, v in arrays.items()]
    out = nc.dram_tensor("out", (N, D), F32, kind="ExternalOutput").ap()
    gnn_two_layers(nc, *args, out)
    return run_bass_kernel_spmd(nc, [arrays], core_ids=[0]).results[0]["out"]
```
